# Optimizing a Trainium2 kernel written in Bass

```python
import numpy as np
import jax
import jax.numpy as jnp

def _softmax(x, axis=-1):
    return jax.nn.softmax(x, axis=axis)

def _gelu(x):
    return jax.nn.gelu(x, approximate=True)

def _silu(x):
    return jax.nn.silu(x)

def _sigmoid(x):
    return jax.nn.sigmoid(x)

def _layernorm(x, axis=-1, eps=1e-05):
    m = jnp.mean(x, axis=axis, keepdims=True)
    v = jnp.var(x, axis=axis, keepdims=True)
    return (x - m) / jnp.sqrt(v + eps)

def _scatter_add(tgt, idx, src, axis=0):
    return tgt.at[idx].add(src)

def _segment_sum(src, seg, n):
    return jax.ops.segment_sum(src, seg, n)
kernel_name = 'mk_vit_tower_d1_tok_img768_r4_8a9df1'

def setup_inputs(seed: int=0):
    np.random.seed(seed)
    _w = jnp.asarray

    def _rec_inputs():
        import jax
        import jax.numpy as jnp
        _rk = jax.random.key(seed)
        x = 7.57192e-06 + 1.00007 * jax.random.normal(jax.random.fold_in(_rk, 1), (64, 3, 224, 224), jnp.float32)
        return x
    x = _rec_inputs()

    def _L0_tok_setup():
        import jax, jax.numpy as jnp
        import numpy as np
        B, IN, IMG = (64, 3, 224)
        PATCH, LEVELS, D = (16, 4, 192)
        ISQ2 = 0.7071067811865476
        DN = ('NCHW', 'OIHW', 'NCHW')

        def conv(x, w, b=None, stride=1, pad=((0, 0), (0, 0)), groups=1):
            y = jax.lax.conv_general_dilated(x, w, (stride, stride), pad, dimension_numbers=DN, feature_group_count=groups)
            return y if b is None else y + b[None, :, None, None]

        def dwconv(x, wd, wp, bp):
            y = conv(x, wd, pad=((1, 1), (1, 1)), groups=x.shape[1])
            return conv(y, wp, bp)

        def haar_dwt2(x):
            xe, xo = (x[..., ::2], x[..., 1::2])
            lo_w, hi_w = ((xe + xo) * ISQ2, (xe - xo) * ISQ2)

            def split_h(t):
                te, to = (t[..., ::2, :], t[..., 1::2, :])
                return ((te + to) * ISQ2, (te - to) * ISQ2)
            ll, lh = split_h(lo_w)
            hl, hh = split_h(hi_w)
            return (ll, lh, hl, hh)

        def wavelet_packet(x):
            f = x
            for _ in range(LEVELS):
                b, k, h, w = f.shape
                ll, lh, hl, hh = haar_dwt2(f)
                bands = jnp.stack([ll, lh, hl, hh], axis=1)
                bands = bands.reshape(b, 4, k // IN, IN, h // 2, w // 2)
                f = jnp.transpose(bands, (0, 2, 1, 3, 4, 5)).reshape(b, 4 * k, h // 2, w // 2)
            return f

        def gelu(x):
            return jax.nn.gelu(x, approximate=False)

        def forward(x, pl_w, pl_b, pl_dw, pl_pw, pl_pwb, pg_w1, pg_b1, pg_dw, pg_pw, pg_pwb, pg_w2, pg_b2, alpha, f1_dw, f1_pw, f1_pwb, f2_dw, f2_pw, f2_pwb, f3_dw, f3_pw, f3_pwb, ln_g, ln_b, cls):
            loc = conv(x, pl_w, pl_b, stride=PATCH)
            loc = dwconv(gelu(loc), pl_dw, pl_pw, pl_pwb)
            g = wavelet_packet(x)
            g = gelu(conv(g, pg_w1, pg_b1))
            g = gelu(dwconv(g, pg_dw, pg_pw, pg_pwb))
            glob = conv(g, pg_w2, pg_b2)
            gate = 0.5 * (jnp.tanh(alpha) + 1.0)
            h = (1.0 - gate) * loc + gate * glob
            h = jax.nn.relu(dwconv(h, f1_dw, f1_pw, f1_pwb))
            h = jax.nn.relu(dwconv(h, f2_dw, f2_pw, f2_pwb))
            h = dwconv(loc + h, f3_dw, f3_pw, f3_pwb)
            t = jnp.transpose(h.reshape(h.shape[0], D, -1), (0, 2, 1))
            mu = jnp.mean(t, -1, keepdims=True)
            var = jnp.mean((t - mu) ** 2, -1, keepdims=True)
            t = (t - mu) / jnp.sqrt(var + 1e-05) * ln_g + ln_b
            cls_tok = jnp.broadcast_to(cls, (t.shape[0], 1, D))
            return jnp.concatenate([cls_tok, t], axis=1)
        key = jax.random.key(seed)
        ks = jax.random.split(key, 32)

        def rn(i, shape, s=0.02):
            return jax.random.normal(ks[i], shape, jnp.float32) * s
        KW = IN * 4 ** LEVELS
        return {'x': jax.random.normal(ks[0], (B, IN, IMG, IMG), jnp.float32), 'pl_w': rn(1, (D, IN, PATCH, PATCH)), 'pl_b': rn(2, (D,)), 'pl_dw': rn(3, (D, 1, 3, 3)), 'pl_pw': rn(4, (D, D, 1, 1)), 'pl_pwb': rn(5, (D,)), 'pg_w1': rn(6, (D, KW, 1, 1)), 'pg_b1': rn(7, (D,)), 'pg_dw': rn(8, (D, 1, 3, 3)), 'pg_pw': rn(9, (D, D, 1, 1)), 'pg_pwb': rn(10, (D,)), 'pg_w2': rn(11, (D, D, 1, 1)), 'pg_b2': rn(12, (D,)), 'alpha': jnp.zeros((1, D, 1, 1), jnp.float32), 'f1_dw': rn(13, (D, 1, 3, 3)), 'f1_pw': rn(14, (D, D, 1, 1)), 'f1_pwb': rn(15, (D,)), 'f2_dw': rn(16, (D, 1, 3, 3)), 'f2_pw': rn(17, (D, D, 1, 1)), 'f2_pwb': rn(18, (D,)), 'f3_dw': rn(19, (D, 1, 3, 3)), 'f3_pw': rn(20, (D, D, 1, 1)), 'f3_pwb': rn(21, (D,)), 'ln_g': jnp.ones((D,), jnp.float32), 'ln_b': jnp.zeros((D,), jnp.float32), 'cls': rn(22, (1, 1, D))}
    _L0_tok_all = _L0_tok_setup()
    _L0_tok_in = {k: v for k, v in _L0_tok_all.items() if k in ('pl_w', 'pl_b', 'pl_dw', 'pl_pw', 'pl_pwb', 'pg_w1', 'pg_b1', 'pg_dw', 'pg_pw', 'pg_pwb', 'pg_w2', 'pg_b2', 'alpha', 'f1_dw', 'f1_pw', 'f1_pwb', 'f2_dw', 'f2_pw', 'f2_pwb', 'f3_dw', 'f3_pw', 'f3_pwb', 'ln_g', 'ln_b', 'cls')}
    del _L0_tok_all

    def _L0_attn_setup():
        import jax, jax.numpy as jnp
        import numpy as np

        def _selective_scan(dt, Bm, Cm, xp, A):
            Bsz, L, d_inner = xp.shape
            N = A.shape[1]

            def step(h, inp):
                dt_t, B_t, C_t, x_t = inp
                dA = jnp.exp(dt_t[..., None] * A)
                dBx = (dt_t * x_t)[..., None] * B_t[:, None, :]
                h = dA * h + dBx
                y = jnp.einsum('bdn,bn->bd', h, C_t)
                return (h, y)
            h0 = jnp.zeros((Bsz, d_inner, N), dtype=xp.dtype)
            inputs = (jnp.moveaxis(dt, 1, 0), jnp.moveaxis(Bm, 1, 0), jnp.moveaxis(Cm, 1, 0), jnp.moveaxis(xp, 1, 0))
            _, ys = jax.lax.scan(step, h0, inputs)
            return jnp.moveaxis(ys, 0, 1)
        key = jax.random.key(seed)
        ks = jax.random.split(key, 9)
        B, L, D = (2, 512, 192)
        d_inner, N, R = (384, 16, 48)
        s = 0.02
        x = jax.random.normal(ks[0], (B, L, D), dtype=jnp.float32)
        W_in = jax.random.normal(ks[1], (D, 2 * d_inner), dtype=jnp.float32) * s
        W_x = jax.random.normal(ks[2], (d_inner, R + 2 * N), dtype=jnp.float32) * s
        W_dt = jax.random.normal(ks[3], (R, d_inner), dtype=jnp.float32) * s
        b_dt = jax.random.normal(ks[4], (d_inner,), dtype=jnp.float32) * s
        A_log = jnp.log(jnp.broadcast_to(jnp.arange(1, N + 1, dtype=jnp.float32), (d_inner, N)))
        D_skip = jnp.ones((d_inner,), dtype=jnp.float32)
        W_out = jax.random.normal(ks[5], (d_inner, D), dtype=jnp.float32) * s
        gamma = jnp.ones((D,), dtype=jnp.float32)
        beta = jnp.zeros((D,), dtype=jnp.float32)
        return {'x': x, 'W_in': W_in, 'W_x': W_x, 'W_dt': W_dt, 'b_dt': b_dt, 'A_log': A_log, 'D_skip': D_skip, 'W_out': W_out, 'gamma': gamma, 'beta': beta}
    _L0_attn_all = _L0_attn_setup()
    _L0_attn_in = {k: v for k, v in _L0_attn_all.items() if k in ('W_in', 'W_x', 'W_dt', 'b_dt', 'A_log', 'D_skip', 'W_out', 'gamma', 'beta')}
    del _L0_attn_all

    def _L0_ffn_setup():
        import jax, jax.numpy as jnp
        import numpy as np
        EPS = 1e-06

        def l2_normalize(x, axis):
            norm = jnp.sqrt(jnp.square(x).sum(axis=axis, keepdims=True))
            return x * (1.0 / (norm + EPS))
        key = jax.random.key(seed)
        ks = jax.random.split(key, 8)
        b, m, d = (32, 256, 192)
        n, p = (8, 4)
        h = d // 8
        X = jax.random.normal(ks[0], (b, m, d), dtype=jnp.float32)
        std_slot = float(np.sqrt(2.0 / (d + n * p)))
        slot_params = jax.random.normal(ks[1], (d, n, p), dtype=jnp.float32) * std_slot
        scale = jnp.ones((), dtype=jnp.float32)
        W_down = jax.random.normal(ks[2], (n, d, h), dtype=jnp.float32) * float(np.sqrt(1.0 / d))
        b_down = jnp.zeros((n, h), dtype=jnp.float32)
        W_up = jax.random.normal(ks[3], (n, h, d), dtype=jnp.float32) * float(np.sqrt(1.0 / h))
        b_up = jnp.zeros((n, d), dtype=jnp.float32)
        return {'X': X, 'slot_params': slot_params, 'scale': scale, 'W_down': W_down, 'b_down': b_down, 'W_up': W_up, 'b_up': b_up}
    _L0_ffn_all = _L0_ffn_setup()
    _L0_ffn_in = {k: v for k, v in _L0_ffn_all.items() if k in ('slot_params', 'scale', 'W_down', 'b_down', 'W_up', 'b_up')}
    del _L0_ffn_all
    return {'x': x, 'L0_tok_pl_w': _L0_tok_in['pl_w'], 'L0_tok_pl_b': _L0_tok_in['pl_b'], 'L0_tok_pl_dw': _L0_tok_in['pl_dw'], 'L0_tok_pl_pw': _L0_tok_in['pl_pw'], 'L0_tok_pl_pwb': _L0_tok_in['pl_pwb'], 'L0_tok_pg_w1': _L0_tok_in['pg_w1'], 'L0_tok_pg_b1': _L0_tok_in['pg_b1'], 'L0_tok_pg_dw': _L0_tok_in['pg_dw'], 'L0_tok_pg_pw': _L0_tok_in['pg_pw'], 'L0_tok_pg_pwb': _L0_tok_in['pg_pwb'], 'L0_tok_pg_w2': _L0_tok_in['pg_w2'], 'L0_tok_pg_b2': _L0_tok_in['pg_b2'], 'L0_tok_alpha': _L0_tok_in['alpha'], 'L0_tok_f1_dw': _L0_tok_in['f1_dw'], 'L0_tok_f1_pw': _L0_tok_in['f1_pw'], 'L0_tok_f1_pwb': _L0_tok_in['f1_pwb'], 'L0_tok_f2_dw': _L0_tok_in['f2_dw'], 'L0_tok_f2_pw': _L0_tok_in['f2_pw'], 'L0_tok_f2_pwb': _L0_tok_in['f2_pwb'], 'L0_tok_f3_dw': _L0_tok_in['f3_dw'], 'L0_tok_f3_pw': _L0_tok_in['f3_pw'], 'L0_tok_f3_pwb': _L0_tok_in['f3_pwb'], 'L0_tok_ln_g': _L0_tok_in['ln_g'], 'L0_tok_ln_b': _L0_tok_in['ln_b'], 'L0_tok_cls': _L0_tok_in['cls'], 'L0_attn_W_in': _L0_attn_in['W_in'], 'L0_attn_W_x': _L0_attn_in['W_x'], 'L0_attn_W_dt': _L0_attn_in['W_dt'], 'L0_attn_b_dt': _L0_attn_in['b_dt'], 'L0_attn_A_log': _L0_attn_in['A_log'], 'L0_attn_D_skip': _L0_attn_in['D_skip'], 'L0_attn_W_out': _L0_attn_in['W_out'], 'L0_attn_gamma': _L0_attn_in['gamma'], 'L0_attn_beta': _L0_attn_in['beta'], 'L0_ffn_slot_params': _L0_ffn_in['slot_params'], 'L0_ffn_scale': _L0_ffn_in['scale'], 'L0_ffn_W_down': _L0_ffn_in['W_down'], 'L0_ffn_b_down': _L0_ffn_in['b_down'], 'L0_ffn_W_up': _L0_ffn_in['W_up'], 'L0_ffn_b_up': _L0_ffn_in['b_up']}

def reference(x, L0_tok_pl_w, L0_tok_pl_b, L0_tok_pl_dw, L0_tok_pl_pw, L0_tok_pl_pwb, L0_tok_pg_w1, L0_tok_pg_b1, L0_tok_pg_dw, L0_tok_pg_pw, L0_tok_pg_pwb, L0_tok_pg_w2, L0_tok_pg_b2, L0_tok_alpha, L0_tok_f1_dw, L0_tok_f1_pw, L0_tok_f1_pwb, L0_tok_f2_dw, L0_tok_f2_pw, L0_tok_f2_pwb, L0_tok_f3_dw, L0_tok_f3_pw, L0_tok_f3_pwb, L0_tok_ln_g, L0_tok_ln_b, L0_tok_cls, L0_attn_W_in, L0_attn_W_x, L0_attn_W_dt, L0_attn_b_dt, L0_attn_A_log, L0_attn_D_skip, L0_attn_W_out, L0_attn_gamma, L0_attn_beta, L0_ffn_slot_params, L0_ffn_scale, L0_ffn_W_down, L0_ffn_b_down, L0_ffn_W_up, L0_ffn_b_up):
    import jax
    import jax.numpy as jnp

    def _L0_tok_ref(x, pl_w, pl_b, pl_dw, pl_pw, pl_pwb, pg_w1, pg_b1, pg_dw, pg_pw, pg_pwb, pg_w2, pg_b2, alpha, f1_dw, f1_pw, f1_pwb, f2_dw, f2_pw, f2_pwb, f3_dw, f3_pw, f3_pwb, ln_g, ln_b, cls):
        import jax, jax.numpy as jnp
        import numpy as np
        B, IN, IMG = (64, 3, 224)
        PATCH, LEVELS, D = (16, 4, 192)
        ISQ2 = 0.7071067811865476
        DN = ('NCHW', 'OIHW', 'NCHW')

        def conv(x, w, b=None, stride=1, pad=((0, 0), (0, 0)), groups=1):
            y = jax.lax.conv_general_dilated(x, w, (stride, stride), pad, dimension_numbers=DN, feature_group_count=groups)
            return y if b is None else y + b[None, :, None, None]

        def dwconv(x, wd, wp, bp):
            y = conv(x, wd, pad=((1, 1), (1, 1)), groups=x.shape[1])
            return conv(y, wp, bp)

        def haar_dwt2(x):
            xe, xo = (x[..., ::2], x[..., 1::2])
            lo_w, hi_w = ((xe + xo) * ISQ2, (xe - xo) * ISQ2)

            def split_h(t):
                te, to = (t[..., ::2, :], t[..., 1::2, :])
                return ((te + to) * ISQ2, (te - to) * ISQ2)
            ll, lh = split_h(lo_w)
            hl, hh = split_h(hi_w)
            return (ll, lh, hl, hh)

        def wavelet_packet(x):
            f = x
            for _ in range(LEVELS):
                b, k, h, w = f.shape
                ll, lh, hl, hh = haar_dwt2(f)
                bands = jnp.stack([ll, lh, hl, hh], axis=1)
                bands = bands.reshape(b, 4, k // IN, IN, h // 2, w // 2)
                f = jnp.transpose(bands, (0, 2, 1, 3, 4, 5)).reshape(b, 4 * k, h // 2, w // 2)
            return f

        def gelu(x):
            return jax.nn.gelu(x, approximate=False)

        def forward(x, pl_w, pl_b, pl_dw, pl_pw, pl_pwb, pg_w1, pg_b1, pg_dw, pg_pw, pg_pwb, pg_w2, pg_b2, alpha, f1_dw, f1_pw, f1_pwb, f2_dw, f2_pw, f2_pwb, f3_dw, f3_pw, f3_pwb, ln_g, ln_b, cls):
            loc = conv(x, pl_w, pl_b, stride=PATCH)
            loc = dwconv(gelu(loc), pl_dw, pl_pw, pl_pwb)
            g = wavelet_packet(x)
            g = gelu(conv(g, pg_w1, pg_b1))
            g = gelu(dwconv(g, pg_dw, pg_pw, pg_pwb))
            glob = conv(g, pg_w2, pg_b2)
            gate = 0.5 * (jnp.tanh(alpha) + 1.0)
            h = (1.0 - gate) * loc + gate * glob
            h = jax.nn.relu(dwconv(h, f1_dw, f1_pw, f1_pwb))
            h = jax.nn.relu(dwconv(h, f2_dw, f2_pw, f2_pwb))
            h = dwconv(loc + h, f3_dw, f3_pw, f3_pwb)
            t = jnp.transpose(h.reshape(h.shape[0], D, -1), (0, 2, 1))
            mu = jnp.mean(t, -1, keepdims=True)
            var = jnp.mean((t - mu) ** 2, -1, keepdims=True)
            t = (t - mu) / jnp.sqrt(var + 1e-05) * ln_g + ln_b
            cls_tok = jnp.broadcast_to(cls, (t.shape[0], 1, D))
            return jnp.concatenate([cls_tok, t], axis=1)
        return forward(x, pl_w, pl_b, pl_dw, pl_pw, pl_pwb, pg_w1, pg_b1, pg_dw, pg_pw, pg_pwb, pg_w2, pg_b2, alpha, f1_dw, f1_pw, f1_pwb, f2_dw, f2_pw, f2_pwb, f3_dw, f3_pw, f3_pwb, ln_g, ln_b, cls)

    def _L0_attn_ref(x, W_in, W_x, W_dt, b_dt, A_log, D_skip, W_out, gamma, beta):
        import jax, jax.numpy as jnp
        import numpy as np

        def _selective_scan(dt, Bm, Cm, xp, A):
            Bsz, L, d_inner = xp.shape
            N = A.shape[1]

            def step(h, inp):
                dt_t, B_t, C_t, x_t = inp
                dA = jnp.exp(dt_t[..., None] * A)
                dBx = (dt_t * x_t)[..., None] * B_t[:, None, :]
                h = dA * h + dBx
                y = jnp.einsum('bdn,bn->bd', h, C_t)
                return (h, y)
            h0 = jnp.zeros((Bsz, d_inner, N), dtype=xp.dtype)
            inputs = (jnp.moveaxis(dt, 1, 0), jnp.moveaxis(Bm, 1, 0), jnp.moveaxis(Cm, 1, 0), jnp.moveaxis(xp, 1, 0))
            _, ys = jax.lax.scan(step, h0, inputs)
            return jnp.moveaxis(ys, 0, 1)
        R = W_dt.shape[0]
        N = A_log.shape[1]
        d_inner = A_log.shape[0]
        xz = jnp.einsum('bld,de->ble', x, W_in)
        xp, z = (xz[..., :d_inner], xz[..., d_inner:])
        xp = jax.nn.silu(xp)
        x_dbl = jnp.einsum('bld,dr->blr', xp, W_x)
        dt = jax.nn.softplus(jnp.einsum('blr,rd->bld', x_dbl[..., :R], W_dt) + b_dt)
        Bm = x_dbl[..., R:R + N]
        Cm = x_dbl[..., R + N:]
        A = -jnp.exp(A_log)
        ys = _selective_scan(dt, Bm, Cm, xp, A)
        y = (ys + D_skip * xp) * jax.nn.silu(z)
        mamba_out = jnp.einsum('bld,de->ble', y, W_out)
        h = x + mamba_out
        mu = jnp.mean(h, axis=-1, keepdims=True)
        var = jnp.mean(jnp.square(h - mu), axis=-1, keepdims=True)
        return (h - mu) * jax.lax.rsqrt(var + 1e-05) * gamma + beta

    def _L0_ffn_ref(X, slot_params, scale, W_down, b_down, W_up, b_up):
        import jax, jax.numpy as jnp
        import numpy as np
        EPS = 1e-06

        def l2_normalize(x, axis):
            norm = jnp.sqrt(jnp.square(x).sum(axis=axis, keepdims=True))
            return x * (1.0 / (norm + EPS))
        b, m, d = X.shape
        _, n, p = slot_params.shape
        Xn = l2_normalize(X, axis=-1)
        sp = l2_normalize(slot_params, axis=1) * scale
        logits = jnp.einsum('bmd,dnp->bmnp', Xn, sp)
        D = jax.nn.softmax(logits, axis=1)
        C = jax.nn.softmax(logits.reshape(b, m, n * p), axis=2).reshape(b, m, n, p)
        X_tilde = jnp.einsum('bmd,bmnp->bnpd', Xn, D)
        H = jax.nn.gelu(jnp.einsum('bnpd,ndh->bnph', X_tilde, W_down) + b_down[None, :, None, :], approximate=False)
        Y_tilde = jnp.einsum('bnph,nhd->bnpd', H, W_up) + b_up[None, :, None, :]
        Y = jnp.einsum('bnpd,bmnp->bmd', Y_tilde, C)
        return Y
    h = _L0_tok_ref(x, L0_tok_pl_w, L0_tok_pl_b, L0_tok_pl_dw, L0_tok_pl_pw, L0_tok_pl_pwb, L0_tok_pg_w1, L0_tok_pg_b1, L0_tok_pg_dw, L0_tok_pg_pw, L0_tok_pg_pwb, L0_tok_pg_w2, L0_tok_pg_b2, L0_tok_alpha, L0_tok_f1_dw, L0_tok_f1_pw, L0_tok_f1_pwb, L0_tok_f2_dw, L0_tok_f2_pw, L0_tok_f2_pwb, L0_tok_f3_dw, L0_tok_f3_pw, L0_tok_f3_pwb, L0_tok_ln_g, L0_tok_ln_b, L0_tok_cls)
    h = h + _L0_attn_ref(_layernorm(h, axis=-1), L0_attn_W_in, L0_attn_W_x, L0_attn_W_dt, L0_attn_b_dt, L0_attn_A_log, L0_attn_D_skip, L0_attn_W_out, L0_attn_gamma, L0_attn_beta)
    h = h + _L0_ffn_ref(_layernorm(h, axis=-1), L0_ffn_slot_params, L0_ffn_scale, L0_ffn_W_down, L0_ffn_b_down, L0_ffn_W_up, L0_ffn_b_up)
    return h

_drawn_inputs = setup_inputs


def setup_inputs(seed=0):
    import zlib

    import numpy as np

    out = dict(_drawn_inputs(seed))
    spreads = {'L0_tok_alpha': (0.0, 0.8),
     'L0_tok_ln_g': (1.0, 0.2),
     'L0_tok_ln_b': (0.0, 0.1),
     'L0_attn_D_skip': (1.0, 0.6),
     'L0_attn_gamma': (1.0, 0.2),
     'L0_attn_beta': (0.0, 0.1),
     'L0_ffn_b_down': (0.0, 0.8),
     'L0_ffn_b_up': (0.0, 0.454)}
    factors = {'x': 8.0,
     'L0_tok_pl_w': 8.0,
     'L0_tok_pl_b': 35.974,
     'L0_tok_pl_dw': 8.0,
     'L0_tok_pl_pw': 8.0,
     'L0_tok_pl_pwb': 24.009,
     'L0_tok_pg_w1': 8.0,
     'L0_tok_pg_b1': 64.0,
     'L0_tok_pg_dw': 8.0,
     'L0_tok_pg_pw': 8.0,
     'L0_tok_pg_pwb': 55.809,
     'L0_tok_pg_w2': 8.0,
     'L0_tok_pg_b2': 64.0,
     'L0_tok_f1_dw': 8.0,
     'L0_tok_f1_pw': 8.0,
     'L0_tok_f1_pwb': 61.214,
     'L0_tok_f2_dw': 8.0,
     'L0_tok_f2_pw': 8.0,
     'L0_tok_f2_pwb': 41.785,
     'L0_tok_f3_pw': 2.955,
     'L0_attn_W_in': 8.0,
     'L0_attn_W_x': 8.0,
     'L0_attn_W_dt': 8.0,
     'L0_attn_b_dt': 24.713,
     'L0_attn_A_log': 8.0,
     'L0_attn_W_out': 8.0,
     'L0_ffn_slot_params': 8.0,
     'L0_ffn_W_down': 8.0,
     'L0_ffn_W_up': 5.649}
    for name, (base, spread) in spreads.items():
        noise = np.random.default_rng([zlib.crc32(name.encode()), seed]).standard_normal(out[name].shape)
        drawn = base * np.exp(spread * noise) if base else spread * noise
        out[name] = jnp.asarray(drawn.astype(out[name].dtype))
    for name, factor in factors.items():
        out[name] = (out[name] * factor).astype(out[name].dtype)
    return out
```

```python
from contextlib import ExitStack

import numpy as np
import concourse.bass as bass
from concourse import mybir
from concourse.alu_op_type import AluOpType as ALU

F32 = mybir.dt.float32
BF16 = mybir.dt.bfloat16
ACT = mybir.ActivationFunctionType
AX_X = mybir.AxisListType.X

P = 128
D = 192
HI = D - P
G = 14
PX = G * G
L = PX + 1
TT = 99
HALF = L - TT
KT = 6
PAD = 16
ROWS2 = 2 * (G + 1) + 1
SPAN2 = (2 * G + 1) * G
IMG2 = (G + 1) * G
TAPS = 9
LN_EPS = 1e-5
L2_EPS = 1e-6
DI = 384
DT = DI // P
NS = 16
RANK = 48
NE, NP_, HID = 8, 4, 24
SLOTS = NE * NP_


def bass_vit_tower(nc, t_in, out, pairs, pe_taps=2):
    scratch_h = nc.dram_tensor("scratch_h", [pairs, TT, 4, D], F32, kind="Internal").ap()
    scratch_x = nc.dram_tensor("scratch_x", [pairs, TT, 4, D], F32, kind="Internal").ap()
    scratch_xt = nc.dram_tensor("scratch_xt", [pairs, P, 2, 2 * L], F32, kind="Internal").ap()
    scratch_h2 = nc.dram_tensor("scratch_h2", [pairs, TT, 4, D], F32, kind="Internal").ap()
    embed_images(nc, t_in, scratch_h, scratch_x, scratch_xt, pairs, pe_taps)
    mix_tokens(nc, t_in, scratch_h, scratch_x, scratch_xt, scratch_h2, pairs)
    mix_slots(nc, t_in, scratch_h2, out, pairs)




def embed_images(nc, t_in, h_out, x_out, xt_out, pairs, pe_taps):
    with ExitStack() as ctx:
        def sb(name, shape, dt=F32):
            return ctx.enter_context(nc.sbuf_tensor(name, shape, dt))

        def sem(name):
            return ctx.enter_context(nc.semaphore(name))

        def bank(name):
            return ctx.enter_context(nc.psum_tensor(name, [P, 512], F32))

        ident = sb("a_ident", [P, P])
        haar = sb("a_haar", [P, 2, 256])
        w_wave = sb("a_w_wave", [P, 2, 3, D])
        w_loc = sb("a_w_loc", [P, KT, D])
        w_conv = sb("a_w_conv", [P, KT, 3, P])
        conv_bias = sb("a_conv_bias", [P, 3])
        dw_w = sb("a_dw_w", [P, 9, TAPS])
        dw_diag = sb("a_dw_diag", [P, 9, pe_taps, P])
        pw = {n: sb(f"a_pw_{n}", [P, 6, P]) for n in ("loc", "glob")}
        pw |= {n: sb(f"a_pw_{n}", [P, 6, P]) for n in ("glob2", "fuse1", "fuse2")}
        pw_bias = sb("a_pw_bias", [P, 5, 2])
        pw3 = sb("a_pw3", [P, 3, D])
        bias3 = sb("a_bias3", [P, D])
        row0 = sb("a_row0", [P, TT])
        alpha = sb("a_alpha", [P, 2])
        gate = sb("a_gate", [P, 2])
        one_minus = sb("a_one_minus", [P, 2])
        gate_b = sb("a_gate_b", [P, 2])
        ln_g = sb("a_ln_g", [TT, D])
        ln_b = sb("a_ln_b", [TT, D])
        cls = sb("a_cls", [1, D])
        minus_half = sb("a_minus_half", [TT, 4])
        x_t = sb("a_x_t", [P, KT, 2 * PX])
        pad_first = [sb(f"a_pad_first{t}", [P, ROWS2, PAD]) for t in range(3)]
        acc_first = [sb(f"a_acc_first{t}", [P, 2 * IMG2]) for t in range(3)]
        loc = [sb("a_loc_low", [P, 2 * PX]), sb("a_loc_high", [P, PX])]
        loc_old = [sb("a_loc_old_low", [P, 2 * PX]), sb("a_loc_old_high", [P, PX])]
        gg = [sb("a_gg_low", [P, 2 * PX]), sb("a_gg_high", [P, PX])]
        loc_part = [sb("a_loc_part_low", [P, 2 * PX]), sb("a_loc_part_high", [P, PX])]
        pad = {k: [sb(f"a_pad{k}_low", [P, ROWS2, PAD]), sb(f"a_pad{k}_high", [P, PAD, PAD])] for k in (1, 2, 3)}
        acc = {k: [sb(f"a_acc{k}_low", [P, 2 * IMG2]), sb(f"a_acc{k}_high", [P, PX])] for k in (1, 2)}
        acc[3] = [sb("a_acc3_low", [P, 1 + 2 * IMG2]), sb("a_acc3_high", [P, 1 + PX])]
        relu2 = [sb("a_relu2_low", [P, 2 * PX]), sb("a_relu2_high", [P, PX])]
        tok = sb("a_tok", [TT, 4, D])
        st1 = sb("a_st1", [TT, 4, 6])
        mv1 = sb("a_mv1", [TT, 4, 2])
        ve1 = sb("a_ve1", [TT, 4])
        rs1 = sb("a_rs1", [TT, 4])
        hn = sb("a_hn", [TT, 4, D])
        hg = sb("a_hg", [TT, 4, D])
        h = sb("a_h", [TT, 4, D])
        st2 = sb("a_st2", [TT, 4, 6])
        mv2 = sb("a_mv2", [TT, 4, 2])
        ve2 = sb("a_ve2", [TT, 4])
        rs2 = sb("a_rs2", [TT, 4])
        xn = sb("a_xn", [TT, 4, D])
        xt = sb("a_xt", [P, 2, 2 * L])

        conv_ps = [bank("a_conv_ps0"), bank("a_conv_ps1")]
        tap_ps = [bank("a_tap_ps0"), bank("a_tap_ps1")]
        pw_ps = [bank("a_pw_ps_low"), bank("a_pw_ps_high")]
        tok_ps = bank("a_tok_ps")
        tr_ps = bank("a_tr_ps")

        S = {n: sem("a_" + n) for n in (
            "fence",
            "weights", "zeroed", "setup", "fold_done", "fold_copied", "diag", "gate_ready", "gate_act",
            "x_loaded", "conv_done", "gelu_done",
            "taps_first", "first_chain", "first_dw",
            "taps1", "chain1", "dw1", "taps2", "chain2", "dw2",
            "taps3", "chain3", "dw3",
            "pw_loc", "loc_out", "pw_glob", "gg_out", "pw_glob2", "part_out", "fused",
            "pw1", "relu1", "pw2", "relu2", "loc_kept", "joined",
            "tok_done", "tok_copied", "ln1_stats", "ln1_rs", "ln1_norm", "ln1_affine",
            "ln2_stats", "ln2_rs", "ln2_norm", "tr_done", "tr_copied", "h_stored", "x_stored", "xt_stored")}

        def maps(t):
            flat = t[:].rearrange("p r c -> p (r c)")
            return flat[:, 0:2 * (G + 1) * PAD].rearrange("p (i r c) -> p i r c", i=2, r=G + 1)[:, :, 1:G + 1, 1:G + 1]

        def shifted(t, tap, rows):
            dy, dx = tap // 3, tap % 3
            return t[:, dy:dy + rows, dx:dx + G]

        def grid(t, rows, lo=0):
            return t[:, lo:lo + rows * G].rearrange("p (r c) -> p r c", c=G)

        def as_maps(t):
            return t.rearrange("p (i r c) -> p i r c", i=2, r=G)

        layers = {
            "first": (0, pad_first, acc_first, [2 * G + 1] * 3, 0),
            "1": (3, pad[1], acc[1], [2 * G + 1, G], 0),
            "2": (5, pad[2], acc[2], [2 * G + 1, G], 0),
            "3": (7, pad[3], acc[3], [2 * G + 1, G], 1),
        }

        def span_of(t, img, lo=0, n=PX):
            return t[:, lo + img * IMG2:lo + img * IMG2 + n]

        def both(t):
            n = t.shape[1] // 2
            return t[:, 0:2 * n].rearrange("p (i n) -> p i n", i=2)[:, :, 0:PX]

        block = ctx.enter_context(nc.Block())

        loads = [(ident, "ident"), (haar, "haar"), (w_wave, "w_wave"), (w_loc, "w_loc"), (conv_bias, "conv_bias"),
                 (dw_w, "dw_w"), (pw["loc"], "pw_loc"), (pw["glob"], "pw_glob"), (pw["glob2"], "pw_glob2"),
                 (pw["fuse1"], "pw_fuse1"), (pw["fuse2"], "pw_fuse2"), (pw_bias, "pw_bias"), (pw3, "pw3"),
                 (bias3, "bias3"), (row0, "row0"), (alpha, "alpha"), (ln_g, "ln_g"), (ln_b, "ln_b"), (cls, "cls")]
        chain2, chain3 = 2 * (TAPS - pe_taps - 1), 3 * (TAPS - pe_taps - 1)
        stages = 6

        def run(eng, body):
            for it in range(stages - 1):
                body(it, [0 <= it - s < pairs for s in range(stages)])
            if pairs > stages - 1:
                with eng.Fori(stages - 1, pairs) as it:
                    body(it, [True] * stages)
            for it in range(max(pairs, stages - 1), pairs + stages - 1):
                body(it, [0 <= it - s < pairs for s in range(stages)])

        def capped(value, most):
            return min(value, most) if type(value) is int else value

        @block.sync
        def _(sp):
            for dst, name in loads:
                sp.dma_start(dst[:], t_in[name]).then_inc(S["weights"], 16)

            def body(it, on):
                if on[0]:
                    if not (type(it) is int and it == 0):
                        sp.wait_ge(S["conv_done"], it * 3)
                    sp.dma_start(x_t[:], t_in["x_t"][it]).then_inc(S["x_loaded"], 16)
                if on[4]:
                    p = it - 4
                    sp.wait_ge(S["ln1_affine"], p * 4 + 4)
                    sp.dma_start(h_out[p], h[:]).then_inc(S["h_stored"], 16)
                if on[5]:
                    p = it - 5
                    sp.wait_ge(S["ln2_norm"], p * 4 + 4)
                    sp.dma_start(x_out[p], xn[:]).then_inc(S["x_stored"], 16)
                    sp.wait_ge(S["tr_copied"], p * 2 + 2)
                    sp.dma_start(xt_out[p], xt[:]).then_inc(S["xt_stored"], 16)

            run(sp, body)
            sp.wait_ge(S["h_stored"], 16 * pairs)
            sp.wait_ge(S["x_stored"], 16 * pairs)
            sp.wait_ge(S["xt_stored"], 16 * pairs)

        @block.tensor
        def _(pe):
            pe.wait_ge(S["weights"], 16 * len(loads))
            for n in range(KT):
                colour, m = n // 2, n % 2
                if n >= 2:
                    pe.wait_ge(S["fold_copied"], 2 * (n - 1))
                for b in range(2):
                    mm = pe.matmul(conv_ps[n % 2][:, 0:D], haar[:, b, m * P:(m + 1) * P], w_wave[:, b, colour, :],
                                   start=(b == 0), stop=(b == 1))
                mm.then_inc(S["fold_done"], 1)
            pe.wait_ge(S["fold_copied"], 2 * KT)
            pe.wait_ge(S["setup"], 1)
            pe.wait_ge(S["diag"], 9 * pe_taps)
            pe.wait_ge(S["zeroed"], 1)

            def conv(it, t):
                if t == 0:
                    pe.wait_ge(S["x_loaded"], it * 16 + 16)
                if t == 2:
                    pe.wait_ge(S["gelu_done"], it * 3 + 1)
                elif not (type(it) is int and it == 0):
                    pe.wait_ge(S["gelu_done"], it * 3 if t == 0 else it * 3 - 1)
                for k in range(KT):
                    mm = pe.matmul(conv_ps[t % 2][:, 0:2 * PX], w_conv[:, k, t, :], x_t[:, k, :],
                                   start=(k == 0), stop=(k == KT - 1))
                mm.then_inc(S["conv_done"], 1)

            def taps(name, t):
                first, pads, _, rows, _ = layers[name]
                for k in range(pe_taps):
                    mm = pe.matmul(grid(tap_ps[t % 2], rows[t]), dw_diag[:, first + t, k, :],
                                   shifted(pads[t], k, rows[t]), start=(k == 0), stop=(k == pe_taps - 1))
                mm.then_inc(S["taps_first" if name == "first" else "taps" + name], 1)

            def pointwise_first(w, low, mixed, done):
                pe.matmul(both(pw_ps[0][:, 0:2 * PX]), w[:, 0, :], both(low), start=True, stop=False)
                pe.matmul(both(pw_ps[0][:, 0:2 * PX]), w[:, 1, :], both(mixed), start=False, stop=True).then_inc(done, 1)
                for img in range(2):
                    pe.matmul(pw_ps[1][:, 0:PX], w[:, 2 + 2 * img, :], span_of(low, img), start=(img == 0), stop=False)
                    mm = pe.matmul(pw_ps[1][:, 0:PX], w[:, 3 + 2 * img, :], span_of(mixed, img), start=False, stop=(img == 1))
                mm.then_inc(done, 1)

            def pointwise_one(w, low, high, done):
                pe.matmul(both(pw_ps[0][:, 0:2 * PX]), w[:, 0, :], both(low), start=True, stop=False)
                for img in range(2):
                    mm = pe.matmul(pw_ps[0][:, img * PX:(img + 1) * PX], w[:, 1 + img, :], high[:, :],
                                   start=False, stop=(img == 1))
                mm.then_inc(done, 1)
                for img in range(2):
                    pe.matmul(pw_ps[1][:, 0:PX], w[:, 3 + img, :], both(low)[:, img, :], start=(img == 0), stop=False)
                pe.matmul(pw_ps[1][:, 0:PX], w[:, 5, :], high[:, :], start=False, stop=True).then_inc(done, 1)

            def body(it, on):
                if on[3]:
                    p = it - 3
                    pe.wait_ge(S["joined"], p * 2 + 2)
                    pe.wait_ge(S["first_chain"], capped(it * chain3, pairs * chain3))
                    taps("3", 0)
                    taps("3", 1)
                if on[0]:
                    conv(it, 0)
                if on[2]:
                    p = it - 2
                    if on[3]:
                        pe.wait_ge(S["chain3"], (it - 3) * chain2 + 2)
                    else:
                        pe.wait_ge(S["first_chain"], it * chain3)
                    pe.wait_ge(S["relu1"], p * 2 + 2)
                    taps("2", 0)
                    taps("2", 1)
                if on[5]:
                    p = it - 5
                    pe.wait_ge(S["ln2_norm"], p * 4 + 4)
                    for part in range(2):
                        if not (type(p) is int and p == 0 and part == 0):
                            pe.wait_ge(S["tr_copied"], p * 2 + part)
                        for q in range(4):
                            o = tr_ps[:, (q // 2) * L + (q % 2) * HALF:(q // 2) * L + (q % 2) * HALF + TT]
                            mm = pe.transpose(o, xn[:, q, part * HI:part * HI + P], ident[0:TT, 0:TT])
                        mm.then_inc(S["tr_done"], 1)
                if on[0]:
                    conv(it, 1)
                if on[3]:
                    p = it - 3
                    pe.wait_ge(S["dw3"], p * 2 + 2)
                    for img in range(2):
                        if not (type(p) is int and p == 0 and img == 0):
                            pe.wait_ge(S["tok_copied"], p * 2 + img)
                        for half in range(2):
                            o = tok_ps[0:TT, half * D:(half + 1) * D]
                            lo = img * IMG2 + half * HALF
                            pe.matmul(o, acc[3][0][:, lo:lo + TT], pw3[:, 0, :], start=True, stop=False)
                            pe.matmul(o, acc[3][1][:, half * HALF:half * HALF + TT], pw3[:, 1 + img, :],
                                      start=False, stop=False)
                            mm = pe.matmul(o, row0[:, :], bias3[:, :], start=False, stop=True)
                        mm.then_inc(S["tok_done"], 1)
                if on[1]:
                    p = it - 1
                    if on[2]:
                        pe.wait_ge(S["chain2"], (it - 2) * chain2 + 2)
                    else:
                        pe.wait_ge(S["first_chain"], it * chain3)
                    pe.wait_ge(S["fused"], p * 3 + 3)
                    taps("1", 0)
                    taps("1", 1)
                if on[0]:
                    conv(it, 2)
                if on[2]:
                    p = it - 2
                    pe.wait_ge(S["dw2"], p * 2 + 2)
                    pe.wait_ge(S["fused"], capped(p * 3 + 6, pairs * 3))
                    pointwise_one(pw["fuse2"], acc[2][0], acc[2][1], S["pw2"])
                if on[0]:
                    if on[1]:
                        pe.wait_ge(S["chain1"], (it - 1) * chain2 + 2)
                    pe.wait_ge(S["gelu_done"], it * 3 + 2)
                    taps("first", 0)
                    taps("first", 1)
                    pe.wait_ge(S["gelu_done"], it * 3 + 3)
                    pe.wait_ge(S["first_chain"], it * chain3 + 1)
                    taps("first", 2)
                if on[1]:
                    p = it - 1
                    pe.wait_ge(S["dw1"], p * 2 + 2)
                    if on[2]:
                        pe.wait_ge(S["relu2"], (it - 2) * 2 + 2)
                    else:
                        pe.wait_ge(S["fused"], p * 3 + 3)
                    pointwise_one(pw["fuse1"], acc[1][0], acc[1][1], S["pw1"])
                if on[0]:
                    pe.wait_ge(S["first_dw"], it * 3 + 3)
                    if on[1]:
                        pe.wait_ge(S["relu1"], (it - 1) * 2 + 2)
                    pointwise_first(pw["loc"], acc_first[0], acc_first[2], S["pw_loc"])
                    pe.wait_ge(S["loc_out"], it * 2 + 2)
                    pointwise_first(pw["glob"], acc_first[1], acc_first[2], S["pw_glob"])
                    pe.wait_ge(S["gg_out"], it * 2 + 2)
                    pointwise_one(pw["glob2"], gg[0], gg[1], S["pw_glob2"])

            run(pe, body)

        @block.scalar
        def _(act):
            act.wait_ge(S["weights"], 16 * len(loads))
            for n in range(KT):
                act.wait_ge(S["fold_done"], n + 1)
                nc.scalar.copy(w_conv[:, n, 1, :], conv_ps[n % 2][:, 0:P]).then_inc(S["fold_copied"], 1)
                nc.scalar.copy(w_conv[:, n, 2, HI:P], conv_ps[n % 2][:, P:D]).then_inc(S["fold_copied"], 1)
            nc.scalar.activation(gate[:, :], alpha[:, :], ACT.Tanh).then_inc(S["gate_act"], 1)
            act.wait_ge(S["gate_ready"], 3)
            act.wait_ge(S["zeroed"], 1)

            def body(it, on):
                def gelu(t):
                    act.wait_ge(S["conv_done"], it * 3 + t + 1)
                    if not (type(it) is int and it == 0):
                        act.wait_ge(S["first_dw"], it * 3)
                    nc.scalar.activation(maps(pad_first[t]), as_maps(conv_ps[t % 2][:, 0:2 * PX]), ACT.Gelu,
                                         bias=conv_bias[:, t:t + 1]).then_inc(S["gelu_done"], 1)

                if on[0]:
                    gelu(0)
                if on[5]:
                    p = it - 5
                    for part in range(2):
                        act.wait_ge(S["tr_done"], p * 2 + part + 1)
                        if part == 0 and not (type(p) is int and p == 0):
                            act.wait_ge(S["xt_stored"], p * 16)
                        nc.scalar.copy(xt[:, part, :], tr_ps[:, 0:2 * L]).then_inc(S["tr_copied"], 1)
                if on[0]:
                    gelu(1)
                if on[3]:
                    p = it - 3
                    for img in range(2):
                        act.wait_ge(S["tok_done"], p * 2 + img + 1)
                        if img == 0 and not (type(p) is int and p == 0):
                            act.wait_ge(S["ln1_norm"], p * 4)
                        nc.scalar.copy(tok[:, 2 * img:2 * img + 2, :],
                                       tok_ps[0:TT, 0:2 * D].rearrange("p (h c) -> p h c", h=2)).then_inc(S["tok_copied"], 1)
                if on[0]:
                    gelu(2)
                if on[2]:
                    p = it - 2
                    for t in range(2):
                        act.wait_ge(S["pw2"], p * 2 + t + 1)
                        if t == 0 and not (type(p) is int and p == 0):
                            act.wait_ge(S["joined"], p * 2)
                        nc.scalar.activation(relu2[t][:, :], pw_ps[t][:, 0:(2 - t) * PX], ACT.Relu,
                                             bias=pw_bias[:, 4, t:t + 1]).then_inc(S["relu2"], 1)
                if on[1]:
                    p = it - 1
                    for t in range(2):
                        act.wait_ge(S["pw1"], p * 2 + t + 1)
                        if t == 0 and not (type(p) is int and p == 0):
                            act.wait_ge(S["dw2"], p * 2)
                        dst, src = ((maps(pad[2][0]), as_maps(pw_ps[0][:, 0:2 * PX])) if t == 0 else
                                    (pad[2][1][:, 1:G + 1, 1:G + 1], grid(pw_ps[1], G)))
                        nc.scalar.activation(dst, src, ACT.Relu, bias=pw_bias[:, 3, t:t + 1]).then_inc(S["relu1"], 1)
                if on[0]:
                    for t in range(2):
                        act.wait_ge(S["pw_loc"], it * 2 + t + 1)
                        if t == 0 and not (type(it) is int and it == 0):
                            act.wait_ge(S["loc_kept"], it * 2)
                            act.wait_ge(S["part_out"], it * 2)
                        nc.scalar.activation(loc[t][:, :], pw_ps[t][:, 0:(2 - t) * PX], ACT.Identity,
                                             bias=pw_bias[:, 0, t:t + 1]).then_inc(S["loc_out"], 1)
                    for t in range(2):
                        act.wait_ge(S["pw_glob"], it * 2 + t + 1)
                        if t == 0 and not (type(it) is int and it == 0):
                            act.wait_ge(S["pw_glob2"], it * 2)
                        nc.scalar.activation(gg[t][:, :], pw_ps[t][:, 0:(2 - t) * PX], ACT.Gelu,
                                             bias=pw_bias[:, 1, t:t + 1]).then_inc(S["gg_out"], 1)
                    for t in range(2):
                        act.wait_ge(S["loc_out"], it * 2 + 2)
                        if t == 0 and not (type(it) is int and it == 0):
                            act.wait_ge(S["fused"], it * 3)
                        nc.scalar.activation(loc_part[t][:, :], loc[t][:, :], ACT.Identity, scale=one_minus[:, t:t + 1],
                                             bias=gate_b[:, t:t + 1]).then_inc(S["part_out"], 1)

            run(act, body)

        @block.gpsimd
        def _(pool):
            for t in pad_first + pad[1] + pad[2] + pad[3]:
                nc.gpsimd.memset(t[:], 0.0)
            nc.gpsimd.memset(acc[3][0][:, 0:1], 0.0)
            nc.gpsimd.memset(acc[3][1][:, 0:1], 0.0)
            nc.gpsimd.memset(minus_half[:], -0.5).then_inc(S["zeroed"], 1)
            pool.wait_ge(S["weights"], 16 * len(loads))
            pool.wait_ge(S["zeroed"], 1)

            def body(it, on):
                if on[5]:
                    p = it - 5
                    pool.wait_ge(S["ln2_stats"], p * 9 + 9)
                    nc.gpsimd.tensor_tensor(rs2[:, :], ve2[:, :], minus_half[:, :], ALU.pow).then_inc(S["ln2_rs"], 1)
                if on[4]:
                    p = it - 4
                    pool.wait_ge(S["ln1_stats"], p * 9 + 9)
                    nc.gpsimd.tensor_tensor(rs1[:, :], ve1[:, :], minus_half[:, :], ALU.pow).then_inc(S["ln1_rs"], 1)
                    pool.wait_ge(S["ln1_norm"], p * 4 + 4)
                    nc.gpsimd.tensor_tensor(hg[:, :, :], hn[:, :, :], ln_g[:, :].unsqueeze(1).broadcast_to([TT, 4, D]),
                                            ALU.mult).then_inc(S["ln1_affine"], 1)
                    pool.wait_ge(S["ln1_affine"], p * 4 + 1)
                    if not (type(p) is int and p == 0):
                        pool.wait_ge(S["h_stored"], p * 16)
                        pool.wait_ge(S["ln2_norm"], p * 4)
                    nc.gpsimd.tensor_tensor(h[:, :, :], hg[:, :, :], ln_b[:, :].unsqueeze(1).broadcast_to([TT, 4, D]),
                                            ALU.add).then_inc(S["ln1_affine"], 1)
                    pool.wait_ge(S["ln1_affine"], p * 4 + 2)
                    for img in range(2):
                        if img == 0:
                            pool.sem_inc(S["fence"], 1)
                        nc.gpsimd.tensor_copy(h[0:1, 2 * img, :], cls[0:1, :]).then_inc(S["ln1_affine"], 1)
                if on[2]:
                    p = it - 2
                    for t in range(2):
                        pool.wait_ge(S["relu2"], p * 2 + t + 1)
                        if t == 0 and not (type(p) is int and p == 0):
                            pool.wait_ge(S["dw3"], p * 2)
                        if t == 0:
                            pool.wait_ge(S["loc_kept"], p * 2 + 2)
                            nc.gpsimd.tensor_tensor(maps(pad[3][0]), as_maps(relu2[0][:, :]), as_maps(loc_old[0][:, :]),
                                                    ALU.add).then_inc(S["joined"], 1)
                        else:
                            nc.gpsimd.tensor_tensor(pad[3][1][:, 1:G + 1, 1:G + 1], grid(relu2[1], G), grid(loc_old[1], G),
                                                    ALU.add).then_inc(S["joined"], 1)
                if on[1]:
                    p = it - 1
                    for t in range(2):
                        pool.wait_ge(S["loc_out"], p * 2 + t + 1)
                        if on[2]:
                            pool.wait_ge(S["joined"], (it - 2) * 2 + t + 1)
                        pool.sem_inc(S["fence"], 1)
                        nc.gpsimd.tensor_copy(loc_old[t][:, :], loc[t][:, :]).then_inc(S["loc_kept"], 1)

            run(pool, body)

        @block.vector
        def _(dve):
            dve.wait_ge(S["weights"], 16 * len(loads))
            for n in range(KT):
                nc.vector.tensor_copy(w_conv[:, n, 0, :], w_loc[:, n, 0:P])
                last = nc.vector.tensor_copy(w_conv[:, n, 2, 0:HI], w_loc[:, n, P:D])
            last.then_inc(S["setup"], 1)
            for q in range(9):
                for k in range(pe_taps):
                    nc.vector.tensor_scalar(dw_diag[:, q, k, :], ident[:, :], dw_w[:, q, k:k + 1], None,
                                            ALU.mult).then_inc(S["diag"], 1)
            dve.wait_ge(S["gate_act"], 1)
            nc.vector.tensor_scalar(one_minus[:, :], gate[:, :], -0.5, 0.5, ALU.mult, ALU.add).then_inc(S["gate_ready"], 1)
            dve.wait_ge(S["gate_ready"], 1)
            nc.vector.tensor_scalar(gate[:, :], gate[:, :], 0.5, 0.5, ALU.mult, ALU.add).then_inc(S["gate_ready"], 1)
            dve.wait_ge(S["gate_ready"], 2)
            nc.vector.tensor_tensor(gate_b[:, :], gate[:, :], pw_bias[:, 2, :], ALU.mult).then_inc(S["gate_ready"], 1)
            dve.wait_ge(S["gate_ready"], 3)
            dve.wait_ge(S["zeroed"], 1)

            def depthwise(name, p, dep_sem, dep):
                first, pads, accs, rows, lo = layers[name]
                n = len(pads)
                steps = TAPS - pe_taps
                taps_done = S["taps_first" if name == "first" else "taps" + name]
                chain = S["first_chain" if name == "first" else "chain" + name]
                done = S["first_dw" if name == "first" else "dw" + name]
                order = [(k - 2 * (t // 2), t) for k in range(steps + 2) for t in range(n) if 0 <= k - 2 * (t // 2) < steps]
                at = {}
                count = 0
                per = n * (steps - 1)
                for k, t in order:
                    tap = pe_taps + k
                    dst = grid(accs[t], rows[t], lo)
                    if k == 0:
                        dve.wait_ge(taps_done, p * n + t + 1)
                        src = grid(tap_ps[t % 2], rows[t])
                        if t == 0 and dep is not None:
                            dve.wait_ge(dep_sem, dep)
                    else:
                        dve.wait_ge(chain, p * per + at[t])
                        src = dst
                    ins = nc.vector.scalar_tensor_tensor(out=dst, in0=shifted(pads[t], tap, rows[t]),
                                                         scalar=dw_w[:, first + t, tap:tap + 1], in1=src,
                                                         op0=ALU.mult, op1=ALU.add)
                    if k < steps - 1:
                        ins.then_inc(chain, 1)
                        count += 1
                        at[t] = count
                    else:
                        ins.then_inc(done, 1)

            def stats(p, src, st, mv, ve, s, norm):
                if not (type(p) is int and p == 0):
                    dve.wait_ge(norm, p * 4)
                for q in range(4):
                    nc.vector.bn_stats(st[:, q, :], src[:, q, :]).then_inc(s, 1)
                for q in range(4):
                    dve.wait_ge(s, p * 9 + q + 1)
                    dve.sem_inc(S["fence"], 1)
                    nc.vector.bn_aggr(mv[:, q, :], st[:, q, :]).then_inc(s, 1)
                dve.wait_ge(s, p * 9 + 8)
                nc.vector.tensor_scalar(ve[:, :], mv[:, :, 1], LN_EPS, None, ALU.add).then_inc(s, 1)

            def normalise(dst, src, mv, rs, s):
                for q in range(4):
                    nc.vector.tensor_scalar(dst[:, q, :], src[:, q, :], mv[:, q, 0:1], rs[:, q:q + 1],
                                            ALU.subtract, ALU.mult).then_inc(s, 1)

            def body(it, on):
                if on[5]:
                    p = it - 5
                    dve.wait_ge(S["ln1_affine"], p * 4 + 4)
                    if not (type(p) is int and p == 0):
                        dve.wait_ge(S["ln2_rs"], p)
                    stats(p, h, st2, mv2, ve2, S["ln2_stats"], S["ln2_norm"])
                if on[4]:
                    p = it - 4
                    dve.wait_ge(S["tok_copied"], p * 2 + 2)
                    if not (type(p) is int and p == 0):
                        dve.wait_ge(S["ln1_rs"], p)
                    stats(p, tok, st1, mv1, ve1, S["ln1_stats"], S["ln1_norm"])
                if on[3]:
                    p = it - 3
                    first = type(p) is int and p == 0
                    depthwise("3", p, S["tok_done"], None if first else p * 2)
                if on[5]:
                    p = it - 5
                    dve.wait_ge(S["ln2_rs"], p + 1)
                    if not (type(p) is int and p == 0):
                        dve.wait_ge(S["x_stored"], p * 16)
                        dve.wait_ge(S["tr_done"], p * 2)
                    normalise(xn, h, mv2, rs2, S["ln2_norm"])
                if on[4]:
                    p = it - 4
                    dve.wait_ge(S["ln1_rs"], p + 1)
                    if not (type(p) is int and p == 0):
                        dve.wait_ge(S["ln1_affine"], p * 4)
                    normalise(hn, tok, mv1, rs1, S["ln1_norm"])
                if on[1]:
                    p = it - 1
                    if not (type(p) is int and p == 0):
                        dve.wait_ge(S["dw1"], p * 2)
                    dve.wait_ge(S["part_out"], p * 2 + 2)
                    dve.wait_ge(S["pw_glob2"], p * 2 + 2)
                    for img in range(2):
                        nc.vector.scalar_tensor_tensor(out=pad[1][0][:, 1 + img * (G + 1):1 + img * (G + 1) + G, 1:G + 1],
                                                       in0=grid(pw_ps[0], G, img * PX), scalar=gate[:, 0:1],
                                                       in1=grid(loc_part[0], G, img * PX),
                                                       op0=ALU.mult, op1=ALU.add).then_inc(S["fused"], 1)
                    nc.vector.scalar_tensor_tensor(out=pad[1][1][:, 1:G + 1, 1:G + 1], in0=grid(pw_ps[1], G),
                                                   scalar=gate[:, 1:2], in1=grid(loc_part[1], G),
                                                   op0=ALU.mult, op1=ALU.add).then_inc(S["fused"], 1)
                if on[2]:
                    p = it - 2
                    first = type(p) is int and p == 0
                    depthwise("2", p, S["pw2"], None if first else p * 2)
                if on[1]:
                    p = it - 1
                    first = type(p) is int and p == 0
                    depthwise("1", p, S["pw1"], None if first else p * 2)
                if on[0]:
                    first = type(it) is int and it == 0
                    depthwise("first", it, S["pw_glob"], None if first else it * 2)

            run(dve, body)


def mix_tokens(nc, t_in, h_in, x_in, xt_in, h_out, pairs):
    assert pairs % 2 == 0 and pairs >= 4
    W = 2 * L
    UNITS = NS * DT
    with ExitStack() as ctx:
        def sb(name, shape, dt=F32):
            return ctx.enter_context(nc.sbuf_tensor(name, shape, dt))

        def sem(name):
            return ctx.enter_context(nc.semaphore(name))

        def bank(name):
            return ctx.enter_context(nc.psum_tensor(name, [P, 512], F32))

        ident = sb("b_ident", [P, P])
        w_in = sb("b_w_in", [P, 2, 2 * DT, P])
        w_x = sb("b_w_x", [P, DT, P])
        w_bc = sb("b_w_bc", [P, DT, 96])
        w_dt = sb("b_w_dt", [P, DT, P])
        b_dt = sb("b_b_dt", [P, DT])
        a_log = sb("b_a_log", [P, DT, NS])
        a_exp = sb("b_a_exp", [P, DT, NS])
        a_neg = sb("b_a_neg", [P, DT, NS])
        d_skip = sb("b_d_skip", [P, DT])
        w_out = sb("b_w_out", [P, DT, D])
        gamma = sb("b_gamma", [TT, D])
        beta = sb("b_beta", [TT, D])
        pick_f = sb("b_pick_f", [96, 2 * NS, P])
        pick = sb("b_pick", [96, 2 * NS, P], BF16)
        minus_half = sb("b_minus_half", [TT, 4])

        xt = sb("b_xt", [P, 2, W])
        xz = [sb(f"b_xz{q}", [P, 2 * DT, W]) for q in range(2)]
        xd = sb("b_xd", [P, W])
        bc_f = sb("b_bc_f", [96, W])
        bc_hi = sb("b_bc_hi", [96, W], BF16)
        bc_r = sb("b_bc_r", [96, W])
        bc_mid = sb("b_bc_mid", [96, W], BF16)
        bc = [sb(f"b_bc{q}", [96, W], BF16) for q in range(2)]
        absd = sb("b_absd", [P, DT, W])
        relud = sb("b_relud", [P, DT, W])
        expd = sb("b_expd", [P, DT, W])
        onep = sb("b_onep", [P, DT, W])
        logd = sb("b_logd", [P, DT, W])
        lost = sb("b_lost", [P, DT, W])
        sumd = sb("b_sumd", [P, DT, W])
        dt = [sb(f"b_dt{q}", [P, DT, W]) for q in range(2)]
        dtx = [sb(f"b_dtx{q}", [P, DT, W]) for q in range(2)]
        b_row = [sb(f"b_b_row{i}", [P, W]) for i in range(2)]
        dbx = [sb(f"b_dbx{i}", [P, W]) for i in range(2 * DT)]
        hid = [sb(f"b_hid{i}", [P, W]) for i in range(3)]
        prod = [sb(f"b_prod{i}", [P, W]) for i in range(4)]
        yd = sb("b_yd", [P, DT, W])
        yg = sb("b_yg", [P, DT, W])
        mo = sb("b_mo", [TT, 4, D])
        xn = sb("b_xn", [TT, 4, D])
        hin = sb("b_hin", [TT, 4, D])
        hs = sb("b_hs", [TT, 4, D])
        st = sb("b_st", [TT, 4, 6])
        mv = sb("b_mv", [TT, 4, 2])
        ve = sb("b_ve", [TT, 4])
        rs = sb("b_rs", [TT, 4])
        hn = sb("b_hn", [TT, 4, D])
        ha = sb("b_ha", [TT, 4, D])
        hb = sb("b_hb", [TT, 4, D])
        h2 = sb("b_h2", [TT, 4, D])

        da_ps = [bank("b_da_ps0"), bank("b_da_ps1")]
        y_ps = [bank(f"b_y_ps{j}") for j in range(DT)]
        b_ps = bank("b_b_ps")
        c_ps = bank("b_c_ps")
        ob = bank("b_ob")

        S = {n: sem("b_" + n) for n in (
            "fence", "weights", "zeroed", "picks", "a_ready", "xt_loaded", "xn_loaded", "h_loaded",
            "in_done", "in_out", "silu", "bc_parts", "bc_rest", "dt_relu", "dt_act", "dt_ready", "dtx_ready",
            "b_done", "b_out", "c_done", "exp_done", "dbx_done", "scan_done", "prod_done", "acc_done",
            "yd_done", "yg_done", "out_done", "mo_out", "res", "stats", "rs_ready", "norm", "affine", "stored")}

        loads = [(ident, "ident"), (w_in, "w_in"), (w_x, "w_x"), (w_bc, "w_bc"), (w_dt, "w_dt"), (b_dt, "b_dt"),
                 (a_log, "a_log"), (d_skip, "d_skip"), (w_out, "w_out"), (gamma, "gamma"), (beta, "beta"), (pick_f, "pick")]

        def run(eng, body):
            body(-1, 1, False, False, True)
            body(0, 0, False, True, True)
            with eng.Fori(0, (pairs - 2) // 2) as m:
                body(m * 2 + 1, 1, True, True, True)
                body(m * 2 + 2, 0, True, True, True)
            body(pairs - 1, 1, True, True, False)
            body(pairs, 0, True, False, False)

        def late(p):
            return not (type(p) is int and p == 0)

        def images(t):
            return t.rearrange("p (i l) -> p i l", i=2)

        STATES = range(NS)

        block = ctx.enter_context(nc.Block())

        @block.sync
        def _(sp):
            for dst, name in loads:
                sp.dma_start(dst[:], t_in[name]).then_inc(S["weights"], 16)

            def body(k, q, last, now, nxt):
                if nxt:
                    p = k + 1
                    if late(p):
                        sp.wait_ge(S["in_done"], p * 11 - 5)
                    sp.dma_start(xt[:], xt_in[p]).then_inc(S["xt_loaded"], 16)
                if last:
                    p = k - 1
                    if late(p):
                        sp.wait_ge(S["res"], p)
                    sp.dma_start(xn[:], x_in[p]).then_inc(S["xn_loaded"], 16)
                    if late(p):
                        sp.wait_ge(S["affine"], p * 3)
                    sp.dma_start(hin[:], h_in[p]).then_inc(S["h_loaded"], 16)
                    sp.wait_ge(S["affine"], p * 3 + 3)
                    sp.dma_start(h_out[p], h2[:]).then_inc(S["stored"], 16)

            run(sp, body)
            sp.wait_ge(S["stored"], pairs * 16)

        @block.tensor
        def _(pe):
            pe.wait_ge(S["weights"], 16 * len(loads))
            pe.wait_ge(S["picks"], 1)

            def start(p, q, i):
                if i == 0:
                    pe.wait_ge(S["xt_loaded"], p * 16 + 16)
                if i == 6:
                    pe.wait_ge(S["silu"], p + 1)
                if late(p) or i > 0:
                    pe.wait_ge(S["in_out"], p * 11 + i)
                o = ob[:, 0:W]
                if i < 6:
                    for part in range(2):
                        mm = pe.matmul(o, w_in[:, part, i, :], xt[:, part, :], start=(part == 0), stop=(part == 1))
                elif i == 6:
                    for j in range(DT):
                        mm = pe.matmul(o, w_x[:, j, :], xz[q][:, j, :], start=(j == 0), stop=(j == DT - 1))
                elif i == 7:
                    for j in range(DT):
                        mm = pe.matmul(o[0:96, :], w_bc[:, j, :], xz[q][:, j, :], start=(j == 0), stop=(j == DT - 1))
                else:
                    mm = pe.matmul(o, w_dt[:, i - 8, :], xd[:, :], start=True, stop=True)
                mm.then_inc(S["in_done"], 1)

            def row(p, q, n, which):
                if which == 0:
                    if n == 0:
                        pe.wait_ge(S["bc_parts"], p * 4 + 4)
                    if late(p) or n > 0:
                        pe.wait_ge(S["b_out"], p * NS + n)
                    pe.matmul(b_ps[:, 0:W], pick[:, n, :], bc[q][:, :], start=True, stop=True).then_inc(S["b_done"], 1)
                else:
                    if late(p) or n > 0:
                        pe.wait_ge(S["prod_done"], p * UNITS + n * DT)
                    pe.matmul(c_ps[:, 0:W], pick[:, NS + n, :], bc[q][:, :], start=True, stop=True).then_inc(S["c_done"], 1)

            def add_up(p, u):
                n, j = u // DT, u % DT
                if n == 0 and late(p):
                    pe.wait_ge(S["yd_done"], p * DT)
                pe.wait_ge(S["prod_done"], p * UNITS + u + 1)
                pe.matmul(y_ps[j][:, 0:W], ident[:, :], prod[u % 4][:, :], start=(n == 0), stop=(n == NS - 1))\
                    .then_inc(S["acc_done"], 1)

            def project(p, img):
                if img == 0:
                    pe.wait_ge(S["yg_done"], p * DT + DT)
                    pe.wait_ge(S["in_out"], (p + 2) * 11 - 11 if type(p) is not int else min((p + 2) * 11 - 11, pairs * 11))
                if late(p) or img > 0:
                    pe.wait_ge(S["mo_out"], p * 2 + img)
                for half in range(2):
                    lo = img * L + half * HALF
                    for j in range(DT):
                        mm = pe.matmul(ob[0:TT, half * D:(half + 1) * D], yg[:, j, lo:lo + TT], w_out[:, j, :],
                                       start=(j == 0), stop=(j == DT - 1))
                mm.then_inc(S["out_done"], 1)

            def body(k, q, last, now, nxt):
                for n in STATES:
                    if now:
                        if n == 0:
                            row(k, q, 0, 0)
                        if n + 1 < NS:
                            row(k, q, n + 1, 0)
                        row(k, q, n, 1)
                    if last and n in (1, 2):
                        project(k - 1, n - 1)
                    if nxt:
                        if n == 2 and last:
                            pe.wait_ge(S["mo_out"], k * 2)
                        for i in START_AT.get(n, ()):
                            start(k + 1, 1 - q, i)
                    if now:
                        for j in range(DT):
                            add_up(k, n * DT + j)

            run(pe, body)

        @block.scalar
        def _(act):
            act.wait_ge(S["weights"], 16 * len(loads))
            act.wait_ge(S["zeroed"], 1)
            nc.scalar.activation(a_exp[:, :, :], a_log[:, :, :], ACT.Exp).then_inc(S["a_ready"], 1)
            act.wait_ge(S["a_ready"], 1)
            nc.scalar.mul(a_neg[:, :, :], a_exp[:, :, :], -1.0).then_inc(S["a_ready"], 1)
            act.wait_ge(S["a_ready"], 2)

            def start(p, q, i):
                act.wait_ge(S["in_done"], p * 11 + i + 1)
                if i < 6:
                    if i == 0 and type(p) is not int or i == 0 and p >= 2:
                        act.wait_ge(S["yg_done"], p * DT - DT)
                    nc.scalar.copy(xz[q][:, i, :], ob[:, 0:W]).then_inc(S["in_out"], 1)
                elif i == 6:
                    nc.scalar.copy(xd[:, :], ob[:, 0:W]).then_inc(S["in_out"], 1)
                elif i == 7:
                    if late(p):
                        act.wait_ge(S["bc_rest"], p * 2)
                    nc.scalar.copy(bc_f[:, :], ob[0:96, 0:W]).then_inc(S["in_out"], 1)
                else:
                    j = i - 8
                    if j == 0 and late(p):
                        act.wait_ge(S["dt_act"], p * 3)
                        act.wait_ge(S["dt_ready"], p * 3)
                    nc.scalar.activation(relud[:, j, :], ob[:, 0:W], ACT.Relu, bias=b_dt[:, j:j + 1]).then_inc(S["dt_relu"], 1)
                    nc.scalar.activation(absd[:, j, :], ob[:, 0:W], ACT.Abs, bias=b_dt[:, j:j + 1]).then_inc(S["in_out"], 1)

            def silu(p, q):
                act.wait_ge(S["in_out"], p * 11 + 6)
                nc.scalar.activation(xz[q][:, :, :], xz[q][:, :, :], ACT.Silu).then_inc(S["silu"], 1)

            def bc_step(p, q, i):
                if i == 0:
                    act.wait_ge(S["in_out"], p * 11 + 8)
                    if late(p):
                        act.wait_ge(S["bc_parts"], p * 4)
                        act.wait_ge(S["bc_rest"], p * 2)
                    nc.scalar.copy(bc_hi[:, :], bc_f[:, :]).then_inc(S["bc_parts"], 1)
                elif i == 1:
                    act.wait_ge(S["bc_rest"], p * 2 + 1)
                    nc.scalar.copy(bc_mid[:, :], bc_r[:, :]).then_inc(S["bc_parts"], 1)
                else:
                    act.wait_ge(S["bc_rest"], p * 2 + 2)
                    nc.scalar.copy(bc[q][0:32, :], bc_hi[0:32, :]).then_inc(S["bc_parts"], 1)
                    nc.scalar.copy(bc[q][32:64, :], bc_mid[32:64, :]).then_inc(S["bc_parts"], 1)

            def softplus(p, i):
                if i == 0:
                    act.wait_ge(S["in_out"], p * 11 + 11)
                    nc.scalar.activation(expd[:, :, :], absd[:, :, :], ACT.Exp, scale=-1.0).then_inc(S["dt_act"], 1)
                elif i == 1:
                    act.wait_ge(S["dt_act"], p * 3 + 1)
                    nc.scalar.activation(onep[:, :, :], expd[:, :, :], ACT.Identity, bias=1.0).then_inc(S["dt_act"], 1)
                else:
                    act.wait_ge(S["dt_act"], p * 3 + 2)
                    nc.scalar.activation(logd[:, :, :], onep[:, :, :], ACT.Ln).then_inc(S["dt_act"], 1)

            def b_row_out(p, n):
                act.wait_ge(S["b_done"], p * NS + n + 1)
                if late(p) or n >= 2:
                    act.wait_ge(S["dbx_done"], p * UNITS + (n - 1) * DT)
                nc.scalar.copy(b_row[n % 2][:, :], b_ps[:, 0:W]).then_inc(S["b_out"], 1)

            def decay(p, q, u):
                n, j = u // DT, u % DT
                if u == 0:
                    act.wait_ge(S["dt_ready"], p * 3 + 3)
                if late(p) or u >= 2:
                    act.wait_ge(S["scan_done"], p * UNITS + u - 1)
                nc.scalar.activation(images(da_ps[u % 2][:, 0:W])[:, :, 1:L], images(dt[q][:, j, :])[:, :, 1:L], ACT.Exp,
                                     scale=a_neg[:, j, n:n + 1]).then_inc(S["exp_done"], 1)

            def body(k, q, last, now, nxt):
                for n in STATES:
                    if now:
                        if n == 0:
                            b_row_out(k, 0)
                        for j in range(DT):
                            decay(k, q, n * DT + j)
                            if j == 0 and n + 1 < NS:
                                b_row_out(k, n + 1)
                    if last and n in (1, 2):
                        p, img = k - 1, n - 1
                        act.wait_ge(S["out_done"], p * 2 + img + 1)
                        if img == 0 and late(p):
                            act.wait_ge(S["res"], p)
                        nc.scalar.copy(mo[:, 2 * img:2 * img + 2, :],
                                       ob[0:TT, 0:2 * D].rearrange("p (h c) -> p h c", h=2)).then_inc(S["mo_out"], 1)
                    if nxt:
                        for i in START_AT.get(n, ()):
                            start(k + 1, 1 - q, i)
                        if n == 5:
                            silu(k + 1, 1 - q)
                        if n in (7, 8, 9):
                            bc_step(k + 1, 1 - q, n - 7)
                        if n in (10, 11, 12):
                            softplus(k + 1, n - 10)

            run(act, body)

        @block.gpsimd
        def _(pool):
            nc.gpsimd.memset(minus_half[:], -0.5).then_inc(S["fence"], 1)
            pool.wait_ge(S["fence"], 1)
            pool.wait_ge(S["weights"], 16 * len(loads))

            def drive(p, q, u):
                n, j = u // DT, u % DT
                if u == 0:
                    pool.wait_ge(S["dtx_ready"], p + 1)
                if j == 0:
                    pool.wait_ge(S["b_out"], p * NS + n + 1)
                if late(p) or u >= 2 * DT:
                    pool.wait_ge(S["scan_done"], p * UNITS + u + 1 - 2 * DT)
                nc.gpsimd.tensor_tensor(dbx[u % (2 * DT)][:, :], dtx[q][:, j, :], b_row[n % 2][:, :], ALU.mult)\
                    .then_inc(S["dbx_done"], 1)

            def affine(p, i):
                if i == 0:
                    pool.wait_ge(S["norm"], p * 4 + 4)
                    nc.gpsimd.tensor_tensor(ha[:, :, :], hn[:, :, :], gamma[:, :].unsqueeze(1).broadcast_to([TT, 4, D]),
                                            ALU.mult).then_inc(S["affine"], 1)
                elif i == 1:
                    pool.wait_ge(S["affine"], p * 3 + 1)
                    nc.gpsimd.tensor_tensor(hb[:, :, :], ha[:, :, :], beta[:, :].unsqueeze(1).broadcast_to([TT, 4, D]),
                                            ALU.add).then_inc(S["affine"], 1)
                else:
                    pool.wait_ge(S["affine"], p * 3 + 2)
                    pool.wait_ge(S["h_loaded"], p * 16 + 16)
                    if late(p):
                        pool.wait_ge(S["stored"], p * 16)
                    nc.gpsimd.tensor_tensor(h2[:, :, :], hb[:, :, :], hin[:, :, :], ALU.add).then_inc(S["affine"], 1)

            def body(k, q, last, now, nxt):
                for n in STATES:
                    if now:
                        for j in range(DT):
                            drive(k, q, n * DT + j)
                    if last and n == 0:
                        p = k - 1
                        for j in range(DT):
                            pool.wait_ge(S["yd_done"], p * DT + j + 1)
                            if j == 0 and late(p):
                                pool.wait_ge(S["out_done"], p * 2)
                            nc.gpsimd.tensor_tensor(yg[:, j, :], yd[:, j, :], xz[1 - q][:, DT + j, :], ALU.mult)\
                                .then_inc(S["yg_done"], 1)
                    if last and n == 5:
                        pool.wait_ge(S["stats"], k * 9)
                        nc.gpsimd.tensor_tensor(rs[:, :], ve[:, :], minus_half[:, :], ALU.pow).then_inc(S["rs_ready"], 1)
                    if last and n in (9, 11, 13):
                        affine(k - 1, (n - 9) // 2)
                    if nxt:
                        p = k + 1
                        if n == 7:
                            pool.wait_ge(S["bc_parts"], p * 4 + 1)
                            nc.gpsimd.tensor_tensor(bc_r[:, :], bc_f[:, :], bc_hi[:, :], ALU.subtract).then_inc(S["bc_rest"], 1)
                        if n == 8:
                            pool.wait_ge(S["bc_parts"], p * 4 + 2)
                            if type(p) is not int or p >= 2:
                                pool.wait_ge(S["c_done"], p * NS - NS)
                            nc.gpsimd.tensor_tensor(bc[1 - q][:, :], bc_r[:, :], bc_mid[:, :], ALU.subtract)\
                                .then_inc(S["bc_rest"], 1)
                        if n == 14:
                            pool.wait_ge(S["dt_ready"], p * 3 + 3)
                            nc.gpsimd.tensor_tensor(dtx[1 - q][:, :, :], dt[1 - q][:, :, :], xz[1 - q][:, 0:DT, :],
                                                    ALU.mult).then_inc(S["dtx_ready"], 1)

            run(pool, body)

        @block.vector
        def _(dve):
            nc.vector.memset(da_ps[0][:, :], 0.0)
            nc.vector.memset(da_ps[1][:, :], 0.0).then_inc(S["zeroed"], 1)
            dve.wait_ge(S["weights"], 16 * len(loads))
            nc.vector.tensor_copy(pick[:, :, :], pick_f[:, :, :]).then_inc(S["picks"], 1)

            def scan(p, u):
                dve.wait_ge(S["exp_done"], p * UNITS + u + 1)
                dve.wait_ge(S["dbx_done"], p * UNITS + u + 1)
                if late(p) or u >= 3:
                    dve.wait_ge(S["prod_done"], p * UNITS + u - 2)
                nc.vector.tensor_tensor_scan(hid[u % 3][:, :], da_ps[u % 2][:, 0:W], dbx[u % (2 * DT)][:, :], 0.0,
                                             ALU.mult, ALU.add).then_inc(S["scan_done"], 1)

            def product(p, u):
                n, j = u // DT, u % DT
                dve.wait_ge(S["scan_done"], p * UNITS + u + 1)
                if j == 0:
                    dve.wait_ge(S["c_done"], p * NS + n + 1)
                if late(p) or u >= 4:
                    dve.wait_ge(S["acc_done"], p * UNITS + u - 3)
                nc.vector.tensor_tensor(prod[u % 4][:, :], hid[u % 3][:, :], c_ps[:, 0:W], ALU.mult)\
                    .then_inc(S["prod_done"], 1)

            def skip_path(p, q):
                for j in range(DT):
                    dve.wait_ge(S["acc_done"], p * UNITS + UNITS - DT + j + 1)
                    if j == 0 and late(p):
                        dve.wait_ge(S["yg_done"], p * DT)
                    nc.vector.scalar_tensor_tensor(out=yd[:, j, :], in0=xz[q][:, j, :], scalar=d_skip[:, j:j + 1],
                                                   in1=y_ps[j][:, 0:W], op0=ALU.mult, op1=ALU.add)\
                        .then_inc(S["yd_done"], 1)

            def end(p, n):
                if n == 3:
                    dve.wait_ge(S["mo_out"], p * 2 + 2)
                    dve.wait_ge(S["xn_loaded"], p * 16 + 16)
                    if late(p):
                        dve.wait_ge(S["norm"], p * 4)
                    nc.vector.tensor_tensor(hs[:, :, :], mo[:, :, :], xn[:, :, :], ALU.add).then_inc(S["res"], 1)
                    dve.wait_ge(S["res"], p + 1)
                    for i in range(4):
                        nc.vector.bn_stats(st[:, i, :], hs[:, i, :]).then_inc(S["stats"], 1)
                if n == 4:
                    for i in range(4):
                        dve.wait_ge(S["stats"], p * 9 + i + 1)
                        dve.sem_inc(S["fence"], 1)
                        nc.vector.bn_aggr(mv[:, i, :], st[:, i, :]).then_inc(S["stats"], 1)
                    dve.wait_ge(S["stats"], p * 9 + 8)
                    if late(p):
                        dve.wait_ge(S["rs_ready"], p)
                    nc.vector.tensor_scalar(ve[:, :], mv[:, :, 1], LN_EPS, None, ALU.add).then_inc(S["stats"], 1)
                if n == 7:
                    dve.wait_ge(S["rs_ready"], p + 1)
                    if late(p):
                        dve.wait_ge(S["affine"], p * 3)
                    for i in range(4):
                        nc.vector.tensor_scalar(hn[:, i, :], hs[:, i, :], mv[:, i, 0:1], rs[:, i:i + 1],
                                                ALU.subtract, ALU.mult).then_inc(S["norm"], 1)

            def softplus(p, q):
                dve.wait_ge(S["dt_act"], p * 3 + 3)
                dve.wait_ge(S["dt_relu"], p * 3 + 3)
                if late(p):
                    dve.wait_ge(S["dt_ready"], p * 3)
                nc.vector.scalar_tensor_tensor(out=lost[:, :, :], in0=onep[:, :, :], scalar=1.0, in1=expd[:, :, :],
                                               op0=ALU.subtract, op1=ALU.subtract).then_inc(S["dt_ready"], 1)
                nc.vector.tensor_tensor(sumd[:, :, :], relud[:, :, :], logd[:, :, :], ALU.add).then_inc(S["dt_ready"], 1)
                dve.wait_ge(S["dt_ready"], p * 3 + 2)
                if type(p) is not int or p >= 2:
                    dve.wait_ge(S["exp_done"], p * UNITS - UNITS)
                    dve.wait_ge(S["dtx_ready"], p - 1)
                nc.vector.tensor_tensor(dt[q][:, :, :], sumd[:, :, :], lost[:, :, :], ALU.subtract)\
                    .then_inc(S["dt_ready"], 1)

            def body(k, q, last, now, nxt):
                for n in STATES:
                    for j in range(DT):
                        u = n * DT + j
                        if now:
                            scan(k, u)
                        if last and u == 0:
                            skip_path(k - 1, 1 - q)
                        if now and u > 0:
                            product(k, u - 1)
                    if last and n in (3, 4, 7):
                        end(k - 1, n)
                    if nxt and n == 13:
                        softplus(k + 1, 1 - q)
                if now:
                    product(k, UNITS - 1)

            run(dve, body)


START_AT = {2: (0,), 3: (1, 2), 4: (3, 4), 5: (5,), 6: (6, 7), 8: (8,), 9: (9, 10)}


def mix_slots(nc, t_in, h_in, out, pairs):
    assert pairs % 2 == 0 and pairs >= 4
    W = 2 * L
    with ExitStack() as ctx:
        def sb(name, shape, dt=F32):
            return ctx.enter_context(nc.sbuf_tensor(name, shape, dt))

        def sem(name):
            return ctx.enter_context(nc.semaphore(name))

        def bank(name):
            return ctx.enter_context(nc.psum_tensor(name, [P, 512], F32))

        ident = sb("c_ident", [P, P])
        slot_raw = sb("c_slot_raw", [P, 2, SLOTS])
        slot_sq = sb("c_slot_sq", [P, 2, SLOTS])
        slot_sum = sb("c_slot_sum", [P, 2, NP_])
        slot_norm = sb("c_slot_norm", [P, 2, NP_])
        scale = sb("c_scale", [P, 1])
        slots = sb("c_slots", [P, 2, SLOTS])
        w_down = sb("c_w_down", [P, 2, 2, P])
        b_down = sb("c_b_down", [P, 2])
        w_up = sb("c_w_up", [P, 2, D])
        b_up = sb("c_b_up", [SLOTS, D])
        own = sb("c_own", [P, 2, SLOTS])
        minus_half = sb("c_minus_half", [TT, 4])
        plus_half = sb("c_plus_half", [P, 2, NP_])
        minus_one = sb("c_minus_one", [P, 2, NP_])

        h = [sb(f"c_h{q}", [TT, 4, D]) for q in range(2)]
        st = sb("c_st", [TT, 4, 6])
        mv = sb("c_mv", [TT, 4, 2])
        sm = [sb(f"c_sm{i}", [TT, 4]) for i in range(9)]
        xn = [sb(f"c_xn{q}", [TT, 4, D]) for q in range(2)]
        xt = [sb(f"c_xt{q}", [P, 2, W]) for q in range(2)]
        mx_d = sb("c_mx_d", [SLOTS, 2])
        e_d = sb("c_e_d", [SLOTS, 2, L])
        sum_d = sb("c_sum_d", [SLOTS, 2])
        inv_d = sb("c_inv_d", [SLOTS, 2])
        p_d = sb("c_p_d", [SLOTS, 2, L])
        mx_c = sb("c_mx_c", [TT, 4])
        l_c = sb("c_l_c", [TT, 4, SLOTS])
        e_c = sb("c_e_c", [TT, 4, SLOTS])
        sum_c = sb("c_sum_c", [TT, 4])
        inv_c = sb("c_inv_c", [TT, 4])
        p_c = sb("c_p_c", [TT, 4, SLOTS])
        dm = sb("c_dm", [TT, 4, SLOTS])
        ct = [sb(f"c_ct{q}", [SLOTS, 4, TT]) for q in range(2)]
        xs = sb("c_xs", [P, 2, 2 * SLOTS])
        hid = sb("c_hid", [P, 2, 2 * SLOTS])
        own_hid = sb("c_own_hid", [P, 2, 2 * SLOTS])
        ys = sb("c_ys", [SLOTS, 2, D])
        h_again = sb("c_h_again", [TT, 4, D])
        res = sb("c_res", [TT, 4, D])

        tr_ps = bank("c_tr_ps")
        lg_ps = bank("c_lg_ps")
        lt_ps = bank("c_lt_ps")
        xs_ps = bank("c_xs_ps")
        hid_ps = bank("c_hid_ps")
        ys_ps = bank("c_ys_ps")
        out_ps = [bank("c_out_ps0"), bank("c_out_ps1")]

        S = {n: sem("c_" + n) for n in (
            "fence", "weights", "consts", "slot_steps", "slots_ready",
            "h_loaded0", "h_loaded1", "h_again_loaded", "stats", "steps", "norm", "tr_done", "xt_out",
            "lg_done", "lt_done", "mx", "e_d", "d_steps", "c_steps", "e_c", "dm_done", "dm_out", "ct_done", "ct_out",
            "xs_done", "xs_out", "hid_done", "hid_out", "masked", "ys_done", "ys_out", "out_done", "summed", "stored")}
        loads = [(ident, "ident"), (slot_raw, "slots"), (scale, "scale"), (w_down, "w_down"), (b_down, "b_down"),
                 (w_up, "w_up"), (b_up, "b_up"), (own, "own")]

        def run(eng, body):
            body(0, 0, 0, True, False, False)
            body(1, 0, 1, True, True, False)
            with eng.Fori(1, pairs // 2) as m:
                body(m * 2, m, 0, True, True, True)
                body(m * 2 + 1, m, 1, True, True, True)
            body(pairs, pairs // 2, 0, False, True, True)
            body(pairs + 1, pairs // 2, 1, False, False, True)

        def late(p, n=1):
            return not (type(p) is int and p < n)

        block = ctx.enter_context(nc.Block())

        @block.sync
        def _(sp):
            for dst, name in loads:
                sp.dma_start(dst[:], t_in[name]).then_inc(S["weights"], 16)

            def body(k, m, q, first, second, third):
                if first:
                    if late(k, 2):
                        sp.wait_ge(S["norm"], k * 4 - 4)
                    sp.dma_start(h[q][:], h_in[k]).then_inc(S[f"h_loaded{q}"], 16)
                if third:
                    p = k - 2
                    if late(p):
                        sp.wait_ge(S["summed"], p * 2)
                    sp.dma_start(h_again[:], h_in[p]).then_inc(S["h_again_loaded"], 16)
                    sp.wait_ge(S["summed"], p * 2 + 2)
                    sp.dma_start(out[p], res[:]).then_inc(S["stored"], 16)

            run(sp, body)
            sp.wait_ge(S["stored"], 16 * pairs)

        @block.tensor
        def _(pe):
            pe.wait_ge(S["weights"], 16 * len(loads))
            pe.wait_ge(S["slots_ready"], 2)

            def body(k, m, q, first, second, third):
                if second:
                    p, r = k - 1, 1 - q
                    pe.wait_ge(S["xt_out"], p * 2 + 2)
                    if late(p):
                        pe.wait_ge(S["ct_out"], p)
                        pe.wait_ge(S["dm_out"], p * 2)
                    for i in range(4):
                        lo = (i // 2) * L + (i % 2) * HALF
                        for part in range(2):
                            mm = pe.matmul(lg_ps[0:TT, i * SLOTS:(i + 1) * SLOTS], xt[r][:, part, lo:lo + TT],
                                           slots[:, part, :], start=(part == 0), stop=(part == 1))
                    mm.then_inc(S["lg_done"], 1)
                    for part in range(2):
                        mm = pe.matmul(lt_ps[0:SLOTS, 0:W], slots[:, part, :], xt[r][:, part, :],
                                       start=(part == 0), stop=(part == 1))
                    mm.then_inc(S["lt_done"], 1)
                if third:
                    p = k - 2
                    pe.wait_ge(S["xs_out"], p + 1)
                    if late(p):
                        pe.wait_ge(S["hid_out"], p * 2)
                    for t in range(2):
                        for part in range(2):
                            mm = pe.matmul(hid_ps[:, t * 2 * SLOTS:(t + 1) * 2 * SLOTS], w_down[:, part, t, :],
                                           xs[:, part, :], start=(part == 0), stop=(part == 1))
                    mm.then_inc(S["hid_done"], 1)
                if second:
                    p, r = k - 1, 1 - q
                    pe.wait_ge(S["d_steps"], p * 4 + 4)
                    pe.sem_inc(S["fence"], 1)
                    for i in range(4):
                        rows, lo = (HALF, 0) if i % 2 == 0 else (TT, HALF)
                        mm = pe.transpose(lt_ps[0:rows, i * SLOTS:(i + 1) * SLOTS], p_d[:, i // 2, lo:lo + rows],
                                          ident[0:SLOTS, 0:SLOTS])
                    mm.then_inc(S["dm_done"], 1)
                    pe.wait_ge(S["c_steps"], p * 4 + 4)
                    for i in range(4):
                        mm = pe.transpose(lg_ps[0:SLOTS, i * TT:(i + 1) * TT], p_c[:, i, :], ident[0:TT, 0:TT])
                    mm.then_inc(S["ct_done"], 1)
                if third:
                    p = k - 2
                    pe.wait_ge(S["masked"], p + 1)
                    if late(p):
                        pe.wait_ge(S["ys_out"], p)
                    for img in range(2):
                        for t in range(2):
                            mm = pe.matmul(ys_ps[0:SLOTS, img * D:(img + 1) * D],
                                           own_hid[:, t, img * SLOTS:(img + 1) * SLOTS], w_up[:, t, :],
                                           start=(t == 0), stop=(t == 1))
                    mm.then_inc(S["ys_done"], 1)
                if first:
                    pe.wait_ge(S["norm"], k * 4 + 4)
                    for part in range(2):
                        if late(k) or part == 1:
                            pe.wait_ge(S["xt_out"], k * 2 + part)
                        for i in range(4):
                            lo = (i // 2) * L + (i % 2) * HALF
                            mm = pe.transpose(tr_ps[:, lo:lo + TT], xn[q][:, i, part * HI:part * HI + P], ident[0:TT, 0:TT])
                        mm.then_inc(S["tr_done"], 1)
                if second:
                    p, r = k - 1, 1 - q
                    pe.wait_ge(S["dm_out"], p * 2 + 2)
                    if late(p):
                        pe.wait_ge(S["xs_out"], p)
                    for part in range(2):
                        for img in range(2):
                            o = xs_ps[:, (part * 2 + img) * SLOTS:(part * 2 + img + 1) * SLOTS]
                            for half, rows in ((0, HALF), (1, TT)):
                                mm = pe.matmul(o, xn[r][0:rows, 2 * img + half, part * HI:part * HI + P],
                                               dm[0:rows, 2 * img + half, :], start=(half == 0), stop=(half == 1))
                    mm.then_inc(S["xs_done"], 1)
                if third:
                    p = k - 2
                    pe.wait_ge(S["ys_out"], p + 1)
                    if late(p):
                        pe.wait_ge(S["summed"], p * 2)
                    for img in range(2):
                        for half in range(2):
                            mm = pe.matmul(out_ps[img][0:TT, half * D:(half + 1) * D], ct[q][:, 2 * img + half, :],
                                           ys[:, img, :], start=True, stop=True)
                        mm.then_inc(S["out_done"], 1)

            run(pe, body)

        @block.scalar
        def _(act):
            act.wait_ge(S["weights"], 16 * len(loads))
            nc.scalar.activation(slot_sq[:, :, :], slot_raw[:, :, :], ACT.Square).then_inc(S["slot_steps"], 1)

            def body(k, m, q, first, second, third):
                if second:
                    p, r = k - 1, 1 - q
                    act.wait_ge(S["mx"], p * 2 + 1)
                    if late(p):
                        act.wait_ge(S["d_steps"], p * 4)
                    for img in range(2):
                        nc.scalar.activation(e_d[:, img, :], lt_ps[0:SLOTS, img * L:(img + 1) * L], ACT.Exp,
                                             bias=mx_d[:, img:img + 1]).then_inc(S["e_d"], 1)
                    act.wait_ge(S["c_steps"], p * 4 + 1)
                    nc.scalar.activation(e_c[:, :, :], l_c[:, :, :], ACT.Exp).then_inc(S["e_c"], 1)
                if third:
                    p = k - 2
                    act.wait_ge(S["hid_done"], p + 1)
                    if late(p):
                        act.wait_ge(S["masked"], p)
                    for t in range(2):
                        nc.scalar.activation(hid[:, t, :], hid_ps[:, t * 2 * SLOTS:(t + 1) * 2 * SLOTS], ACT.Gelu,
                                             bias=b_down[:, t:t + 1]).then_inc(S["hid_out"], 1)
                if second:
                    p, r = k - 1, 1 - q
                    act.wait_ge(S["dm_done"], p + 1)
                    if late(p):
                        act.wait_ge(S["xs_done"], p)
                    for half, rows in ((0, HALF), (1, TT)):
                        nc.scalar.copy(dm[0:rows, half::2, :], lt_ps[0:rows, 0:4 * SLOTS].rearrange(
                            "p (i s) -> p i s", i=4)[:, half::2, :]).then_inc(S["dm_out"], 1)
                    act.wait_ge(S["ct_done"], p + 1)
                    if late(p, 2):
                        act.wait_ge(S["out_done"], p * 2 - 2)
                    nc.scalar.copy(ct[r][:, :, :], lg_ps[0:SLOTS, 0:4 * TT].rearrange("p (i t) -> p i t", i=4))\
                        .then_inc(S["ct_out"], 1)
                if first:
                    for part in range(2):
                        act.wait_ge(S["tr_done"], k * 2 + part + 1)
                        if part == 0 and late(k, 2):
                            act.wait_ge(S["lt_done"], k - 1)
                        nc.scalar.copy(xt[q][:, part, :], tr_ps[:, 0:W]).then_inc(S["xt_out"], 1)
                if second:
                    p = k - 1
                    act.wait_ge(S["xs_done"], p + 1)
                    if late(p):
                        act.wait_ge(S["hid_done"], p)
                    nc.scalar.copy(xs[:, :, :], xs_ps[:, 0:4 * SLOTS].rearrange("p (a s) -> p a s", a=2))\
                        .then_inc(S["xs_out"], 1)

            run(act, body)

        @block.gpsimd
        def _(pool):
            nc.gpsimd.memset(minus_half[:], -0.5).then_inc(S["consts"], 1)
            nc.gpsimd.memset(plus_half[:], 0.5).then_inc(S["consts"], 1)
            nc.gpsimd.memset(minus_one[:], -1.0).then_inc(S["consts"], 1)
            pool.wait_ge(S["consts"], 3)
            pool.wait_ge(S["slot_steps"], 2)
            nc.gpsimd.tensor_tensor(slot_norm[:, :, :], slot_sum[:, :, :], plus_half[:, :, :], ALU.pow).then_inc(S["slot_steps"], 1)
            pool.wait_ge(S["slot_steps"], 3)
            nc.gpsimd.tensor_scalar(slot_sum[:, :, :], slot_norm[:, :, :], L2_EPS, None, ALU.add).then_inc(S["slot_steps"], 1)
            pool.wait_ge(S["slot_steps"], 4)
            nc.gpsimd.tensor_tensor(slot_norm[:, :, :], slot_sum[:, :, :], minus_one[:, :, :], ALU.pow).then_inc(S["slot_steps"], 1)

            def body(k, m, q, first, second, third):
                if first:
                    v = [x[:, :] for x in sm]
                    pool.wait_ge(S["stats"], k * 10 + 10)
                    if late(k):
                        pool.wait_ge(S["norm"], k * 4)
                    nc.gpsimd.tensor_tensor(v[2], v[0], minus_half[:, :], ALU.pow).then_inc(S["steps"], 1)
                    pool.wait_ge(S["steps"], k * 7 + 1)
                    nc.gpsimd.tensor_tensor(v[3], v[2], v[2], ALU.mult).then_inc(S["steps"], 1)
                    pool.wait_ge(S["steps"], k * 7 + 2)
                    nc.gpsimd.tensor_tensor(v[4], v[3], v[1], ALU.mult).then_inc(S["steps"], 1)
                    pool.wait_ge(S["steps"], k * 7 + 3)
                    nc.gpsimd.tensor_tensor(v[5], v[4], plus_half[0:TT, 0, :], ALU.pow).then_inc(S["steps"], 1)
                    pool.wait_ge(S["steps"], k * 7 + 4)
                    pool.sem_inc(S["fence"], 1)
                    nc.gpsimd.tensor_scalar(v[6], v[5], L2_EPS, None, ALU.add).then_inc(S["steps"], 1)
                    pool.wait_ge(S["steps"], k * 7 + 5)
                    nc.gpsimd.tensor_tensor(v[7], v[6], minus_one[0:TT, 0, :], ALU.pow).then_inc(S["steps"], 1)
                    pool.wait_ge(S["steps"], k * 7 + 6)
                    nc.gpsimd.tensor_tensor(v[8], v[7], v[2], ALU.mult).then_inc(S["steps"], 1)
                if third:
                    p = k - 2
                    pool.wait_ge(S["hid_out"], p * 2 + 2)
                    if late(p):
                        pool.wait_ge(S["ys_done"], p)
                    nc.gpsimd.tensor_tensor(own_hid[:, :, :].rearrange("p m (i s) -> p m i s", i=2),
                                            hid[:, :, :].rearrange("p m (i s) -> p m i s", i=2),
                                            own[:, :, :].unsqueeze(2).broadcast_to([P, 2, 2, SLOTS]), ALU.mult)\
                        .then_inc(S["masked"], 1)

            run(pool, body)

        @block.vector
        def _(dve):
            dve.wait_ge(S["weights"], 16 * len(loads))
            dve.wait_ge(S["slot_steps"], 1)
            nc.vector.tensor_reduce(slot_sum[:, :, :], slot_sq[:, :, :].rearrange("p a (n s) -> p a s n", s=NP_), AX_X,
                                    ALU.add).then_inc(S["slot_steps"], 1)
            dve.wait_ge(S["slot_steps"], 5)
            for part in range(2):
                nc.vector.scalar_tensor_tensor(out=slots[:, part, :].rearrange("p (n s) -> p n s", s=NP_),
                                               in0=slot_raw[:, part, :].rearrange("p (n s) -> p n s", s=NP_),
                                               scalar=scale[:, 0:1],
                                               in1=slot_norm[:, part, :].unsqueeze(1).broadcast_to([P, NE, NP_]),
                                               op0=ALU.mult, op1=ALU.mult).then_inc(S["slots_ready"], 1)

            def body(k, m, q, first, second, third):
                if first:
                    dve.wait_ge(S[f"h_loaded{q}"], m * 16 + 16)
                    if late(k):
                        dve.wait_ge(S["norm"], k * 4)
                        dve.wait_ge(S["steps"], k * 7)
                    for i in range(4):
                        nc.vector.bn_stats(st[:, i, :], h[q][:, i, :]).then_inc(S["stats"], 1)
                if second:
                    p = k - 1
                    dve.wait_ge(S["lt_done"], p + 1)
                    if late(p):
                        dve.wait_ge(S["e_d"], p * 2)
                    nc.vector.tensor_reduce(mx_d[:, :], lt_ps[0:SLOTS, 0:W].rearrange("p (i l) -> p i l", i=2), AX_X,
                                            ALU.max, negate=True).then_inc(S["mx"], 1)
                    if late(p):
                        dve.wait_ge(S["c_steps"], p * 4)
                    lg = lg_ps[0:TT, 0:4 * SLOTS].rearrange("p (i s) -> p i s", i=4)
                    nc.vector.tensor_reduce(mx_c[:, :], lg, AX_X, ALU.max).then_inc(S["mx"], 1)
                    dve.wait_ge(S["mx"], p * 2 + 2)
                    if late(p):
                        dve.wait_ge(S["e_c"], p)
                    nc.vector.tensor_tensor(l_c[:, :, :], lg, mx_c[:, :].unsqueeze(2).broadcast_to([TT, 4, SLOTS]),
                                            ALU.subtract).then_inc(S["c_steps"], 1)
                if first:
                    for i in range(4):
                        dve.wait_ge(S["stats"], k * 10 + i + 1)
                        dve.sem_inc(S["fence"], 1)
                        nc.vector.bn_aggr(mv[:, i, :], st[:, i, :]).then_inc(S["stats"], 1)
                    dve.wait_ge(S["stats"], k * 10 + 8)
                    nc.vector.tensor_scalar(sm[0][:, :], mv[:, :, 1], LN_EPS, None, ALU.add).then_inc(S["stats"], 1)
                    nc.vector.tensor_scalar(sm[1][:, :], mv[:, :, 1], float(D), None, ALU.mult).then_inc(S["stats"], 1)
                if second:
                    p = k - 1
                    dve.wait_ge(S["e_d"], p * 2 + 2)
                    nc.vector.tensor_reduce(sum_d[:, :], e_d[:, :, :], AX_X, ALU.add).then_inc(S["d_steps"], 1)
                    dve.wait_ge(S["d_steps"], p * 4 + 1)
                    nc.vector.reciprocal(inv_d[:, :], sum_d[:, :]).then_inc(S["d_steps"], 1)
                    dve.wait_ge(S["d_steps"], p * 4 + 2)
                    if late(p):
                        dve.wait_ge(S["dm_done"], p)
                    for img in range(2):
                        nc.vector.tensor_scalar(p_d[:, img, :], e_d[:, img, :], inv_d[:, img:img + 1], None,
                                                ALU.mult).then_inc(S["d_steps"], 1)
                    dve.wait_ge(S["e_c"], p + 1)
                    nc.vector.tensor_reduce(sum_c[:, :], e_c[:, :, :], AX_X, ALU.add).then_inc(S["c_steps"], 1)
                    dve.wait_ge(S["c_steps"], p * 4 + 2)
                    nc.vector.reciprocal(inv_c[:, :], sum_c[:, :]).then_inc(S["c_steps"], 1)
                    dve.wait_ge(S["c_steps"], p * 4 + 3)
                    if late(p):
                        dve.wait_ge(S["ct_done"], p)
                    nc.vector.tensor_tensor(p_c[:, :, :], e_c[:, :, :], inv_c[:, :].unsqueeze(2).broadcast_to([TT, 4, SLOTS]),
                                            ALU.mult).then_inc(S["c_steps"], 1)
                if first:
                    dve.wait_ge(S["steps"], k * 7 + 7)
                    if late(k, 2):
                        dve.wait_ge(S["xs_done"], k - 1)
                        dve.wait_ge(S["tr_done"], k * 2 - 2)
                    for i in range(4):
                        nc.vector.tensor_scalar(xn[q][:, i, :], h[q][:, i, :], mv[:, i, 0:1], sm[8][:, i:i + 1],
                                                ALU.subtract, ALU.mult).then_inc(S["norm"], 1)
                if third:
                    p = k - 2
                    dve.wait_ge(S["ys_done"], p + 1)
                    if late(p):
                        dve.wait_ge(S["out_done"], p * 2)
                    nc.vector.tensor_tensor(ys[:, :, :], ys_ps[0:SLOTS, 0:2 * D].rearrange("p (i d) -> p i d", i=2),
                                            b_up[:, :].unsqueeze(1).broadcast_to([SLOTS, 2, D]), ALU.add)\
                        .then_inc(S["ys_out"], 1)
                    dve.wait_ge(S["h_again_loaded"], p * 16 + 16)
                    if late(p):
                        dve.wait_ge(S["stored"], p * 16)
                    for img in range(2):
                        dve.wait_ge(S["out_done"], p * 2 + img + 1)
                        nc.vector.tensor_tensor(res[:, 2 * img:2 * img + 2, :],
                                                out_ps[img][0:TT, 0:2 * D].rearrange("p (i d) -> p i d", i=2),
                                                h_again[:, 2 * img:2 * img + 2, :], ALU.add).then_inc(S["summed"], 1)

            run(dve, body)


def pointwise_tiles(w, mode):
    wt = np.ascontiguousarray(w.reshape(D, D).T)
    o = np.zeros((P, 6, P), wt.dtype)
    if mode == "one":
        o[:, 0] = wt[:P, :P]
        for i in range(2):
            o[HI * i:HI * i + HI, 1 + i] = wt[P:, :P]
            o[:, 3 + i, HI * i:HI * i + HI] = wt[:P, P:]
            o[HI * i:HI * i + HI, 5, HI * i:HI * i + HI] = wt[P:, P:]
    else:
        r = 0 if mode == "loc" else HI
        o[:, 0] = wt[:P, :P]
        o[r:r + HI, 1] = wt[P:, :P]
        for i in range(2):
            o[:, 2 + 2 * i, HI * i:HI * i + HI] = wt[:P, P:]
            o[r:r + HI, 3 + 2 * i, HI * i:HI * i + HI] = wt[P:, P:]
    return o


def low_high(v):
    return np.stack([v[:P], np.concatenate([v[P:], v[P:]])], 1)


def haar_bands():
    bands = np.zeros((256, 256), np.float32)
    for b in range(256):
        for i in range(16):
            for j in range(16):
                odd = 0
                for level in range(4):
                    digit = (b >> (2 * (3 - level))) & 3
                    odd ^= (digit >> 1) & (j >> level) & 1
                    odd ^= digit & (i >> level) & 1
                bands[b, i * 16 + j] = -0.0625 if odd else 0.0625
    return bands


def host_inputs(i, pairs):
    f = {}
    x = i["x"][:2 * pairs].reshape(pairs, 2, 3, G, 16, G, 16)
    x = x.transpose(0, 2, 4, 6, 1, 3, 5).reshape(pairs, KT, P, 2 * PX)
    f["x_t"] = x.transpose(0, 2, 1, 3)
    t = {k[7:]: v for k, v in i.items() if k.startswith("L0_tok_")}
    f["ident"] = np.eye(P, dtype=np.float32)
    f["haar"] = haar_bands().reshape(2, P, 256).transpose(1, 0, 2)
    f["w_wave"] = t["pg_w1"].reshape(D, 2, P, 3).transpose(2, 1, 3, 0)
    f["w_loc"] = t["pl_w"].reshape(D, KT, P).transpose(2, 1, 0)
    f["conv_bias"] = np.stack([t["pl_b"][:P], t["pg_b1"][:P], np.concatenate([t["pl_b"][P:], t["pg_b1"][P:]])], 1)
    dw = [t[n].reshape(D, TAPS) for n in ("pl_dw", "pg_dw", "f1_dw", "f2_dw", "f3_dw")]
    tiles = [dw[0][:P], dw[1][:P], np.concatenate([dw[0][P:], dw[1][P:]])]
    for w in dw[2:]:
        tiles += [w[:P], np.concatenate([w[P:], w[P:]])]
    f["dw_w"] = np.stack(tiles, 1)
    f["pw_loc"] = pointwise_tiles(t["pl_pw"], "loc")
    f["pw_glob"] = pointwise_tiles(t["pg_pw"], "glob")
    f["pw_glob2"] = pointwise_tiles(t["pg_w2"], "one")
    f["pw_fuse1"] = pointwise_tiles(t["f1_pw"], "one")
    f["pw_fuse2"] = pointwise_tiles(t["f2_pw"], "one")
    biases = np.stack([t[n] for n in ("pl_pwb", "pg_pwb", "pg_b2", "f1_pwb", "f2_pwb")], 1)
    f["pw_bias"] = low_high(biases).transpose(0, 2, 1)
    w3 = t["f3_pw"].reshape(D, D).T
    f["pw3"] = np.zeros((P, 3, D), np.float32)
    f["pw3"][:, 0] = w3[:P]
    for n in range(2):
        f["pw3"][HI * n:HI * n + HI, 1 + n] = w3[P:]
    f["bias3"] = np.zeros((P, D), np.float32)
    f["bias3"][0] = t["f3_pwb"]
    f["row0"] = np.zeros((P, TT), np.float32)
    f["row0"][0] = 1.0
    f["alpha"] = low_high(t["alpha"].reshape(D, 1))[:, :, 0]
    f["ln_g"] = np.broadcast_to(t["ln_g"], (TT, D))
    f["ln_b"] = np.broadcast_to(t["ln_b"], (TT, D))
    f["cls"] = t["cls"].reshape(1, D)
    a = {k[8:]: v for k, v in i.items() if k.startswith("L0_attn_")}

    def high_part(w):
        o = w[HI:].copy()
        o[:HI] = 0.0
        return o

    f["w_in"] = np.stack([a["W_in"][:P], high_part(a["W_in"])], 1).reshape(P, 2, 2 * DT, P)
    wx = a["W_x"].reshape(DT, P, RANK + 2 * NS).transpose(1, 0, 2)
    f["w_x"] = np.zeros((P, DT, P), np.float32)
    f["w_x"][:, :, :RANK] = wx[:, :, :RANK]
    f["w_bc"] = np.concatenate([wx[:, :, RANK:]] * 3, 2)
    f["w_dt"] = np.zeros((P, DT, P), np.float32)
    f["w_dt"][:RANK] = a["W_dt"].reshape(RANK, DT, P)
    f["b_dt"] = a["b_dt"].reshape(DT, P).T
    f["a_log"] = a["A_log"].reshape(DT, P, NS).transpose(1, 0, 2)
    f["d_skip"] = a["D_skip"].reshape(DT, P).T
    f["w_out"] = a["W_out"].reshape(DT, P, D).transpose(1, 0, 2)
    f["gamma"] = np.broadcast_to(a["gamma"], (TT, D))
    f["beta"] = np.broadcast_to(a["beta"], (TT, D))
    pick = np.zeros((96, 2 * NS, P), np.float32)
    for row in range(96):
        pick[row, row % (2 * NS)] = 1.0
    f["pick"] = pick
    s = {k[7:]: v for k, v in i.items() if k.startswith("L0_ffn_")}
    raw = s["slot_params"].reshape(D, SLOTS)
    f["slots"] = np.stack([raw[:P], high_part(raw)], 1)
    f["scale"] = np.broadcast_to(s["scale"].reshape(1, 1), (P, 1))
    down = s["W_down"].transpose(1, 0, 2).reshape(D, D)
    down = np.stack([down[:, :P], down[:, HI:]], 1).reshape(D, 2 * P)
    f["w_down"] = np.stack([down[:P], high_part(down)], 1).reshape(P, 2, 2, P)
    b = s["b_down"].reshape(D)
    f["b_down"] = np.stack([b[:P], b[HI:]], 1)
    up = s["W_up"].reshape(D, D)
    f["w_up"] = np.stack([up[:P], high_part(up)], 1)
    f["b_up"] = np.repeat(s["b_up"], NP_, 0)
    own = np.zeros((D, SLOTS), np.float32)
    for e in range(NE):
        own[e * HID:(e + 1) * HID, e * NP_:(e + 1) * NP_] = 1.0
    f["own"] = np.stack([own[:P], own[HI:]], 1)
    return {name: np.ascontiguousarray(v) for name, v in f.items()}


def kernel(**inputs):
    import concourse.bacc as bacc
    from concourse.bass_utils import run_bass_kernel_spmd

    given = {name: np.asarray(v) for name, v in inputs.items()}
    images = given["x"].shape[0]
    pairs = images // 2
    arrays = host_inputs(given, pairs)
    nc = bacc.Bacc("TRN2", target_bir_lowering=False, num_devices=1)
    t_in = {name: nc.dram_tensor("in_" + name, v.shape, mybir.dt.from_np(v.dtype), kind="ExternalInput").ap()
            for name, v in arrays.items()}
    out = nc.dram_tensor("out_tokens", (pairs, TT, 4, D), F32, kind="ExternalOutput").ap()
    bass_vit_tower(nc, t_in, out, pairs)
    got = run_bass_kernel_spmd(nc, [{"in_" + name: v for name, v in arrays.items()}], core_ids=[0])
    tiles = np.asarray(got.results[0]["out_tokens"]).reshape(pairs, TT, 2, 2, D).transpose(0, 2, 3, 1, 4)
    return np.concatenate([tiles[:, :, 0, :HALF], tiles[:, :, 1]], 2).reshape(images, L, D)
```

```python
from contextlib import ExitStack

import numpy as np
import concourse.bass as bass
from concourse import mybir
from concourse.alu_op_type import AluOpType as ALU

F32 = mybir.dt.float32
BF16 = mybir.dt.bfloat16
ACT = mybir.ActivationFunctionType
AX_X = mybir.AxisListType.X

P = 128
D = 192
HI = D - P
G = 14
PX = G * G
L = PX + 1
TT = 99
HALF = L - TT
KT = 6
PAD = 16
ROWS2 = 2 * (G + 1) + 1
SPAN2 = (2 * G + 1) * G
IMG2 = (G + 1) * G
TAPS = 9
LN_EPS = 1e-5
L2_EPS = 1e-6
DI = 384
DT = DI // P
NS = 16
RANK = 48
NE, NP_, HID = 8, 4, 24
SLOTS = NE * NP_


def bass_vit_tower(nc, t_in, out, pairs, pe_taps=2):
    scratch_h = nc.dram_tensor("scratch_h", [pairs, TT, 4, D], F32, kind="Internal").ap()
    scratch_x = nc.dram_tensor("scratch_x", [pairs, TT, 4, D], F32, kind="Internal").ap()
    scratch_xt = nc.dram_tensor("scratch_xt", [pairs, P, 2, 2 * L], F32, kind="Internal").ap()
    scratch_h2 = nc.dram_tensor("scratch_h2", [pairs, TT, 4, D], F32, kind="Internal").ap()
    embed_images(nc, t_in, scratch_h, scratch_x, scratch_xt, pairs, pe_taps)
    mix_tokens(nc, t_in, scratch_h, scratch_x, scratch_xt, scratch_h2, pairs)
    mix_slots(nc, t_in, scratch_h2, out, pairs)




def embed_images(nc, t_in, h_out, x_out, xt_out, pairs, pe_taps):
    with ExitStack() as ctx:
        def sb(name, shape, dt=F32):
            return ctx.enter_context(nc.sbuf_tensor(name, shape, dt))

        def sem(name):
            return ctx.enter_context(nc.semaphore(name))

        def bank(name):
            return ctx.enter_context(nc.psum_tensor(name, [P, 512], F32))

        ident = sb("a_ident", [P, P])
        haar = sb("a_haar", [P, 2, 256])
        w_wave = sb("a_w_wave", [P, 2, 3, D])
        w_loc = sb("a_w_loc", [P, KT, D])
        w_conv = sb("a_w_conv", [P, KT, 3, P])
        conv_bias = sb("a_conv_bias", [P, 3])
        dw_w = sb("a_dw_w", [P, 9, TAPS])
        dw_diag = sb("a_dw_diag", [P, 9, pe_taps, P])
        pw = {n: sb(f"a_pw_{n}", [P, 6, P]) for n in ("loc", "glob")}
        pw |= {n: sb(f"a_pw_{n}", [P, 6, P]) for n in ("glob2", "fuse1", "fuse2")}
        pw_bias = sb("a_pw_bias", [P, 5, 2])
        pw3 = sb("a_pw3", [P, 3, D])
        bias3 = sb("a_bias3", [P, D])
        row0 = sb("a_row0", [P, TT])
        alpha = sb("a_alpha", [P, 2])
        gate = sb("a_gate", [P, 2])
        one_minus = sb("a_one_minus", [P, 2])
        gate_b = sb("a_gate_b", [P, 2])
        ln_g = sb("a_ln_g", [TT, D])
        ln_b = sb("a_ln_b", [TT, D])
        cls = sb("a_cls", [1, D])
        minus_half = sb("a_minus_half", [TT, 4])
        x_t = sb("a_x_t", [P, KT, 2 * PX])
        pad_first = [sb(f"a_pad_first{t}", [P, ROWS2, PAD]) for t in range(3)]
        acc_first = [sb(f"a_acc_first{t}", [P, 2 * IMG2]) for t in range(3)]
        loc = [sb("a_loc_low", [P, 2 * PX]), sb("a_loc_high", [P, PX])]
        loc_old = [sb("a_loc_old_low", [P, 2 * PX]), sb("a_loc_old_high", [P, PX])]
        gg = [sb("a_gg_low", [P, 2 * PX]), sb("a_gg_high", [P, PX])]
        loc_part = [sb("a_loc_part_low", [P, 2 * PX]), sb("a_loc_part_high", [P, PX])]
        pad = {k: [sb(f"a_pad{k}_low", [P, ROWS2, PAD]), sb(f"a_pad{k}_high", [P, PAD, PAD])] for k in (1, 2, 3)}
        acc = {k: [sb(f"a_acc{k}_low", [P, 2 * IMG2]), sb(f"a_acc{k}_high", [P, PX])] for k in (1, 2)}
        acc[3] = [sb("a_acc3_low", [P, 1 + 2 * IMG2]), sb("a_acc3_high", [P, 1 + PX])]
        relu2 = [sb("a_relu2_low", [P, 2 * PX]), sb("a_relu2_high", [P, PX])]
        tok = sb("a_tok", [TT, 4, D])
        st1 = sb("a_st1", [TT, 4, 6])
        mv1 = sb("a_mv1", [TT, 4, 2])
        ve1 = sb("a_ve1", [TT, 4])
        rs1 = sb("a_rs1", [TT, 4])
        hn = sb("a_hn", [TT, 4, D])
        hg = sb("a_hg", [TT, 4, D])
        h = sb("a_h", [TT, 4, D])
        st2 = sb("a_st2", [TT, 4, 6])
        mv2 = sb("a_mv2", [TT, 4, 2])
        ve2 = sb("a_ve2", [TT, 4])
        rs2 = sb("a_rs2", [TT, 4])
        xn = sb("a_xn", [TT, 4, D])
        xt = sb("a_xt", [P, 2, 2 * L])

        conv_ps = [bank("a_conv_ps0"), bank("a_conv_ps1")]
        tap_ps = [bank("a_tap_ps0"), bank("a_tap_ps1")]
        pw_ps = [bank("a_pw_ps_low"), bank("a_pw_ps_high")]
        tok_ps = bank("a_tok_ps")
        tr_ps = bank("a_tr_ps")

        S = {n: sem("a_" + n) for n in (
            "fence",
            "weights", "zeroed", "setup", "fold_done", "fold_copied", "diag", "gate_ready", "gate_act",
            "x_loaded", "conv_done", "gelu_done",
            "taps_first", "first_chain", "first_dw",
            "taps1", "chain1", "dw1", "taps2", "chain2", "dw2",
            "taps3", "chain3", "dw3",
            "pw_loc", "loc_out", "pw_glob", "gg_out", "pw_glob2", "part_out", "fused",
            "pw1", "relu1", "pw2", "relu2", "loc_kept", "joined",
            "tok_done", "tok_copied", "ln1_stats", "ln1_rs", "ln1_norm", "ln1_affine",
            "ln2_stats", "ln2_rs", "ln2_norm", "tr_done", "tr_copied", "h_stored", "x_stored", "xt_stored")}

        def maps(t):
            flat = t[:].rearrange("p r c -> p (r c)")
            return flat[:, 0:2 * (G + 1) * PAD].rearrange("p (i r c) -> p i r c", i=2, r=G + 1)[:, :, 1:G + 1, 1:G + 1]

        def shifted(t, tap, rows):
            dy, dx = tap // 3, tap % 3
            return t[:, dy:dy + rows, dx:dx + G]

        def grid(t, rows, lo=0):
            return t[:, lo:lo + rows * G].rearrange("p (r c) -> p r c", c=G)

        def as_maps(t):
            return t.rearrange("p (i r c) -> p i r c", i=2, r=G)

        layers = {
            "first": (0, pad_first, acc_first, [2 * G + 1] * 3, 0),
            "1": (3, pad[1], acc[1], [2 * G + 1, G], 0),
            "2": (5, pad[2], acc[2], [2 * G + 1, G], 0),
            "3": (7, pad[3], acc[3], [2 * G + 1, G], 1),
        }

        def span_of(t, img, lo=0, n=PX):
            return t[:, lo + img * IMG2:lo + img * IMG2 + n]

        def both(t):
            n = t.shape[1] // 2
            return t[:, 0:2 * n].rearrange("p (i n) -> p i n", i=2)[:, :, 0:PX]

        block = ctx.enter_context(nc.Block())

        loads = [(ident, "ident"), (haar, "haar"), (w_wave, "w_wave"), (w_loc, "w_loc"), (conv_bias, "conv_bias"),
                 (dw_w, "dw_w"), (pw["loc"], "pw_loc"), (pw["glob"], "pw_glob"), (pw["glob2"], "pw_glob2"),
                 (pw["fuse1"], "pw_fuse1"), (pw["fuse2"], "pw_fuse2"), (pw_bias, "pw_bias"), (pw3, "pw3"),
                 (bias3, "bias3"), (row0, "row0"), (alpha, "alpha"), (ln_g, "ln_g"), (ln_b, "ln_b"), (cls, "cls")]
        chain2, chain3 = 2 * (TAPS - pe_taps - 1), 3 * (TAPS - pe_taps - 1)
        first_reads = 7
        stages = 6
        assert pairs > stages

        def run(eng, body):
            for it in range(stages):
                body(it, [0 <= it - s < pairs for s in range(stages)])
            with eng.Fori(stages, pairs) as it:
                body(it, [True] * stages)
            for it in range(pairs, pairs + stages - 1):
                body(it, [0 <= it - s < pairs for s in range(stages)])

        def capped(value, most):
            return min(value, most) if type(value) is int else value

        @block.sync
        def _(sp):
            for dst, name in loads:
                sp.dma_start(dst[:], t_in[name]).then_inc(S["weights"], 16)

            def body(it, on):
                if on[0]:
                    if not (type(it) is int and it == 0):
                        sp.wait_ge(S["conv_done"], it * 3)
                    sp.dma_start(x_t[:], t_in["x_t"][it]).then_inc(S["x_loaded"], 16)
                if on[4]:
                    p = it - 4
                    sp.wait_ge(S["ln1_affine"], p * 4 + 4)
                    sp.dma_start(h_out[p], h[:]).then_inc(S["h_stored"], 16)
                if on[5]:
                    p = it - 5
                    sp.wait_ge(S["ln2_norm"], p * 4 + 4)
                    sp.dma_start(x_out[p], xn[:]).then_inc(S["x_stored"], 16)
                    sp.wait_ge(S["tr_copied"], p * 2 + 2)
                    sp.dma_start(xt_out[p], xt[:]).then_inc(S["xt_stored"], 16)

            run(sp, body)
            sp.wait_ge(S["h_stored"], 16 * pairs)
            sp.wait_ge(S["x_stored"], 16 * pairs)
            sp.wait_ge(S["xt_stored"], 16 * pairs)

        @block.tensor
        def _(pe):
            pe.wait_ge(S["weights"], 16 * len(loads))
            for n in range(KT):
                colour, m = n // 2, n % 2
                if n >= 2:
                    pe.wait_ge(S["fold_copied"], 2 * (n - 1))
                for b in range(2):
                    mm = pe.matmul(conv_ps[n % 2][:, 0:D], haar[:, b, m * P:(m + 1) * P], w_wave[:, b, colour, :],
                                   start=(b == 0), stop=(b == 1))
                mm.then_inc(S["fold_done"], 1)
            pe.wait_ge(S["fold_copied"], 2 * KT)
            pe.wait_ge(S["setup"], 1)
            pe.wait_ge(S["diag"], 9 * pe_taps)
            pe.wait_ge(S["zeroed"], 1)

            def conv(it, t):
                if t == 0:
                    pe.wait_ge(S["x_loaded"], it * 16 + 16)
                if t == 2:
                    pe.wait_ge(S["gelu_done"], it * 3 + 1)
                elif not (type(it) is int and it == 0):
                    pe.wait_ge(S["gelu_done"], it * 3 if t == 0 else it * 3 - 1)
                for k in range(KT):
                    mm = pe.matmul(conv_ps[t % 2][:, 0:2 * PX], w_conv[:, k, t, :], x_t[:, k, :],
                                   start=(k == 0), stop=(k == KT - 1))
                mm.then_inc(S["conv_done"], 1)

            def taps(name, t):
                first, pads, _, rows, _ = layers[name]
                for k in range(pe_taps):
                    mm = pe.matmul(grid(tap_ps[t % 2], rows[t]), dw_diag[:, first + t, k, :],
                                   shifted(pads[t], k, rows[t]), start=(k == 0), stop=(k == pe_taps - 1))
                mm.then_inc(S["taps_first" if name == "first" else "taps" + name], 1)

            def pointwise_first(w, low, mixed, done):
                pe.matmul(both(pw_ps[0][:, 0:2 * PX]), w[:, 0, :], both(low), start=True, stop=False)
                pe.matmul(both(pw_ps[0][:, 0:2 * PX]), w[:, 1, :], both(mixed), start=False, stop=True).then_inc(done, 1)
                for img in range(2):
                    pe.matmul(pw_ps[1][:, 0:PX], w[:, 2 + 2 * img, :], span_of(low, img), start=(img == 0), stop=False)
                    mm = pe.matmul(pw_ps[1][:, 0:PX], w[:, 3 + 2 * img, :], span_of(mixed, img), start=False, stop=(img == 1))
                mm.then_inc(done, 1)

            def pointwise_one(w, low, high, done):
                pe.matmul(both(pw_ps[0][:, 0:2 * PX]), w[:, 0, :], both(low), start=True, stop=False)
                for img in range(2):
                    mm = pe.matmul(pw_ps[0][:, img * PX:(img + 1) * PX], w[:, 1 + img, :], high[:, :],
                                   start=False, stop=(img == 1))
                mm.then_inc(done, 1)
                for img in range(2):
                    pe.matmul(pw_ps[1][:, 0:PX], w[:, 3 + img, :], both(low)[:, img, :], start=(img == 0), stop=False)
                pe.matmul(pw_ps[1][:, 0:PX], w[:, 5, :], high[:, :], start=False, stop=True).then_inc(done, 1)

            def transposes(p):
                pe.wait_ge(S["ln2_norm"], p * 4 + 4)
                for part in range(2):
                    if not (type(p) is int and p == 0 and part == 0):
                        pe.wait_ge(S["tr_copied"], p * 2 + part)
                    for q in range(4):
                        o = tr_ps[:, (q // 2) * L + (q % 2) * HALF:(q // 2) * L + (q % 2) * HALF + TT]
                        mm = pe.transpose(o, xn[:, q, part * HI:part * HI + P], ident[0:TT, 0:TT])
                    mm.then_inc(S["tr_done"], 1)

            def tokens(p):
                pe.wait_ge(S["dw3"], p * 2 + 2)
                for img in range(2):
                    if not (type(p) is int and p == 0 and img == 0):
                        pe.wait_ge(S["tok_copied"], p * 2 + img)
                    for half in range(2):
                        o = tok_ps[0:TT, half * D:(half + 1) * D]
                        lo = img * IMG2 + half * HALF
                        pe.matmul(o, acc[3][0][:, lo:lo + TT], pw3[:, 0, :], start=True, stop=False)
                        pe.matmul(o, acc[3][1][:, half * HALF:half * HALF + TT], pw3[:, 1 + img, :],
                                  start=False, stop=False)
                        mm = pe.matmul(o, row0[:, :], bias3[:, :], start=False, stop=True)
                    mm.then_inc(S["tok_done"], 1)

            def body(it, on):
                if on[3]:
                    p = it - 3
                    pe.wait_ge(S["joined"], p * 2 + 2)
                    pe.wait_ge(S["first_chain"], capped(it, pairs) * chain3 - chain3 + first_reads)
                    taps("3", 0)
                    taps("3", 1)
                if on[0]:
                    conv(it, 0)
                if on[1]:
                    p = it - 1
                    pe.wait_ge(S["first_dw"], p * 3 + 3)
                    if on[2]:
                        pe.wait_ge(S["relu1"], p * 2)
                    pointwise_first(pw["loc"], acc_first[0], acc_first[2], S["pw_loc"])
                if on[2]:
                    p = it - 2
                    if on[3]:
                        pe.wait_ge(S["chain3"], (it - 3) * chain2 + 2)
                    else:
                        pe.wait_ge(S["first_chain"], it * chain3)
                    pe.wait_ge(S["relu1"], p * 2 + 2)
                    taps("2", 0)
                    taps("2", 1)
                if on[1]:
                    p = it - 1
                    pe.wait_ge(S["loc_out"], p * 2 + 2)
                    pointwise_first(pw["glob"], acc_first[1], acc_first[2], S["pw_glob"])
                if on[3]:
                    tokens(it - 3)
                if on[1]:
                    p = it - 1
                    pe.wait_ge(S["gg_out"], p * 2 + 2)
                    pointwise_one(pw["glob2"], gg[0], gg[1], S["pw_glob2"])
                if on[0]:
                    conv(it, 1)
                if on[1]:
                    p = it - 1
                    if on[2]:
                        pe.wait_ge(S["chain2"], (it - 2) * chain2 + 2)
                    else:
                        pe.wait_ge(S["first_chain"], it * chain3)
                    pe.wait_ge(S["fused"], p * 3 + 3)
                    taps("1", 0)
                    taps("1", 1)
                if on[0]:
                    conv(it, 2)
                if on[5]:
                    transposes(it - 5)
                if on[2]:
                    p = it - 2
                    pe.wait_ge(S["dw2"], p * 2 + 2)
                    pe.wait_ge(S["fused"], capped(p * 3 + 6, pairs * 3))
                    pointwise_one(pw["fuse2"], acc[2][0], acc[2][1], S["pw2"])
                if on[0]:
                    if on[1]:
                        pe.wait_ge(S["chain1"], (it - 1) * chain2 + 2)
                    pe.wait_ge(S["gelu_done"], it * 3 + 2)
                    taps("first", 0)
                    taps("first", 1)
                if on[1]:
                    p = it - 1
                    pe.wait_ge(S["dw1"], p * 2 + 2)
                    if on[2]:
                        pe.wait_ge(S["relu2"], (it - 2) * 2 + 2)
                    else:
                        pe.wait_ge(S["fused"], p * 3 + 3)
                    pointwise_one(pw["fuse1"], acc[1][0], acc[1][1], S["pw1"])
                if on[0]:
                    pe.wait_ge(S["gelu_done"], it * 3 + 3)
                    pe.wait_ge(S["first_chain"], it * chain3 + 1)
                    taps("first", 2)

            run(pe, body)

        @block.scalar
        def _(act):
            act.wait_ge(S["weights"], 16 * len(loads))
            for n in range(KT):
                act.wait_ge(S["fold_done"], n + 1)
                nc.scalar.copy(w_conv[:, n, 1, :], conv_ps[n % 2][:, 0:P]).then_inc(S["fold_copied"], 1)
                nc.scalar.copy(w_conv[:, n, 2, HI:P], conv_ps[n % 2][:, P:D]).then_inc(S["fold_copied"], 1)
            nc.scalar.activation(gate[:, :], alpha[:, :], ACT.Tanh).then_inc(S["gate_act"], 1)
            act.wait_ge(S["gate_ready"], 3)
            act.wait_ge(S["zeroed"], 1)

            def body(it, on):
                def gelu(t):
                    act.wait_ge(S["conv_done"], it * 3 + t + 1)
                    if not (type(it) is int and it == 0):
                        act.wait_ge(S["first_dw"], it * 3)
                    nc.scalar.activation(maps(pad_first[t]), as_maps(conv_ps[t % 2][:, 0:2 * PX]), ACT.Gelu,
                                         bias=conv_bias[:, t:t + 1]).then_inc(S["gelu_done"], 1)

                if on[0]:
                    gelu(0)
                if on[1]:
                    p = it - 1
                    for t in range(2):
                        act.wait_ge(S["pw_loc"], p * 2 + t + 1)
                        if t == 0 and not (type(p) is int and p == 0):
                            act.wait_ge(S["loc_kept"], p * 2)
                            act.wait_ge(S["part_out"], p * 2)
                        nc.scalar.activation(loc[t][:, :], pw_ps[t][:, 0:(2 - t) * PX], ACT.Identity,
                                             bias=pw_bias[:, 0, t:t + 1]).then_inc(S["loc_out"], 1)
                if on[1]:
                    p = it - 1
                    for t in range(2):
                        act.wait_ge(S["pw_glob"], p * 2 + t + 1)
                        if t == 0 and not (type(p) is int and p == 0):
                            act.wait_ge(S["pw_glob2"], p * 2)
                        nc.scalar.activation(gg[t][:, :], pw_ps[t][:, 0:(2 - t) * PX], ACT.Gelu,
                                             bias=pw_bias[:, 1, t:t + 1]).then_inc(S["gg_out"], 1)
                    for t in range(2):
                        act.wait_ge(S["loc_out"], p * 2 + 2)
                        if t == 0 and not (type(p) is int and p == 0):
                            act.wait_ge(S["fused"], p * 3)
                        nc.scalar.activation(loc_part[t][:, :], loc[t][:, :], ACT.Identity, scale=one_minus[:, t:t + 1],
                                             bias=gate_b[:, t:t + 1]).then_inc(S["part_out"], 1)
                if on[3]:
                    p = it - 3
                    for img in range(2):
                        act.wait_ge(S["tok_done"], p * 2 + img + 1)
                        if img == 0 and not (type(p) is int and p == 0):
                            act.wait_ge(S["ln1_norm"], p * 4)
                        nc.scalar.copy(tok[:, 2 * img:2 * img + 2, :],
                                       tok_ps[0:TT, 0:2 * D].rearrange("p (h c) -> p h c", h=2)).then_inc(S["tok_copied"], 1)
                if on[0]:
                    gelu(1)
                if on[0]:
                    gelu(2)
                if on[5]:
                    p = it - 5
                    for part in range(2):
                        act.wait_ge(S["tr_done"], p * 2 + part + 1)
                        if part == 0 and not (type(p) is int and p == 0):
                            act.wait_ge(S["xt_stored"], p * 16)
                        nc.scalar.copy(xt[:, part, :], tr_ps[:, 0:2 * L]).then_inc(S["tr_copied"], 1)
                if on[2]:
                    p = it - 2
                    for t in range(2):
                        act.wait_ge(S["pw2"], p * 2 + t + 1)
                        if t == 0 and not (type(p) is int and p == 0):
                            act.wait_ge(S["joined"], p * 2)
                        nc.scalar.activation(relu2[t][:, :], pw_ps[t][:, 0:(2 - t) * PX], ACT.Relu,
                                             bias=pw_bias[:, 4, t:t + 1]).then_inc(S["relu2"], 1)
                if on[1]:
                    p = it - 1
                    for t in range(2):
                        act.wait_ge(S["pw1"], p * 2 + t + 1)
                        if t == 0 and not (type(p) is int and p == 0):
                            act.wait_ge(S["dw2"], p * 2)
                        dst, src = ((maps(pad[2][0]), as_maps(pw_ps[0][:, 0:2 * PX])) if t == 0 else
                                    (pad[2][1][:, 1:G + 1, 1:G + 1], grid(pw_ps[1], G)))
                        nc.scalar.activation(dst, src, ACT.Relu, bias=pw_bias[:, 3, t:t + 1]).then_inc(S["relu1"], 1)

            run(act, body)

        @block.gpsimd
        def _(pool):
            for t in pad_first + pad[1] + pad[2] + pad[3]:
                nc.gpsimd.memset(t[:], 0.0)
            nc.gpsimd.memset(acc[3][0][:, 0:1], 0.0)
            nc.gpsimd.memset(acc[3][1][:, 0:1], 0.0)
            nc.gpsimd.memset(minus_half[:], -0.5).then_inc(S["zeroed"], 1)
            pool.wait_ge(S["weights"], 16 * len(loads))
            pool.wait_ge(S["zeroed"], 1)

            def body(it, on):
                if on[5]:
                    p = it - 5
                    pool.wait_ge(S["ln2_stats"], p * 9 + 9)
                    nc.gpsimd.tensor_tensor(rs2[:, :], ve2[:, :], minus_half[:, :], ALU.pow).then_inc(S["ln2_rs"], 1)
                if on[4]:
                    p = it - 4
                    pool.wait_ge(S["ln1_stats"], p * 9 + 9)
                    nc.gpsimd.tensor_tensor(rs1[:, :], ve1[:, :], minus_half[:, :], ALU.pow).then_inc(S["ln1_rs"], 1)
                    pool.wait_ge(S["ln1_norm"], p * 4 + 4)
                    nc.gpsimd.tensor_tensor(hg[:, :, :], hn[:, :, :], ln_g[:, :].unsqueeze(1).broadcast_to([TT, 4, D]),
                                            ALU.mult).then_inc(S["ln1_affine"], 1)
                    pool.wait_ge(S["ln1_affine"], p * 4 + 1)
                    if not (type(p) is int and p == 0):
                        pool.wait_ge(S["h_stored"], p * 16)
                        pool.wait_ge(S["ln2_norm"], p * 4)
                    nc.gpsimd.tensor_tensor(h[:, :, :], hg[:, :, :], ln_b[:, :].unsqueeze(1).broadcast_to([TT, 4, D]),
                                            ALU.add).then_inc(S["ln1_affine"], 1)
                    pool.wait_ge(S["ln1_affine"], p * 4 + 2)
                    for img in range(2):
                        if img == 0:
                            pool.sem_inc(S["fence"], 1)
                        nc.gpsimd.tensor_copy(h[0:1, 2 * img, :], cls[0:1, :]).then_inc(S["ln1_affine"], 1)
                if on[2]:
                    p = it - 2
                    for t in range(2):
                        pool.wait_ge(S["relu2"], p * 2 + t + 1)
                        if t == 0 and not (type(p) is int and p == 0):
                            pool.wait_ge(S["dw3"], p * 2)
                        if t == 0:
                            pool.wait_ge(S["loc_kept"], p * 2 + 2)
                            nc.gpsimd.tensor_tensor(maps(pad[3][0]), as_maps(relu2[0][:, :]), as_maps(loc_old[0][:, :]),
                                                    ALU.add).then_inc(S["joined"], 1)
                        else:
                            nc.gpsimd.tensor_tensor(pad[3][1][:, 1:G + 1, 1:G + 1], grid(relu2[1], G), grid(loc_old[1], G),
                                                    ALU.add).then_inc(S["joined"], 1)
                if on[1]:
                    p = it - 1
                    for t in range(2):
                        pool.wait_ge(S["loc_out"], p * 2 + t + 1)
                        if on[2]:
                            pool.wait_ge(S["joined"], (it - 2) * 2 + t + 1)
                        pool.sem_inc(S["fence"], 1)
                        nc.gpsimd.tensor_copy(loc_old[t][:, :], loc[t][:, :]).then_inc(S["loc_kept"], 1)

            run(pool, body)

        @block.vector
        def _(dve):
            dve.wait_ge(S["weights"], 16 * len(loads))
            for n in range(KT):
                nc.vector.tensor_copy(w_conv[:, n, 0, :], w_loc[:, n, 0:P])
                last = nc.vector.tensor_copy(w_conv[:, n, 2, 0:HI], w_loc[:, n, P:D])
            last.then_inc(S["setup"], 1)
            for q in range(9):
                for k in range(pe_taps):
                    nc.vector.tensor_scalar(dw_diag[:, q, k, :], ident[:, :], dw_w[:, q, k:k + 1], None,
                                            ALU.mult).then_inc(S["diag"], 1)
            dve.wait_ge(S["gate_act"], 1)
            nc.vector.tensor_scalar(one_minus[:, :], gate[:, :], -0.5, 0.5, ALU.mult, ALU.add).then_inc(S["gate_ready"], 1)
            dve.wait_ge(S["gate_ready"], 1)
            nc.vector.tensor_scalar(gate[:, :], gate[:, :], 0.5, 0.5, ALU.mult, ALU.add).then_inc(S["gate_ready"], 1)
            dve.wait_ge(S["gate_ready"], 2)
            nc.vector.tensor_tensor(gate_b[:, :], gate[:, :], pw_bias[:, 2, :], ALU.mult).then_inc(S["gate_ready"], 1)
            dve.wait_ge(S["gate_ready"], 3)
            dve.wait_ge(S["zeroed"], 1)

            def depthwise(name, p, dep_sem, dep):
                first, pads, accs, rows, lo = layers[name]
                n = len(pads)
                steps = TAPS - pe_taps
                taps_done = S["taps_first" if name == "first" else "taps" + name]
                chain = S["first_chain" if name == "first" else "chain" + name]
                done = S["first_dw" if name == "first" else "dw" + name]
                order = [(k - 2 * (t // 2), t) for k in range(steps + 2) for t in range(n) if 0 <= k - 2 * (t // 2) < steps]
                at = {}
                count = 0
                per = n * (steps - 1)
                for k, t in order:
                    tap = pe_taps + k
                    dst = grid(accs[t], rows[t], lo)
                    if k == 0:
                        dve.wait_ge(taps_done, p * n + t + 1)
                        src = grid(tap_ps[t % 2], rows[t])
                        if t == 0 and dep is not None:
                            dve.wait_ge(dep_sem, dep)
                    else:
                        dve.wait_ge(chain, p * per + at[t])
                        src = dst
                    ins = nc.vector.scalar_tensor_tensor(out=dst, in0=shifted(pads[t], tap, rows[t]),
                                                         scalar=dw_w[:, first + t, tap:tap + 1], in1=src,
                                                         op0=ALU.mult, op1=ALU.add)
                    if k < steps - 1:
                        ins.then_inc(chain, 1)
                        count += 1
                        at[t] = count
                    else:
                        ins.then_inc(done, 1)

            def stats(p, src, st, mv, ve, s, norm):
                if not (type(p) is int and p == 0):
                    dve.wait_ge(norm, p * 4)
                for q in range(4):
                    nc.vector.bn_stats(st[:, q, :], src[:, q, :]).then_inc(s, 1)
                for q in range(4):
                    dve.wait_ge(s, p * 9 + q + 1)
                    dve.sem_inc(S["fence"], 1)
                    nc.vector.bn_aggr(mv[:, q, :], st[:, q, :]).then_inc(s, 1)
                dve.wait_ge(s, p * 9 + 8)
                nc.vector.tensor_scalar(ve[:, :], mv[:, :, 1], LN_EPS, None, ALU.add).then_inc(s, 1)

            def normalise(dst, src, mv, rs, s):
                for q in range(4):
                    nc.vector.tensor_scalar(dst[:, q, :], src[:, q, :], mv[:, q, 0:1], rs[:, q:q + 1],
                                            ALU.subtract, ALU.mult).then_inc(s, 1)

            def body(it, on):
                if on[5]:
                    p = it - 5
                    dve.wait_ge(S["ln1_affine"], p * 4 + 4)
                    if not (type(p) is int and p == 0):
                        dve.wait_ge(S["ln2_rs"], p)
                    stats(p, h, st2, mv2, ve2, S["ln2_stats"], S["ln2_norm"])
                if on[4]:
                    p = it - 4
                    dve.wait_ge(S["tok_copied"], p * 2 + 2)
                    if not (type(p) is int and p == 0):
                        dve.wait_ge(S["ln1_rs"], p)
                    stats(p, tok, st1, mv1, ve1, S["ln1_stats"], S["ln1_norm"])
                if on[3]:
                    p = it - 3
                    first = type(p) is int and p == 0
                    depthwise("3", p, S["tok_done"], None if first else p * 2)
                if on[5]:
                    p = it - 5
                    dve.wait_ge(S["ln2_rs"], p + 1)
                    if not (type(p) is int and p == 0):
                        dve.wait_ge(S["x_stored"], p * 16)
                        dve.wait_ge(S["tr_done"], p * 2)
                    normalise(xn, h, mv2, rs2, S["ln2_norm"])
                if on[4]:
                    p = it - 4
                    dve.wait_ge(S["ln1_rs"], p + 1)
                    if not (type(p) is int and p == 0):
                        dve.wait_ge(S["ln1_affine"], p * 4)
                    normalise(hn, tok, mv1, rs1, S["ln1_norm"])
                if on[2]:
                    p = it - 2
                    first = type(p) is int and p == 0
                    depthwise("2", p, S["pw2"], None if first else p * 2)
                if on[1]:
                    p = it - 1
                    if not (type(p) is int and p == 0):
                        dve.wait_ge(S["dw1"], p * 2)
                    dve.wait_ge(S["part_out"], p * 2 + 2)
                    dve.wait_ge(S["pw_glob2"], p * 2 + 2)
                    for img in range(2):
                        nc.vector.scalar_tensor_tensor(out=pad[1][0][:, 1 + img * (G + 1):1 + img * (G + 1) + G, 1:G + 1],
                                                       in0=grid(pw_ps[0], G, img * PX), scalar=gate[:, 0:1],
                                                       in1=grid(loc_part[0], G, img * PX),
                                                       op0=ALU.mult, op1=ALU.add).then_inc(S["fused"], 1)
                    nc.vector.scalar_tensor_tensor(out=pad[1][1][:, 1:G + 1, 1:G + 1], in0=grid(pw_ps[1], G),
                                                   scalar=gate[:, 1:2], in1=grid(loc_part[1], G),
                                                   op0=ALU.mult, op1=ALU.add).then_inc(S["fused"], 1)
                if on[1]:
                    p = it - 1
                    first = type(p) is int and p == 0
                    depthwise("1", p, S["pw1"], None if first else p * 2)
                if on[0]:
                    first = type(it) is int and it == 0
                    depthwise("first", it, S["pw_glob"], None if first else it * 2)

            run(dve, body)


B_ROWS, DECAYS, DRIVES, HIDS, PRODS = 4, 8, 12, 4, 8

PE_START = (0, 1, 3, 4, 6, 7, 15, 17, 20, 22, 24)
PE_PROJECT = (11, 13)
ACT_START = (5, 6, 8, 9, 11, 12, 20, 21, 24, 26, 28)
ACT_SILU = 13
ACT_OUT = (16, 18)
ACT_SPLIT = (22, 31, 36)
ACT_SOFTPLUS = (29, 30, 32)
POOL_GATE = (11, 12, 13)
POOL_ROOT = 31
POOL_SPLIT = (29, 36)
POOL_AFFINE = (38, 41, 44)
DVE_SKIP = (1, 2, 3)
DVE_END = (19, 20, 21, 23, 27)
DVE_SOFTPLUS = (31, 33, 34, 35)


def mix_tokens(nc, t_in, h_in, x_in, xt_in, h_out, pairs):
    assert pairs % 2 == 0 and pairs >= 6
    W = 2 * L
    UNITS = NS * DT
    with ExitStack() as ctx:
        def sb(name, shape, dt=F32):
            return ctx.enter_context(nc.sbuf_tensor(name, shape, dt))

        def sem(name):
            return ctx.enter_context(nc.semaphore(name))

        def bank(name):
            return ctx.enter_context(nc.psum_tensor(name, [P, 512], F32))

        ident = sb("b_ident", [P, P])
        w_in = sb("b_w_in", [P, 2, 2 * DT, P])
        w_x = sb("b_w_x", [P, DT, P])
        w_bc = sb("b_w_bc", [P, DT, 96])
        w_dt = sb("b_w_dt", [P, DT, P])
        b_dt = sb("b_b_dt", [P, DT])
        a_log = sb("b_a_log", [P, DT, NS])
        a_exp = sb("b_a_exp", [P, DT, NS])
        a_neg = sb("b_a_neg", [P, DT, NS])
        d_skip = sb("b_d_skip", [P, DT])
        w_out = sb("b_w_out", [P, DT, D])
        gamma = sb("b_gamma", [TT, D])
        beta = sb("b_beta", [TT, D])
        pick_f = sb("b_pick_f", [96, 2 * NS, P])
        pick = sb("b_pick", [96, 2 * NS, P], BF16)
        minus_half = sb("b_minus_half", [TT, 4])

        xt = sb("b_xt", [P, 2, W])
        xz_raw = sb("b_xz_raw", [P, 2 * DT, W])
        xz = [sb(f"b_xz{q}", [P, 2 * DT, W]) for q in range(2)]
        xd = sb("b_xd", [P, W])
        bc_f = sb("b_bc_f", [96, W])
        bc_hi = sb("b_bc_hi", [96, W], BF16)
        bc_r = sb("b_bc_r", [96, W])
        bc_mid = sb("b_bc_mid", [96, W], BF16)
        bc = [sb(f"b_bc{q}", [96, W], BF16) for q in range(2)]
        absd = sb("b_absd", [P, DT, W])
        relud = sb("b_relud", [P, DT, W])
        expd = sb("b_expd", [P, DT, W])
        onep = sb("b_onep", [P, DT, W])
        logd = sb("b_logd", [P, DT, W])
        lost, sumd = absd, logd
        dt = [sb(f"b_dt{q}", [P, DT, W]) for q in range(2)]
        dtx = [sb(f"b_dtx{q}", [P, DT, W]) for q in range(2)]
        b_row = [sb(f"b_b_row{i}", [P, W]) for i in range(B_ROWS)]
        decays = [sb(f"b_decays{i}", [P, W]) for i in range(DECAYS)]
        dbx = [sb(f"b_dbx{i}", [P, W]) for i in range(DRIVES)]
        hid = [sb(f"b_hid{i}", [P, W]) for i in range(HIDS)]
        prod = [sb(f"b_prod{i}", [P, W]) for i in range(PRODS)]
        yd = sb("b_yd", [P, DT, W])
        yg = sb("b_yg", [P, DT, W])
        mo = sb("b_mo", [TT, 4, D])
        xn = sb("b_xn", [TT, 4, D])
        hin = sb("b_hin", [TT, 4, D])
        hs = sb("b_hs", [TT, 4, D])
        st = sb("b_st", [TT, 4, 6])
        mv = sb("b_mv", [TT, 4, 2])
        ve = sb("b_ve", [TT, 4])
        rs = sb("b_rs", [TT, 4])
        hn = sb("b_hn", [TT, 4, D])
        ha = sb("b_ha", [TT, 4, D])
        hb = hn
        h2 = sb("b_h2", [TT, 4, D])

        y_ps = [bank(f"b_y_ps{j}") for j in range(DT)]
        b_ps = bank("b_b_ps")
        c_ps = [bank(f"b_c_ps{i}") for i in range(2)]
        ob = [bank(f"b_ob{i}") for i in range(2)]

        S = {n: sem("b_" + n) for n in (
            "fence", "weights", "zeroed", "picks", "a_ready", "xt_loaded", "xn_loaded", "h_loaded",
            "in_done", "in_out", "silu", "bc_parts", "bc_rest", "dt_relu", "dt_act", "dt_ready", "dtx_ready",
            "b_done", "b_out", "c_done", "exp_done", "dbx_done", "scan_done", "prod_done", "acc_done",
            "yd_done", "yg_done", "out_done", "mo_out", "res", "stats", "rs_ready", "norm", "affine", "stored")}

        loads = [(ident, "ident"), (w_in, "w_in"), (w_x, "w_x"), (w_bc, "w_bc"), (w_dt, "w_dt"), (b_dt, "b_dt"),
                 (a_log, "a_log"), (d_skip, "d_skip"), (w_out, "w_out"), (gamma, "gamma"), (beta, "beta"), (pick_f, "pick")]

        def run(eng, body):
            body(-1, 1, False, False, True)
            body(0, 0, False, True, True)
            body(1, 1, True, True, True)
            body(2, 0, True, True, True)
            with eng.Fori(1, (pairs - 2) // 2) as m:
                body(m * 2 + 1, 1, True, True, True)
                body(m * 2 + 2, 0, True, True, True)
            body(pairs - 1, 1, True, True, False)
            body(pairs, 0, True, False, False)

        def late(p):
            return not (type(p) is int and p == 0)

        def images(t):
            return t.rearrange("p (i l) -> p i l", i=2)

        block = ctx.enter_context(nc.Block())

        @block.sync
        def _(sp):
            for dst, name in loads:
                sp.dma_start(dst[:], t_in[name]).then_inc(S["weights"], 16)

            def body(k, q, last, now, nxt):
                if nxt:
                    p = k + 1
                    if late(p):
                        sp.wait_ge(S["in_done"], p * 11 - 5)
                    sp.dma_start(xt[:], xt_in[p]).then_inc(S["xt_loaded"], 16)
                if last:
                    p = k - 1
                    if late(p):
                        sp.wait_ge(S["res"], p)
                    sp.dma_start(xn[:], x_in[p]).then_inc(S["xn_loaded"], 16)
                    if late(p):
                        sp.wait_ge(S["affine"], p * 3)
                    sp.dma_start(hin[:], h_in[p]).then_inc(S["h_loaded"], 16)
                    sp.wait_ge(S["affine"], p * 3 + 3)
                    sp.dma_start(h_out[p], h2[:]).then_inc(S["stored"], 16)

            run(sp, body)
            sp.wait_ge(S["stored"], pairs * 16)

        @block.tensor
        def _(pe):
            pe.wait_ge(S["weights"], 16 * len(loads))
            pe.wait_ge(S["picks"], 1)

            def start(p, q, i, ends):
                if i == 0:
                    pe.wait_ge(S["xt_loaded"], p * 16 + 16)
                if i >= 2:
                    pe.wait_ge(S["in_out"], p * 11 + i - 1)
                elif late(p):
                    pe.wait_ge(S["in_out"], p * 11)
                if i in (6, 7) and ends:
                    pe.wait_ge(S["mo_out"], p * 2 + i - 9)
                if i == 6:
                    pe.wait_ge(S["silu"], p + 1)
                if i == 8:
                    pe.wait_ge(S["in_out"], p * 11 + 7)
                o = ob[i % 2][:, 0:W]
                if i < 6:
                    for part in range(2):
                        mm = pe.matmul(o, w_in[:, part, i, :], xt[:, part, :], start=(part == 0), stop=(part == 1))
                elif i == 6:
                    for j in range(DT):
                        mm = pe.matmul(o, w_x[:, j, :], xz[q][:, j, :], start=(j == 0), stop=(j == DT - 1))
                elif i == 7:
                    for j in range(DT):
                        mm = pe.matmul(o[0:96, :], w_bc[:, j, :], xz[q][:, j, :], start=(j == 0), stop=(j == DT - 1))
                else:
                    mm = pe.matmul(o, w_dt[:, i - 8, :], xd[:, :], start=True, stop=True)
                mm.then_inc(S["in_done"], 1)

            def row_b(p, q, n):
                if n == 0:
                    pe.wait_ge(S["bc_parts"], p * 4 + 4)
                    pe.wait_ge(S["bc_rest"], p * 2 + 2)
                if late(p) or n > 0:
                    pe.wait_ge(S["b_out"], p * NS + n)
                pe.matmul(b_ps[:, 0:W], pick[:, n, :], bc[q][:, :], start=True, stop=True).then_inc(S["b_done"], 1)

            def row_c(p, q, n):
                if late(p) or n > 1:
                    pe.wait_ge(S["prod_done"], p * UNITS + (n - 1) * DT)
                pe.matmul(c_ps[n % 2][:, 0:W], pick[:, NS + n, :], bc[q][:, :], start=True, stop=True)\
                    .then_inc(S["c_done"], 1)

            def add_up(p, u):
                n, j = u // DT, u % DT
                if n == 0 and late(p):
                    pe.wait_ge(S["yd_done"], p * DT - DT + j + 1)
                pe.wait_ge(S["prod_done"], p * UNITS + u + 1)
                pe.matmul(y_ps[j][:, 0:W], ident[:, :], prod[u % PRODS][:, :], start=(n == 0), stop=(n == NS - 1))\
                    .then_inc(S["acc_done"], 1)

            def project(p, img, starts):
                if img == 0:
                    pe.wait_ge(S["yg_done"], p * DT + DT)
                if starts:
                    pe.wait_ge(S["in_out"], p * 11 + 2 * 11 + 5 + img)
                else:
                    pe.wait_ge(S["in_out"], pairs * 11)
                if late(p):
                    pe.wait_ge(S["mo_out"], p * 2)
                for half in range(2):
                    lo = img * L + half * HALF
                    for j in range(DT):
                        mm = pe.matmul(ob[img][0:TT, half * D:(half + 1) * D], yg[:, j, lo:lo + TT], w_out[:, j, :],
                                       start=(j == 0), stop=(j == DT - 1))
                mm.then_inc(S["out_done"], 1)

            def body(k, q, last, now, nxt):
                for u in range(UNITS):
                    n, j = u // DT, u % DT
                    if j == 0:
                        if n + 3 < NS:
                            if now:
                                row_b(k, q, n + 3)
                        elif nxt:
                            row_b(k + 1, 1 - q, n + 3 - NS)
                        if n + 1 < NS:
                            if now:
                                row_c(k, q, n + 1)
                        elif nxt:
                            row_c(k + 1, 1 - q, 0)
                    if nxt and u in PE_START:
                        start(k + 1, 1 - q, PE_START.index(u), last)
                    if last and u in PE_PROJECT:
                        project(k - 1, PE_PROJECT.index(u), nxt)
                    if now:
                        add_up(k, u)

            run(pe, body)

        @block.scalar
        def _(act):
            act.wait_ge(S["weights"], 16 * len(loads))
            act.wait_ge(S["zeroed"], DECAYS)
            nc.scalar.activation(a_exp[:, :, :], a_log[:, :, :], ACT.Exp).then_inc(S["a_ready"], 1)
            act.wait_ge(S["a_ready"], 1)
            nc.scalar.mul(a_neg[:, :, :], a_exp[:, :, :], -1.0).then_inc(S["a_ready"], 1)
            act.wait_ge(S["a_ready"], 2)

            def start(p, q, i):
                act.wait_ge(S["in_done"], p * 11 + i + 1)
                if i < 6:
                    if i == 0 and late(p):
                        act.wait_ge(S["silu"], p)
                    nc.scalar.copy(xz_raw[:, i, :], ob[i % 2][:, 0:W]).then_inc(S["in_out"], 1)
                elif i == 6:
                    nc.scalar.copy(xd[:, :], ob[0][:, 0:W]).then_inc(S["in_out"], 1)
                elif i == 7:
                    if late(p):
                        act.wait_ge(S["bc_rest"], p * 2)
                    nc.scalar.copy(bc_f[:, :], ob[1][0:96, 0:W]).then_inc(S["in_out"], 1)
                else:
                    j = i - 8
                    if j == 0 and late(p):
                        act.wait_ge(S["dt_act"], p * 3)
                        act.wait_ge(S["dt_ready"], p * 3)
                    nc.scalar.activation(relud[:, j, :], ob[i % 2][:, 0:W], ACT.Relu, bias=b_dt[:, j:j + 1]).then_inc(S["dt_relu"], 1)
                    nc.scalar.activation(absd[:, j, :], ob[i % 2][:, 0:W], ACT.Abs, bias=b_dt[:, j:j + 1]).then_inc(S["in_out"], 1)

            def silu(p, q):
                act.wait_ge(S["in_out"], p * 11 + 6)
                if type(p) is not int or p >= 2:
                    act.wait_ge(S["yg_done"], p * DT - DT)
                nc.scalar.activation(xz[q][:, :, :], xz_raw[:, :, :], ACT.Silu).then_inc(S["silu"], 1)

            def bc_step(p, q, i):
                if i == 0:
                    act.wait_ge(S["in_out"], p * 11 + 8)
                    if late(p):
                        act.wait_ge(S["bc_parts"], p * 4)
                        act.wait_ge(S["bc_rest"], p * 2)
                    nc.scalar.copy(bc_hi[:, :], bc_f[:, :]).then_inc(S["bc_parts"], 1)
                elif i == 1:
                    act.wait_ge(S["bc_rest"], p * 2 + 1)
                    nc.scalar.copy(bc_mid[:, :], bc_r[:, :]).then_inc(S["bc_parts"], 1)
                else:
                    act.wait_ge(S["bc_rest"], p * 2 + 2)
                    nc.scalar.copy(bc[q][0:32, :], bc_hi[0:32, :]).then_inc(S["bc_parts"], 1)
                    nc.scalar.copy(bc[q][32:64, :], bc_mid[32:64, :]).then_inc(S["bc_parts"], 1)

            def softplus(p, i):
                if i == 0:
                    act.wait_ge(S["in_out"], p * 11 + 11)
                    nc.scalar.activation(expd[:, :, :], absd[:, :, :], ACT.Exp, scale=-1.0).then_inc(S["dt_act"], 1)
                elif i == 1:
                    act.wait_ge(S["dt_act"], p * 3 + 1)
                    nc.scalar.activation(onep[:, :, :], expd[:, :, :], ACT.Identity, bias=1.0).then_inc(S["dt_act"], 1)
                else:
                    act.wait_ge(S["dt_act"], p * 3 + 2)
                    nc.scalar.activation(logd[:, :, :], onep[:, :, :], ACT.Ln).then_inc(S["dt_act"], 1)

            def b_row_out(p, n):
                act.wait_ge(S["b_done"], p * NS + n + 1)
                if late(p) or n >= B_ROWS:
                    act.wait_ge(S["dbx_done"], p * UNITS + (n - B_ROWS + 1) * DT)
                nc.scalar.copy(b_row[n % B_ROWS][:, :], b_ps[:, 0:W]).then_inc(S["b_out"], 1)

            def decay(p, q, u):
                n, j = u // DT, u % DT
                if u == 0:
                    act.wait_ge(S["dt_ready"], p * 3 + 3)
                if late(p) or u >= DECAYS:
                    act.wait_ge(S["scan_done"], p * UNITS + u + 1 - DECAYS)
                nc.scalar.activation(images(decays[u % DECAYS])[:, :, 1:L], images(dt[q][:, j, :])[:, :, 1:L], ACT.Exp,
                                     scale=a_neg[:, j, n:n + 1]).then_inc(S["exp_done"], 1)

            def body(k, q, last, now, nxt):
                for u in range(UNITS):
                    n, j = u // DT, u % DT
                    if j == 2:
                        if n + 2 < NS:
                            if now:
                                b_row_out(k, n + 2)
                        elif nxt:
                            b_row_out(k + 1, n + 2 - NS)
                    if now:
                        decay(k, q, u)
                    if nxt and u in ACT_START:
                        start(k + 1, 1 - q, ACT_START.index(u))
                    if nxt and u == ACT_SILU:
                        silu(k + 1, 1 - q)
                    if last and u in ACT_OUT:
                        p, img = k - 1, ACT_OUT.index(u)
                        act.wait_ge(S["out_done"], p * 2 + img + 1)
                        if img == 0 and late(p):
                            act.wait_ge(S["res"], p)
                        nc.scalar.copy(mo[:, 2 * img:2 * img + 2, :],
                                       ob[img][0:TT, 0:2 * D].rearrange("p (h c) -> p h c", h=2)).then_inc(S["mo_out"], 1)
                    if nxt and u in ACT_SPLIT:
                        bc_step(k + 1, 1 - q, ACT_SPLIT.index(u))
                    if nxt and u in ACT_SOFTPLUS:
                        softplus(k + 1, ACT_SOFTPLUS.index(u))

            run(act, body)

        @block.gpsimd
        def _(pool):
            nc.gpsimd.memset(minus_half[:], -0.5).then_inc(S["fence"], 1)
            pool.wait_ge(S["fence"], 1)
            pool.wait_ge(S["weights"], 16 * len(loads))

            def drive(p, q, u):
                n, j = u // DT, u % DT
                if u == 0:
                    pool.wait_ge(S["dtx_ready"], p + 1)
                if j == 0:
                    pool.wait_ge(S["b_out"], p * NS + n + 1)
                if late(p) or u >= DRIVES:
                    pool.wait_ge(S["scan_done"], p * UNITS + u + 1 - DRIVES)
                nc.gpsimd.tensor_tensor(dbx[u % DRIVES][:, :], dtx[q][:, j, :], b_row[n % B_ROWS][:, :], ALU.mult)\
                    .then_inc(S["dbx_done"], 1)

            def affine(p, i):
                if i == 0:
                    pool.wait_ge(S["norm"], p * 4 + 4)
                    nc.gpsimd.tensor_tensor(ha[:, :, :], hn[:, :, :], gamma[:, :].unsqueeze(1).broadcast_to([TT, 4, D]),
                                            ALU.mult).then_inc(S["affine"], 1)
                elif i == 1:
                    pool.wait_ge(S["affine"], p * 3 + 1)
                    nc.gpsimd.tensor_tensor(hb[:, :, :], ha[:, :, :], beta[:, :].unsqueeze(1).broadcast_to([TT, 4, D]),
                                            ALU.add).then_inc(S["affine"], 1)
                else:
                    pool.wait_ge(S["affine"], p * 3 + 2)
                    pool.wait_ge(S["h_loaded"], p * 16 + 16)
                    if late(p):
                        pool.wait_ge(S["stored"], p * 16)
                    nc.gpsimd.tensor_tensor(h2[:, :, :], hb[:, :, :], hin[:, :, :], ALU.add).then_inc(S["affine"], 1)

            def gate(p, q, j):
                pool.wait_ge(S["yd_done"], p * DT + j + 1)
                if j == 0 and late(p):
                    pool.wait_ge(S["out_done"], p * 2)
                nc.gpsimd.tensor_tensor(yg[:, j, :], yd[:, j, :], xz[q][:, DT + j, :], ALU.mult).then_inc(S["yg_done"], 1)

            def bc_step(p, q, i):
                pool.wait_ge(S["bc_parts"], p * 4 + i + 1)
                if i == 0:
                    nc.gpsimd.tensor_tensor(bc_r[:, :], bc_f[:, :], bc_hi[:, :], ALU.subtract).then_inc(S["bc_rest"], 1)
                else:
                    if type(p) is not int or p >= 2:
                        pool.wait_ge(S["c_done"], p * NS - NS)
                    nc.gpsimd.tensor_tensor(bc[q][:, :], bc_r[:, :], bc_mid[:, :], ALU.subtract).then_inc(S["bc_rest"], 1)

            def body(k, q, last, now, nxt):
                for u in range(UNITS):
                    if now:
                        drive(k, q, u)
                    if last and u in POOL_GATE:
                        gate(k - 1, 1 - q, POOL_GATE.index(u))
                    if last and u == POOL_ROOT:
                        pool.wait_ge(S["stats"], k * 9)
                        nc.gpsimd.tensor_tensor(rs[:, :], ve[:, :], minus_half[:, :], ALU.pow).then_inc(S["rs_ready"], 1)
                    if last and u in POOL_AFFINE:
                        affine(k - 1, POOL_AFFINE.index(u))
                    if nxt and u in POOL_SPLIT:
                        bc_step(k + 1, 1 - q, POOL_SPLIT.index(u))

            run(pool, body)

        @block.vector
        def _(dve):
            for i in range(DECAYS):
                nc.vector.memset(decays[i][:, :], 0.0).then_inc(S["zeroed"], 1)
            dve.wait_ge(S["weights"], 16 * len(loads))
            nc.vector.tensor_copy(pick[:, :, :], pick_f[:, :, :]).then_inc(S["picks"], 1)

            def scan(p, u):
                dve.wait_ge(S["exp_done"], p * UNITS + u + 1)
                dve.wait_ge(S["dbx_done"], p * UNITS + u + 1)
                if late(p) or u >= HIDS:
                    dve.wait_ge(S["prod_done"], p * UNITS + u + 1 - HIDS)
                nc.vector.tensor_tensor_scan(hid[u % HIDS][:, :], decays[u % DECAYS][:, :], dbx[u % DRIVES][:, :], 0.0,
                                             ALU.mult, ALU.add).then_inc(S["scan_done"], 1)

            def product(p, u):
                n, j = u // DT, u % DT
                dve.wait_ge(S["scan_done"], p * UNITS + u + 1)
                if j == 0:
                    dve.wait_ge(S["c_done"], p * NS + n + 1)
                if late(p) or u >= PRODS:
                    dve.wait_ge(S["acc_done"], p * UNITS + u + 1 - PRODS)
                nc.vector.tensor_tensor(prod[u % PRODS][:, :], hid[u % HIDS][:, :], c_ps[n % 2][:, 0:W], ALU.mult)\
                    .then_inc(S["prod_done"], 1)

            def skip_path(p, q, j):
                dve.wait_ge(S["acc_done"], p * UNITS + UNITS - DT + j + 1)
                if j == 0 and late(p):
                    dve.wait_ge(S["yg_done"], p * DT)
                nc.vector.scalar_tensor_tensor(out=yd[:, j, :], in0=xz[q][:, j, :], scalar=d_skip[:, j:j + 1],
                                               in1=y_ps[j][:, 0:W], op0=ALU.mult, op1=ALU.add)\
                    .then_inc(S["yd_done"], 1)

            def end(p, i):
                if i == 0:
                    dve.wait_ge(S["mo_out"], p * 2 + 2)
                    dve.wait_ge(S["xn_loaded"], p * 16 + 16)
                    if late(p):
                        dve.wait_ge(S["norm"], p * 4)
                    nc.vector.tensor_tensor(hs[:, :, :], mo[:, :, :], xn[:, :, :], ALU.add).then_inc(S["res"], 1)
                elif i == 1:
                    dve.wait_ge(S["res"], p + 1)
                    for t in range(4):
                        nc.vector.bn_stats(st[:, t, :], hs[:, t, :]).then_inc(S["stats"], 1)
                elif i == 2:
                    dve.wait_ge(S["stats"], p * 9 + 4)
                    dve.sem_inc(S["fence"], 1)
                    for t in range(4):
                        nc.vector.bn_aggr(mv[:, t, :], st[:, t, :]).then_inc(S["stats"], 1)
                elif i == 3:
                    dve.wait_ge(S["stats"], p * 9 + 8)
                    if late(p):
                        dve.wait_ge(S["rs_ready"], p)
                    nc.vector.tensor_scalar(ve[:, :], mv[:, :, 1], LN_EPS, None, ALU.add).then_inc(S["stats"], 1)
                else:
                    dve.wait_ge(S["rs_ready"], p + 1)
                    if late(p):
                        dve.wait_ge(S["affine"], p * 3)
                    for t in range(4):
                        nc.vector.tensor_scalar(hn[:, t, :], hs[:, t, :], mv[:, t, 0:1], rs[:, t:t + 1],
                                                ALU.subtract, ALU.mult).then_inc(S["norm"], 1)

            def softplus(p, q, i):
                if i == 0:
                    dve.wait_ge(S["dt_act"], p * 3 + 2)
                    nc.vector.scalar_tensor_tensor(out=lost[:, :, :], in0=onep[:, :, :], scalar=1.0, in1=expd[:, :, :],
                                                   op0=ALU.subtract, op1=ALU.subtract).then_inc(S["dt_ready"], 1)
                elif i == 1:
                    dve.wait_ge(S["dt_act"], p * 3 + 3)
                    dve.wait_ge(S["dt_relu"], p * 3 + 3)
                    nc.vector.tensor_tensor(sumd[:, :, :], relud[:, :, :], logd[:, :, :], ALU.add).then_inc(S["dt_ready"], 1)
                elif i == 2:
                    dve.wait_ge(S["dt_ready"], p * 3 + 2)
                    if type(p) is not int or p >= 2:
                        dve.wait_ge(S["exp_done"], p * UNITS - UNITS)
                    nc.vector.tensor_tensor(dt[q][:, :, :], sumd[:, :, :], lost[:, :, :], ALU.subtract)\
                        .then_inc(S["dt_ready"], 1)
                else:
                    dve.wait_ge(S["dt_ready"], p * 3 + 3)
                    dve.wait_ge(S["silu"], p + 1)
                    if type(p) is not int or p >= 2:
                        dve.wait_ge(S["dbx_done"], p * UNITS - UNITS)
                    nc.vector.tensor_tensor(dtx[q][:, :, :], dt[q][:, :, :], xz[q][:, 0:DT, :], ALU.mult)\
                        .then_inc(S["dtx_ready"], 1)

            def body(k, q, last, now, nxt):
                for u in range(UNITS):
                    if now:
                        scan(k, u)
                        if u > 0:
                            product(k, u - 1)
                    if last and u in DVE_SKIP:
                        skip_path(k - 1, 1 - q, DVE_SKIP.index(u))
                    if last and u in DVE_END:
                        end(k - 1, DVE_END.index(u))
                    if nxt and u in DVE_SOFTPLUS:
                        softplus(k + 1, 1 - q, DVE_SOFTPLUS.index(u))
                if now:
                    product(k, UNITS - 1)

            run(dve, body)


def mix_slots(nc, t_in, h_in, out, pairs):
    stages = 6
    assert pairs % 2 == 0 and pairs >= stages
    W = 2 * L
    with ExitStack() as ctx:
        def sb(name, shape, dt=F32):
            return ctx.enter_context(nc.sbuf_tensor(name, shape, dt))

        def sem(name):
            return ctx.enter_context(nc.semaphore(name))

        def bank(name):
            return ctx.enter_context(nc.psum_tensor(name, [P, 512], F32))

        ident = sb("c_ident", [P, P])
        slot_raw = sb("c_slot_raw", [P, 2, SLOTS])
        slot_sq = sb("c_slot_sq", [P, 2, SLOTS])
        slot_sum = sb("c_slot_sum", [P, 2, NP_])
        slot_norm = sb("c_slot_norm", [P, 2, NP_])
        scale = sb("c_scale", [P, 1])
        slots = sb("c_slots", [P, 2, SLOTS])
        w_down = sb("c_w_down", [P, 2, 2, P])
        b_down = sb("c_b_down", [P, 2])
        w_up = sb("c_w_up", [P, 2, D])
        b_up = sb("c_b_up", [SLOTS, D])
        own = sb("c_own", [P, 2, SLOTS])
        minus_half = sb("c_minus_half", [TT, 4])
        plus_half = sb("c_plus_half", [P, 2, NP_])
        minus_one = sb("c_minus_one", [P, 2, NP_])

        h = [sb(f"c_h{q}", [TT, 4, D]) for q in range(2)]
        st = sb("c_st", [TT, 4, 6])
        mv = sb("c_mv", [TT, 4, 2])
        sm = [sb(f"c_sm{i}", [TT, 4]) for i in range(9)]
        xn = [sb(f"c_xn{q}", [TT, 4, D]) for q in range(2)]
        xt = [sb(f"c_xt{q}", [P, 2, W]) for q in range(2)]
        mx_d = sb("c_mx_d", [SLOTS, 2])
        e_d = sb("c_e_d", [SLOTS, 2, L])
        sum_d = sb("c_sum_d", [SLOTS, 2])
        inv_d = sb("c_inv_d", [SLOTS, 2])
        p_d = sb("c_p_d", [SLOTS, 2, L])
        mx_c = sb("c_mx_c", [TT, 4])
        l_c = sb("c_l_c", [TT, 4, SLOTS])
        e_c = sb("c_e_c", [TT, 4, SLOTS])
        sum_c = sb("c_sum_c", [TT, 4])
        inv_c = sb("c_inv_c", [TT, 4])
        p_c = sb("c_p_c", [TT, 4, SLOTS])
        dm = sb("c_dm", [TT, 4, SLOTS])
        ct = [sb(f"c_ct{q}", [SLOTS, 4, TT]) for q in range(2)]
        xs = sb("c_xs", [P, 2, 2 * SLOTS])
        hid = sb("c_hid", [P, 2, 2 * SLOTS])
        own_hid = sb("c_own_hid", [P, 2, 2 * SLOTS])
        ys = sb("c_ys", [SLOTS, 2, D])
        h_again = sb("c_h_again", [TT, 4, D])
        res = sb("c_res", [TT, 4, D])

        tr_ps = bank("c_tr_ps")
        lg_ps = bank("c_lg_ps")
        lt_ps = bank("c_lt_ps")
        xs_ps = bank("c_xs_ps")
        hid_ps = bank("c_hid_ps")
        ys_ps = bank("c_ys_ps")
        out_ps = [bank("c_out_ps0"), bank("c_out_ps1")]

        S = {n: sem("c_" + n) for n in (
            "fence", "weights", "consts", "slot_steps", "slots_ready",
            "h_loaded0", "h_loaded1", "h_again_loaded", "stats", "steps", "norm", "tr_done", "xt_out",
            "lg_done", "lt_done", "mx", "e_d", "d_steps", "c_steps", "e_c", "dm_done", "dm_out", "ct_done", "ct_out",
            "xs_done", "xs_out", "hid_done", "hid_out", "masked", "ys_done", "ys_out", "out_done", "summed", "stored")}
        loads = [(ident, "ident"), (slot_raw, "slots"), (scale, "scale"), (w_down, "w_down"), (b_down, "b_down"),
                 (w_up, "w_up"), (b_up, "b_up"), (own, "own")]

        def run(eng, body):
            def peeled(k):
                body(k, k // 2, k % 2, [0 <= k - stage < pairs for stage in range(stages)])

            for k in range(stages):
                peeled(k)
            with eng.Fori(stages // 2, pairs // 2) as m:
                body(m * 2, m, 0, [True] * stages)
                body(m * 2 + 1, m, 1, [True] * stages)
            for k in range(pairs, pairs + stages - 1):
                peeled(k)

        def late(p, n=1):
            return not (type(p) is int and p < n)

        block = ctx.enter_context(nc.Block())

        @block.sync
        def _(sp):
            for dst, name in loads:
                sp.dma_start(dst[:], t_in[name]).then_inc(S["weights"], 16)

            def body(k, m, q, on):
                if on[0]:
                    if late(k, 2):
                        sp.wait_ge(S["norm"], k * 4 - 4)
                    sp.dma_start(h[q][:], h_in[k]).then_inc(S[f"h_loaded{q}"], 16)
                if on[5]:
                    p = k - 5
                    sp.wait_ge(S["summed"], p * 2 + 2)
                    sp.dma_start(out[p], res[:]).then_inc(S["stored"], 16)
                if on[4]:
                    p = k - 4
                    if late(p):
                        sp.wait_ge(S["summed"], p * 2)
                    sp.dma_start(h_again[:], h_in[p]).then_inc(S["h_again_loaded"], 16)

            run(sp, body)
            sp.wait_ge(S["stored"], 16 * pairs)

        @block.tensor
        def _(pe):
            pe.wait_ge(S["weights"], 16 * len(loads))
            pe.wait_ge(S["slots_ready"], 2)

            def body(k, m, q, on):
                if on[3]:
                    p = k - 3
                    pe.wait_ge(S["d_steps"], p * 4 + 4)
                    pe.sem_inc(S["fence"], 1)
                    for i in range(4):
                        rows, lo = (HALF, 0) if i % 2 == 0 else (TT, HALF)
                        mm = pe.transpose(lt_ps[0:rows, i * SLOTS:(i + 1) * SLOTS], p_d[:, i // 2, lo:lo + rows],
                                          ident[0:SLOTS, 0:SLOTS])
                    mm.then_inc(S["dm_done"], 1)
                    pe.wait_ge(S["c_steps"], p * 4 + 4)
                    for i in range(4):
                        mm = pe.transpose(lg_ps[0:SLOTS, i * TT:(i + 1) * TT], p_c[:, i, :], ident[0:TT, 0:TT])
                    mm.then_inc(S["ct_done"], 1)
                if on[4]:
                    p = k - 4
                    pe.wait_ge(S["xs_out"], p + 1)
                    if late(p):
                        pe.wait_ge(S["hid_out"], p * 2)
                    for t in range(2):
                        for part in range(2):
                            mm = pe.matmul(hid_ps[:, t * 2 * SLOTS:(t + 1) * 2 * SLOTS], w_down[:, part, t, :],
                                           xs[:, part, :], start=(part == 0), stop=(part == 1))
                    mm.then_inc(S["hid_done"], 1)
                if on[3]:
                    p = k - 3
                    pe.wait_ge(S["dm_out"], p * 2 + 2)
                    if late(p):
                        pe.wait_ge(S["xs_out"], p)
                    for part in range(2):
                        for img in range(2):
                            o = xs_ps[:, (part * 2 + img) * SLOTS:(part * 2 + img + 1) * SLOTS]
                            for half, rows in ((0, HALF), (1, TT)):
                                mm = pe.matmul(o, xn[1 - q][0:rows, 2 * img + half, part * HI:part * HI + P],
                                               dm[0:rows, 2 * img + half, :], start=(half == 0), stop=(half == 1))
                    mm.then_inc(S["xs_done"], 1)
                if on[2]:
                    p = k - 2
                    pe.wait_ge(S["xt_out"], p * 2 + 2)
                    if late(p):
                        pe.wait_ge(S["ct_out"], p)
                        pe.wait_ge(S["dm_out"], p * 2)
                    for i in range(4):
                        lo = (i // 2) * L + (i % 2) * HALF
                        for part in range(2):
                            mm = pe.matmul(lg_ps[0:TT, i * SLOTS:(i + 1) * SLOTS], xt[q][:, part, lo:lo + TT],
                                           slots[:, part, :], start=(part == 0), stop=(part == 1))
                    mm.then_inc(S["lg_done"], 1)
                    for part in range(2):
                        mm = pe.matmul(lt_ps[0:SLOTS, 0:W], slots[:, part, :], xt[q][:, part, :],
                                       start=(part == 0), stop=(part == 1))
                    mm.then_inc(S["lt_done"], 1)
                if on[4]:
                    p = k - 4
                    pe.wait_ge(S["masked"], p + 1)
                    if late(p):
                        pe.wait_ge(S["ys_out"], p)
                    for img in range(2):
                        for t in range(2):
                            mm = pe.matmul(ys_ps[0:SLOTS, img * D:(img + 1) * D],
                                           own_hid[:, t, img * SLOTS:(img + 1) * SLOTS], w_up[:, t, :],
                                           start=(t == 0), stop=(t == 1))
                    mm.then_inc(S["ys_done"], 1)
                if on[1]:
                    p = k - 1
                    pe.wait_ge(S["norm"], p * 4 + 4)
                    for part in range(2):
                        if late(p) or part == 1:
                            pe.wait_ge(S["xt_out"], p * 2 + part)
                        for i in range(4):
                            lo = (i // 2) * L + (i % 2) * HALF
                            mm = pe.transpose(tr_ps[:, lo:lo + TT], xn[1 - q][:, i, part * HI:part * HI + P], ident[0:TT, 0:TT])
                        mm.then_inc(S["tr_done"], 1)
                if on[4]:
                    p = k - 4
                    pe.wait_ge(S["ys_out"], p + 1)
                    if late(p):
                        pe.wait_ge(S["summed"], p * 2)
                    for img in range(2):
                        for half in range(2):
                            mm = pe.matmul(out_ps[img][0:TT, half * D:(half + 1) * D], ct[q][:, 2 * img + half, :],
                                           ys[:, img, :], start=True, stop=True)
                        mm.then_inc(S["out_done"], 1)

            run(pe, body)

        @block.scalar
        def _(act):
            act.wait_ge(S["weights"], 16 * len(loads))
            nc.scalar.activation(slot_sq[:, :, :], slot_raw[:, :, :], ACT.Square).then_inc(S["slot_steps"], 1)

            def body(k, m, q, on):
                if on[3]:
                    p = k - 3
                    act.wait_ge(S["dm_done"], p + 1)
                    if late(p):
                        act.wait_ge(S["xs_done"], p)
                    for half, rows in ((0, HALF), (1, TT)):
                        nc.scalar.copy(dm[0:rows, half::2, :], lt_ps[0:rows, 0:4 * SLOTS].rearrange(
                            "p (i s) -> p i s", i=4)[:, half::2, :]).then_inc(S["dm_out"], 1)
                    act.wait_ge(S["ct_done"], p + 1)
                    if late(p, 2):
                        act.wait_ge(S["out_done"], p * 2 - 2)
                    nc.scalar.copy(ct[1 - q][:, :, :], lg_ps[0:SLOTS, 0:4 * TT].rearrange("p (i t) -> p i t", i=4))\
                        .then_inc(S["ct_out"], 1)
                if on[4]:
                    p = k - 4
                    act.wait_ge(S["hid_done"], p + 1)
                    if late(p):
                        act.wait_ge(S["masked"], p)
                    for t in range(2):
                        nc.scalar.activation(hid[:, t, :], hid_ps[:, t * 2 * SLOTS:(t + 1) * 2 * SLOTS], ACT.Gelu,
                                             bias=b_down[:, t:t + 1]).then_inc(S["hid_out"], 1)
                if on[3]:
                    p = k - 3
                    act.wait_ge(S["xs_done"], p + 1)
                    if late(p):
                        act.wait_ge(S["hid_done"], p)
                    nc.scalar.copy(xs[:, :, :], xs_ps[:, 0:4 * SLOTS].rearrange("p (a s) -> p a s", a=2))\
                        .then_inc(S["xs_out"], 1)
                if on[2]:
                    p = k - 2
                    act.wait_ge(S["mx"], p * 2 + 1)
                    if late(p):
                        act.wait_ge(S["d_steps"], p * 4)
                    for img in range(2):
                        nc.scalar.activation(e_d[:, img, :], lt_ps[0:SLOTS, img * L:(img + 1) * L], ACT.Exp,
                                             bias=mx_d[:, img:img + 1]).then_inc(S["e_d"], 1)
                    act.wait_ge(S["c_steps"], p * 4 + 1)
                    nc.scalar.activation(e_c[:, :, :], l_c[:, :, :], ACT.Exp).then_inc(S["e_c"], 1)
                if on[1]:
                    p = k - 1
                    for part in range(2):
                        act.wait_ge(S["tr_done"], p * 2 + part + 1)
                        if part == 0 and late(p, 2):
                            act.wait_ge(S["lt_done"], p - 1)
                        nc.scalar.copy(xt[1 - q][:, part, :], tr_ps[:, 0:W]).then_inc(S["xt_out"], 1)

            run(act, body)

        @block.gpsimd
        def _(pool):
            nc.gpsimd.memset(minus_half[:], -0.5).then_inc(S["consts"], 1)
            nc.gpsimd.memset(plus_half[:], 0.5).then_inc(S["consts"], 1)
            nc.gpsimd.memset(minus_one[:], -1.0).then_inc(S["consts"], 1)
            pool.wait_ge(S["consts"], 3)
            pool.wait_ge(S["slot_steps"], 2)
            nc.gpsimd.tensor_tensor(slot_norm[:, :, :], slot_sum[:, :, :], plus_half[:, :, :], ALU.pow).then_inc(S["slot_steps"], 1)
            pool.wait_ge(S["slot_steps"], 3)
            nc.gpsimd.tensor_scalar(slot_sum[:, :, :], slot_norm[:, :, :], L2_EPS, None, ALU.add).then_inc(S["slot_steps"], 1)
            pool.wait_ge(S["slot_steps"], 4)
            nc.gpsimd.tensor_tensor(slot_norm[:, :, :], slot_sum[:, :, :], minus_one[:, :, :], ALU.pow).then_inc(S["slot_steps"], 1)

            def body(k, m, q, on):
                if on[4]:
                    p = k - 4
                    pool.wait_ge(S["hid_out"], p * 2 + 2)
                    if late(p):
                        pool.wait_ge(S["ys_done"], p)
                    nc.gpsimd.tensor_tensor(own_hid[:, :, :].rearrange("p m (i s) -> p m i s", i=2),
                                            hid[:, :, :].rearrange("p m (i s) -> p m i s", i=2),
                                            own[:, :, :].unsqueeze(2).broadcast_to([P, 2, 2, SLOTS]), ALU.mult)\
                        .then_inc(S["masked"], 1)
                if on[0]:
                    v = [x[:, :] for x in sm]
                    pool.wait_ge(S["stats"], k * 10 + 10)
                    if late(k):
                        pool.wait_ge(S["norm"], k * 4)
                    nc.gpsimd.tensor_tensor(v[2], v[0], minus_half[:, :], ALU.pow).then_inc(S["steps"], 1)
                    pool.wait_ge(S["steps"], k * 7 + 1)
                    nc.gpsimd.tensor_tensor(v[3], v[2], v[2], ALU.mult).then_inc(S["steps"], 1)
                    pool.wait_ge(S["steps"], k * 7 + 2)
                    nc.gpsimd.tensor_tensor(v[4], v[3], v[1], ALU.mult).then_inc(S["steps"], 1)
                    pool.wait_ge(S["steps"], k * 7 + 3)
                    nc.gpsimd.tensor_tensor(v[5], v[4], plus_half[0:TT, 0, :], ALU.pow).then_inc(S["steps"], 1)
                    pool.wait_ge(S["steps"], k * 7 + 4)
                    pool.sem_inc(S["fence"], 1)
                    nc.gpsimd.tensor_scalar(v[6], v[5], L2_EPS, None, ALU.add).then_inc(S["steps"], 1)
                    pool.wait_ge(S["steps"], k * 7 + 5)
                    nc.gpsimd.tensor_tensor(v[7], v[6], minus_one[0:TT, 0, :], ALU.pow).then_inc(S["steps"], 1)
                    pool.wait_ge(S["steps"], k * 7 + 6)
                    nc.gpsimd.tensor_tensor(v[8], v[7], v[2], ALU.mult).then_inc(S["steps"], 1)

            run(pool, body)

        @block.vector
        def _(dve):
            dve.wait_ge(S["weights"], 16 * len(loads))
            dve.wait_ge(S["slot_steps"], 1)
            nc.vector.tensor_reduce(slot_sum[:, :, :], slot_sq[:, :, :].rearrange("p a (n s) -> p a s n", s=NP_), AX_X,
                                    ALU.add).then_inc(S["slot_steps"], 1)
            dve.wait_ge(S["slot_steps"], 5)
            for part in range(2):
                nc.vector.scalar_tensor_tensor(out=slots[:, part, :].rearrange("p (n s) -> p n s", s=NP_),
                                               in0=slot_raw[:, part, :].rearrange("p (n s) -> p n s", s=NP_),
                                               scalar=scale[:, 0:1],
                                               in1=slot_norm[:, part, :].unsqueeze(1).broadcast_to([P, NE, NP_]),
                                               op0=ALU.mult, op1=ALU.mult).then_inc(S["slots_ready"], 1)

            def body(k, m, q, on):
                if on[1]:
                    p = k - 1
                    dve.wait_ge(S["steps"], p * 7 + 7)
                    if late(p, 2):
                        dve.wait_ge(S["xs_done"], p - 1)
                        dve.wait_ge(S["tr_done"], p * 2 - 2)
                    for i in range(4):
                        nc.vector.tensor_scalar(xn[1 - q][:, i, :], h[1 - q][:, i, :], mv[:, i, 0:1], sm[8][:, i:i + 1],
                                                ALU.subtract, ALU.mult).then_inc(S["norm"], 1)
                if on[0]:
                    dve.wait_ge(S[f"h_loaded{q}"], m * 16 + 16)
                    if late(k):
                        dve.wait_ge(S["norm"], k * 4)
                        dve.wait_ge(S["steps"], k * 7)
                    for i in range(4):
                        nc.vector.bn_stats(st[:, i, :], h[q][:, i, :]).then_inc(S["stats"], 1)
                if on[2]:
                    p = k - 2
                    dve.wait_ge(S["lt_done"], p + 1)
                    if late(p):
                        dve.wait_ge(S["e_d"], p * 2)
                    nc.vector.tensor_reduce(mx_d[:, :], lt_ps[0:SLOTS, 0:W].rearrange("p (i l) -> p i l", i=2), AX_X,
                                            ALU.max, negate=True).then_inc(S["mx"], 1)
                    if late(p):
                        dve.wait_ge(S["c_steps"], p * 4)
                    lg = lg_ps[0:TT, 0:4 * SLOTS].rearrange("p (i s) -> p i s", i=4)
                    nc.vector.tensor_reduce(mx_c[:, :], lg, AX_X, ALU.max).then_inc(S["mx"], 1)
                    dve.wait_ge(S["mx"], p * 2 + 2)
                    if late(p):
                        dve.wait_ge(S["e_c"], p)
                    nc.vector.tensor_tensor(l_c[:, :, :], lg, mx_c[:, :].unsqueeze(2).broadcast_to([TT, 4, SLOTS]),
                                            ALU.subtract).then_inc(S["c_steps"], 1)
                if on[0]:
                    for i in range(4):
                        dve.wait_ge(S["stats"], k * 10 + i + 1)
                        dve.sem_inc(S["fence"], 1)
                        nc.vector.bn_aggr(mv[:, i, :], st[:, i, :]).then_inc(S["stats"], 1)
                    dve.wait_ge(S["stats"], k * 10 + 8)
                    nc.vector.tensor_scalar(sm[0][:, :], mv[:, :, 1], LN_EPS, None, ALU.add).then_inc(S["stats"], 1)
                    nc.vector.tensor_scalar(sm[1][:, :], mv[:, :, 1], float(D), None, ALU.mult).then_inc(S["stats"], 1)
                if on[4]:
                    p = k - 4
                    dve.wait_ge(S["ys_done"], p + 1)
                    if late(p):
                        dve.wait_ge(S["out_done"], p * 2)
                    nc.vector.tensor_tensor(ys[:, :, :], ys_ps[0:SLOTS, 0:2 * D].rearrange("p (i d) -> p i d", i=2),
                                            b_up[:, :].unsqueeze(1).broadcast_to([SLOTS, 2, D]), ALU.add)\
                        .then_inc(S["ys_out"], 1)
                if on[2]:
                    p = k - 2
                    dve.wait_ge(S["e_d"], p * 2 + 2)
                    nc.vector.tensor_reduce(sum_d[:, :], e_d[:, :, :], AX_X, ALU.add).then_inc(S["d_steps"], 1)
                    dve.wait_ge(S["d_steps"], p * 4 + 1)
                    nc.vector.reciprocal(inv_d[:, :], sum_d[:, :]).then_inc(S["d_steps"], 1)
                    dve.wait_ge(S["d_steps"], p * 4 + 2)
                    if late(p):
                        dve.wait_ge(S["dm_done"], p)
                    for img in range(2):
                        nc.vector.tensor_scalar(p_d[:, img, :], e_d[:, img, :], inv_d[:, img:img + 1], None,
                                                ALU.mult).then_inc(S["d_steps"], 1)
                    dve.wait_ge(S["e_c"], p + 1)
                    nc.vector.tensor_reduce(sum_c[:, :], e_c[:, :, :], AX_X, ALU.add).then_inc(S["c_steps"], 1)
                    dve.wait_ge(S["c_steps"], p * 4 + 2)
                    nc.vector.reciprocal(inv_c[:, :], sum_c[:, :]).then_inc(S["c_steps"], 1)
                    dve.wait_ge(S["c_steps"], p * 4 + 3)
                    if late(p):
                        dve.wait_ge(S["ct_done"], p)
                    nc.vector.tensor_tensor(p_c[:, :, :], e_c[:, :, :], inv_c[:, :].unsqueeze(2).broadcast_to([TT, 4, SLOTS]),
                                            ALU.mult).then_inc(S["c_steps"], 1)
                if on[4]:
                    p = k - 4
                    dve.wait_ge(S["h_again_loaded"], p * 16 + 16)
                    if late(p):
                        dve.wait_ge(S["stored"], p * 16)
                    for img in range(2):
                        dve.wait_ge(S["out_done"], p * 2 + img + 1)
                        nc.vector.tensor_tensor(res[:, 2 * img:2 * img + 2, :],
                                                out_ps[img][0:TT, 0:2 * D].rearrange("p (i d) -> p i d", i=2),
                                                h_again[:, 2 * img:2 * img + 2, :], ALU.add).then_inc(S["summed"], 1)

            run(dve, body)


def pointwise_tiles(w, mode):
    wt = np.ascontiguousarray(w.reshape(D, D).T)
    o = np.zeros((P, 6, P), wt.dtype)
    if mode == "one":
        o[:, 0] = wt[:P, :P]
        for i in range(2):
            o[HI * i:HI * i + HI, 1 + i] = wt[P:, :P]
            o[:, 3 + i, HI * i:HI * i + HI] = wt[:P, P:]
            o[HI * i:HI * i + HI, 5, HI * i:HI * i + HI] = wt[P:, P:]
    else:
        r = 0 if mode == "loc" else HI
        o[:, 0] = wt[:P, :P]
        o[r:r + HI, 1] = wt[P:, :P]
        for i in range(2):
            o[:, 2 + 2 * i, HI * i:HI * i + HI] = wt[:P, P:]
            o[r:r + HI, 3 + 2 * i, HI * i:HI * i + HI] = wt[P:, P:]
    return o


def low_high(v):
    return np.stack([v[:P], np.concatenate([v[P:], v[P:]])], 1)


def haar_bands():
    bands = np.zeros((256, 256), np.float32)
    for b in range(256):
        for i in range(16):
            for j in range(16):
                odd = 0
                for level in range(4):
                    digit = (b >> (2 * (3 - level))) & 3
                    odd ^= (digit >> 1) & (j >> level) & 1
                    odd ^= digit & (i >> level) & 1
                bands[b, i * 16 + j] = -0.0625 if odd else 0.0625
    return bands


def host_inputs(i, pairs):
    f = {}
    x = i["x"][:2 * pairs].reshape(pairs, 2, 3, G, 16, G, 16)
    x = x.transpose(0, 2, 4, 6, 1, 3, 5).reshape(pairs, KT, P, 2 * PX)
    f["x_t"] = x.transpose(0, 2, 1, 3)
    t = {k[7:]: v for k, v in i.items() if k.startswith("L0_tok_")}
    f["ident"] = np.eye(P, dtype=np.float32)
    f["haar"] = haar_bands().reshape(2, P, 256).transpose(1, 0, 2)
    f["w_wave"] = t["pg_w1"].reshape(D, 2, P, 3).transpose(2, 1, 3, 0)
    f["w_loc"] = t["pl_w"].reshape(D, KT, P).transpose(2, 1, 0)
    f["conv_bias"] = np.stack([t["pl_b"][:P], t["pg_b1"][:P], np.concatenate([t["pl_b"][P:], t["pg_b1"][P:]])], 1)
    dw = [t[n].reshape(D, TAPS) for n in ("pl_dw", "pg_dw", "f1_dw", "f2_dw", "f3_dw")]
    tiles = [dw[0][:P], dw[1][:P], np.concatenate([dw[0][P:], dw[1][P:]])]
    for w in dw[2:]:
        tiles += [w[:P], np.concatenate([w[P:], w[P:]])]
    f["dw_w"] = np.stack(tiles, 1)
    f["pw_loc"] = pointwise_tiles(t["pl_pw"], "loc")
    f["pw_glob"] = pointwise_tiles(t["pg_pw"], "glob")
    f["pw_glob2"] = pointwise_tiles(t["pg_w2"], "one")
    f["pw_fuse1"] = pointwise_tiles(t["f1_pw"], "one")
    f["pw_fuse2"] = pointwise_tiles(t["f2_pw"], "one")
    biases = np.stack([t[n] for n in ("pl_pwb", "pg_pwb", "pg_b2", "f1_pwb", "f2_pwb")], 1)
    f["pw_bias"] = low_high(biases).transpose(0, 2, 1)
    w3 = t["f3_pw"].reshape(D, D).T
    f["pw3"] = np.zeros((P, 3, D), np.float32)
    f["pw3"][:, 0] = w3[:P]
    for n in range(2):
        f["pw3"][HI * n:HI * n + HI, 1 + n] = w3[P:]
    f["bias3"] = np.zeros((P, D), np.float32)
    f["bias3"][0] = t["f3_pwb"]
    f["row0"] = np.zeros((P, TT), np.float32)
    f["row0"][0] = 1.0
    f["alpha"] = low_high(t["alpha"].reshape(D, 1))[:, :, 0]
    f["ln_g"] = np.broadcast_to(t["ln_g"], (TT, D))
    f["ln_b"] = np.broadcast_to(t["ln_b"], (TT, D))
    f["cls"] = t["cls"].reshape(1, D)
    a = {k[8:]: v for k, v in i.items() if k.startswith("L0_attn_")}

    def high_part(w):
        o = w[HI:].copy()
        o[:HI] = 0.0
        return o

    f["w_in"] = np.stack([a["W_in"][:P], high_part(a["W_in"])], 1).reshape(P, 2, 2 * DT, P)
    wx = a["W_x"].reshape(DT, P, RANK + 2 * NS).transpose(1, 0, 2)
    f["w_x"] = np.zeros((P, DT, P), np.float32)
    f["w_x"][:, :, :RANK] = wx[:, :, :RANK]
    f["w_bc"] = np.concatenate([wx[:, :, RANK:]] * 3, 2)
    f["w_dt"] = np.zeros((P, DT, P), np.float32)
    f["w_dt"][:RANK] = a["W_dt"].reshape(RANK, DT, P)
    f["b_dt"] = a["b_dt"].reshape(DT, P).T
    f["a_log"] = a["A_log"].reshape(DT, P, NS).transpose(1, 0, 2)
    f["d_skip"] = a["D_skip"].reshape(DT, P).T
    f["w_out"] = a["W_out"].reshape(DT, P, D).transpose(1, 0, 2)
    f["gamma"] = np.broadcast_to(a["gamma"], (TT, D))
    f["beta"] = np.broadcast_to(a["beta"], (TT, D))
    pick = np.zeros((96, 2 * NS, P), np.float32)
    for row in range(96):
        pick[row, row % (2 * NS)] = 1.0
    f["pick"] = pick
    s = {k[7:]: v for k, v in i.items() if k.startswith("L0_ffn_")}
    raw = s["slot_params"].reshape(D, SLOTS)
    f["slots"] = np.stack([raw[:P], high_part(raw)], 1)
    f["scale"] = np.broadcast_to(s["scale"].reshape(1, 1), (P, 1))
    down = s["W_down"].transpose(1, 0, 2).reshape(D, D)
    down = np.stack([down[:, :P], down[:, HI:]], 1).reshape(D, 2 * P)
    f["w_down"] = np.stack([down[:P], high_part(down)], 1).reshape(P, 2, 2, P)
    b = s["b_down"].reshape(D)
    f["b_down"] = np.stack([b[:P], b[HI:]], 1)
    up = s["W_up"].reshape(D, D)
    f["w_up"] = np.stack([up[:P], high_part(up)], 1)
    f["b_up"] = np.repeat(s["b_up"], NP_, 0)
    own = np.zeros((D, SLOTS), np.float32)
    for e in range(NE):
        own[e * HID:(e + 1) * HID, e * NP_:(e + 1) * NP_] = 1.0
    f["own"] = np.stack([own[:P], own[HI:]], 1)
    return {name: np.ascontiguousarray(v) for name, v in f.items()}


def kernel(**inputs):
    import concourse.bacc as bacc
    from concourse.bass_utils import run_bass_kernel_spmd

    given = {name: np.asarray(v) for name, v in inputs.items()}
    images = given["x"].shape[0]
    pairs = images // 2
    arrays = host_inputs(given, pairs)
    nc = bacc.Bacc("TRN2", target_bir_lowering=False, num_devices=1)
    t_in = {name: nc.dram_tensor("in_" + name, v.shape, mybir.dt.from_np(v.dtype), kind="ExternalInput").ap()
            for name, v in arrays.items()}
    out = nc.dram_tensor("out_tokens", (pairs, TT, 4, D), F32, kind="ExternalOutput").ap()
    bass_vit_tower(nc, t_in, out, pairs)
    got = run_bass_kernel_spmd(nc, [{"in_" + name: v for name, v in arrays.items()}], core_ids=[0])
    tiles = np.asarray(got.results[0]["out_tokens"]).reshape(pairs, TT, 2, 2, D).transpose(0, 2, 3, 1, 4)
    return np.concatenate([tiles[:, :, 0, :HALF], tiles[:, :, 1]], 2).reshape(images, L, D)
```

```python
from contextlib import ExitStack

import numpy as np
import concourse.bass as bass
from concourse import mybir
from concourse.alu_op_type import AluOpType as ALU

F32 = mybir.dt.float32
BF16 = mybir.dt.bfloat16
ACT = mybir.ActivationFunctionType
AX_X = mybir.AxisListType.X

P = 128
D = 192
HI = D - P
G = 14
PX = G * G
L = PX + 1
TT = 99
HALF = L - TT
KT = 6
PAD = 16
ROWS2 = 2 * (G + 1) + 1
SPAN2 = (2 * G + 1) * G
IMG2 = (G + 1) * G
TAPS = 9
LN_EPS = 1e-5
L2_EPS = 1e-6
DI = 384
DT = DI // P
NS = 16
RANK = 48
NE, NP_, HID = 8, 4, 24
SLOTS = NE * NP_


def bass_vit_tower(nc, t_in, out, pairs, pe_taps=1):
    scratch_h = nc.dram_tensor("scratch_h", [pairs, TT, 4, D], F32, kind="Internal").ap()
    scratch_x = nc.dram_tensor("scratch_x", [pairs, TT, 4, D], F32, kind="Internal").ap()
    scratch_xt = nc.dram_tensor("scratch_xt", [pairs, P, 2, 2 * L], F32, kind="Internal").ap()
    scratch_h2 = nc.dram_tensor("scratch_h2", [pairs, TT, 4, D], F32, kind="Internal").ap()
    with ExitStack() as ctx:
        def sb(name, shape, dt=F32):
            return ctx.enter_context(nc.sbuf_tensor(name, shape, dt))

        mixer, slots = token_mixer_weights(sb), slot_mixer_weights(sb)
        mixer_loaded = ctx.enter_context(nc.semaphore("mixer_loaded"))
        slots_loaded = ctx.enter_context(nc.semaphore("slots_loaded"))
        later = [(mixer, mixer_loaded), (slots, slots_loaded)]
        embed_images(nc, t_in, later, scratch_h, scratch_x, scratch_xt, pairs, pe_taps)
        mix_tokens(nc, mixer, mixer_loaded, scratch_h, scratch_x, scratch_xt, scratch_h2, pairs)
        mix_slots(nc, slots, mixer["ident"], slots_loaded, scratch_h2, out, pairs)




def embed_images(nc, t_in, later, h_out, x_out, xt_out, pairs, pe_taps):
    with ExitStack() as ctx:
        def sb(name, shape, dt=F32):
            return ctx.enter_context(nc.sbuf_tensor(name, shape, dt))

        def sem(name):
            return ctx.enter_context(nc.semaphore(name))

        def bank(name):
            return ctx.enter_context(nc.psum_tensor(name, [P, 512], F32))

        ident = sb("a_ident", [P, P])
        haar = sb("a_haar", [P, 2, 256])
        w_wave = sb("a_w_wave", [P, 2, 3, D])
        w_loc = sb("a_w_loc", [P, KT, D])
        w_conv = sb("a_w_conv", [P, KT, 3, P])
        conv_bias = sb("a_conv_bias", [P, 3])
        dw_w = sb("a_dw_w", [P, 9, TAPS])
        dw_diag = sb("a_dw_diag", [P, 9, pe_taps, P])
        pw = {n: sb(f"a_pw_{n}", [P, 6, P]) for n in ("loc", "glob")}
        pw |= {n: sb(f"a_pw_{n}", [P, 6, P]) for n in ("glob2", "fuse1", "fuse2")}
        pw_bias = sb("a_pw_bias", [P, 5, 2])
        pw3 = sb("a_pw3", [P, 3, D])
        bias3 = sb("a_bias3", [P, D])
        row0 = sb("a_row0", [P, TT])
        alpha = sb("a_alpha", [P, 2])
        gate = sb("a_gate", [P, 2])
        one_minus = sb("a_one_minus", [P, 2])
        gate_b = sb("a_gate_b", [P, 2])
        ln_g = sb("a_ln_g", [TT, D])
        ln_b = sb("a_ln_b", [TT, D])
        cls = sb("a_cls", [1, D])
        minus_half = sb("a_minus_half", [TT, 4])
        x_t = sb("a_x_t", [P, KT, 2 * PX])
        pad_first = [sb(f"a_pad_first{t}", [P, ROWS2, PAD]) for t in range(3)]
        acc_first = [sb(f"a_acc_first{t}", [P, 2 * IMG2]) for t in range(3)]
        loc = [sb("a_loc_low", [P, 2 * PX]), sb("a_loc_high", [P, PX])]
        loc_old = [sb("a_loc_old_low", [P, 2 * PX]), sb("a_loc_old_high", [P, PX])]
        gg = [sb("a_gg_low", [P, 2 * PX]), sb("a_gg_high", [P, PX])]
        loc_part = [sb("a_loc_part_low", [P, 2 * PX]), sb("a_loc_part_high", [P, PX])]
        pad = {k: [sb(f"a_pad{k}_low", [P, ROWS2, PAD]), sb(f"a_pad{k}_high", [P, PAD, PAD])] for k in (1, 2, 3)}
        acc = {k: [sb(f"a_acc{k}_low", [P, 2 * IMG2]), sb(f"a_acc{k}_high", [P, PX])] for k in (1, 2)}
        acc[3] = [sb("a_acc3_low", [P, 1 + 2 * IMG2]), sb("a_acc3_high", [P, 1 + PX])]
        products = {n: [[sb(f"a_products{n}_{t}_{k}", [P, SPAN2 if t == 0 else PX]) for k in range(TAPS - pe_taps - 1)]
                        for t in range(2)] for n in ("2", "3")}
        relu2 = [sb("a_relu2_low", [P, 2 * PX]), sb("a_relu2_high", [P, PX])]
        tok = sb("a_tok", [TT, 4, D])
        st1 = sb("a_st1", [TT, 4, 6])
        mv1 = sb("a_mv1", [TT, 4, 2])
        ve1 = sb("a_ve1", [TT, 4])
        rs1 = sb("a_rs1", [TT, 4])
        hn = sb("a_hn", [TT, 4, D])
        hg = sb("a_hg", [TT, 4, D])
        h = sb("a_h", [TT, 4, D])
        st2 = sb("a_st2", [TT, 4, 6])
        mv2 = sb("a_mv2", [TT, 4, 2])
        ve2 = sb("a_ve2", [TT, 4])
        rs2 = sb("a_rs2", [TT, 4])
        xn = sb("a_xn", [TT, 4, D])
        xt = sb("a_xt", [P, 2, 2 * L])

        conv_ps = [bank("a_conv_ps0"), bank("a_conv_ps1")]
        tap_ps = [bank("a_tap_ps0"), bank("a_tap_ps1")]
        pw_ps = [bank("a_pw_ps_low"), bank("a_pw_ps_high")]
        tok_ps = bank("a_tok_ps")
        tr_ps = bank("a_tr_ps")

        S = {n: sem("a_" + n) for n in (
            "fence",
            "conv_weights", "weights", "zeroed", "setup", "fold_done", "fold_copied", "diag", "gate_ready", "gate_act",
            "x_loaded", "conv_done", "gelu_done",
            "taps_first", "first_chain", "first_dw",
            "taps1", "chain1", "dw1", "taps2", "start2", "mul2", "chain2", "dw2",
            "taps3", "start3", "mul3", "chain3", "dw3",
            "pw_loc", "loc_out", "pw_glob", "gg_out", "pw_glob2", "part_out", "fused",
            "pw1", "relu1", "pw2", "relu2", "loc_kept", "joined",
            "tok_done", "tok_copied", "ln1_stats", "ln1_rs", "ln1_norm", "ln1_affine",
            "ln2_stats", "ln2_rs", "ln2_norm", "tr_done", "tr_copied", "h_stored", "x_stored", "xt_stored")}

        def maps(t):
            flat = t[:].rearrange("p r c -> p (r c)")
            return flat[:, 0:2 * (G + 1) * PAD].rearrange("p (i r c) -> p i r c", i=2, r=G + 1)[:, :, 1:G + 1, 1:G + 1]

        def shifted(t, tap, rows):
            dy, dx = tap // 3, tap % 3
            return t[:, dy:dy + rows, dx:dx + G]

        def grid(t, rows, lo=0):
            return t[:, lo:lo + rows * G].rearrange("p (r c) -> p r c", c=G)

        def as_maps(t):
            return t.rearrange("p (i r c) -> p i r c", i=2, r=G)

        layers = {
            "first": (0, pad_first, acc_first, [2 * G + 1] * 3, 0),
            "1": (3, pad[1], acc[1], [2 * G + 1, G], 0),
            "2": (5, pad[2], acc[2], [2 * G + 1, G], 0),
            "3": (7, pad[3], acc[3], [2 * G + 1, G], 1),
        }

        def span_of(t, img, lo=0, n=PX):
            return t[:, lo + img * IMG2:lo + img * IMG2 + n]

        def both(t):
            n = t.shape[1] // 2
            return t[:, 0:2 * n].rearrange("p (i n) -> p i n", i=2)[:, :, 0:PX]

        block = ctx.enter_context(nc.Block())

        conv_loads = [(haar, "haar"), (w_wave, "w_wave"), (w_loc, "w_loc")]
        loads = [(ident, "ident"), (conv_bias, "conv_bias"),
                 (dw_w, "dw_w"), (pw["loc"], "pw_loc"), (pw["glob"], "pw_glob"), (pw["glob2"], "pw_glob2"),
                 (pw["fuse1"], "pw_fuse1"), (pw["fuse2"], "pw_fuse2"), (pw_bias, "pw_bias"), (pw3, "pw3"),
                 (bias3, "bias3"), (row0, "row0"), (alpha, "alpha"), (ln_g, "ln_g"), (ln_b, "ln_b"), (cls, "cls")]
        chain2, chain3 = 2 * (TAPS - pe_taps - 1), 3 * (TAPS - pe_taps - 1)
        first_reads = 7
        stages = 7
        assert pairs > stages

        def run(eng, body):
            for it in range(stages):
                body(it, [0 <= it - s < pairs for s in range(stages)])
            with eng.Fori(stages, pairs) as it:
                body(it, [True] * stages)
            for it in range(pairs, pairs + stages - 1):
                body(it, [0 <= it - s < pairs for s in range(stages)])

        def capped(value, most):
            return min(value, most) if type(value) is int else value

        @block.sync
        def _(sp):
            for dst, name in conv_loads:
                sp.dma_start(dst[:], t_in[name]).then_inc(S["conv_weights"], 16)
            for dst, name in loads:
                sp.dma_start(dst[:], t_in[name]).then_inc(S["weights"], 16)

            def body(it, on):
                if type(it) is int and it == pairs:
                    for weights, loaded in later:
                        for name, dst in weights.items():
                            sp.dma_start(dst[:], t_in[name]).then_inc(loaded, 16)
                if on[0]:
                    if not (type(it) is int and it == 0):
                        sp.wait_ge(S["conv_done"], it * 3)
                    sp.dma_start(x_t[:], t_in["x_t"][it]).then_inc(S["x_loaded"], 16)
                if on[5]:
                    p = it - 5
                    sp.wait_ge(S["ln1_affine"], p * 4 + 4)
                    sp.dma_start(h_out[p], h[:]).then_inc(S["h_stored"], 16)
                if on[6]:
                    p = it - 6
                    sp.wait_ge(S["ln2_norm"], p * 4 + 4)
                    sp.dma_start(x_out[p], xn[:]).then_inc(S["x_stored"], 16)
                    sp.wait_ge(S["tr_copied"], p * 2 + 2)
                    sp.dma_start(xt_out[p], xt[:]).then_inc(S["xt_stored"], 16)

            run(sp, body)
            sp.wait_ge(S["h_stored"], 16 * pairs)
            sp.wait_ge(S["x_stored"], 16 * pairs)
            sp.wait_ge(S["xt_stored"], 16 * pairs)

        @block.tensor
        def _(pe):
            pe.wait_ge(S["conv_weights"], 16 * len(conv_loads))
            for n in range(KT):
                colour, m = n // 2, n % 2
                if n >= 2:
                    pe.wait_ge(S["fold_copied"], 2 * (n - 1))
                for b in range(2):
                    mm = pe.matmul(conv_ps[n % 2][:, 0:D], haar[:, b, m * P:(m + 1) * P], w_wave[:, b, colour, :],
                                   start=(b == 0), stop=(b == 1))
                mm.then_inc(S["fold_done"], 1)
            pe.wait_ge(S["weights"], 16 * len(loads))
            pe.wait_ge(S["fold_copied"], 2 * KT)
            pe.wait_ge(S["setup"], 1)
            pe.wait_ge(S["diag"], 9 * pe_taps)
            pe.wait_ge(S["zeroed"], 1)

            def conv(it, t):
                if t == 0:
                    pe.wait_ge(S["x_loaded"], it * 16 + 16)
                if t == 2:
                    pe.wait_ge(S["gelu_done"], it * 3 + 1)
                elif not (type(it) is int and it == 0):
                    pe.wait_ge(S["gelu_done"], it * 3 if t == 0 else it * 3 - 1)
                for k in range(KT):
                    mm = pe.matmul(conv_ps[t % 2][:, 0:2 * PX], w_conv[:, k, t, :], x_t[:, k, :],
                                   start=(k == 0), stop=(k == KT - 1))
                mm.then_inc(S["conv_done"], 1)

            def taps(name, t):
                first, pads, _, rows, _ = layers[name]
                for k in range(pe_taps):
                    mm = pe.matmul(grid(tap_ps[t % 2], rows[t]), dw_diag[:, first + t, k, :],
                                   shifted(pads[t], k, rows[t]), start=(k == 0), stop=(k == pe_taps - 1))
                mm.then_inc(S["taps_first" if name == "first" else "taps" + name], 1)

            def pointwise_first(w, low, mixed, done):
                pe.matmul(both(pw_ps[0][:, 0:2 * PX]), w[:, 0, :], both(low), start=True, stop=False)
                pe.matmul(both(pw_ps[0][:, 0:2 * PX]), w[:, 1, :], both(mixed), start=False, stop=True).then_inc(done, 1)
                for img in range(2):
                    pe.matmul(pw_ps[1][:, 0:PX], w[:, 2 + 2 * img, :], span_of(low, img), start=(img == 0), stop=False)
                    mm = pe.matmul(pw_ps[1][:, 0:PX], w[:, 3 + 2 * img, :], span_of(mixed, img), start=False, stop=(img == 1))
                mm.then_inc(done, 1)

            def pointwise_one(w, low, high, done):
                pe.matmul(both(pw_ps[0][:, 0:2 * PX]), w[:, 0, :], both(low), start=True, stop=False)
                for img in range(2):
                    mm = pe.matmul(pw_ps[0][:, img * PX:(img + 1) * PX], w[:, 1 + img, :], high[:, :],
                                   start=False, stop=(img == 1))
                mm.then_inc(done, 1)
                for img in range(2):
                    pe.matmul(pw_ps[1][:, 0:PX], w[:, 3 + img, :], both(low)[:, img, :], start=(img == 0), stop=False)
                pe.matmul(pw_ps[1][:, 0:PX], w[:, 5, :], high[:, :], start=False, stop=True).then_inc(done, 1)

            def transposes(p, part):
                pe.wait_ge(S["ln2_norm"], p * 4 + 4)
                if not (type(p) is int and p == 0 and part == 0):
                    pe.wait_ge(S["tr_copied"], p * 2 + part)
                for q in range(4):
                    o = tr_ps[:, (q // 2) * L + (q % 2) * HALF:(q // 2) * L + (q % 2) * HALF + TT]
                    mm = pe.transpose(o, xn[:, q, part * HI:part * HI + P], ident[0:TT, 0:TT])
                mm.then_inc(S["tr_done"], 1)

            def tokens(p, img):
                pe.wait_ge(S["dw3"], p * 2 + 2)
                if not (type(p) is int and p == 0 and img == 0):
                    pe.wait_ge(S["tok_copied"], p * 2 + img)
                for half in range(2):
                    o = tok_ps[0:TT, half * D:(half + 1) * D]
                    lo = img * IMG2 + half * HALF
                    pe.matmul(o, acc[3][0][:, lo:lo + TT], pw3[:, 0, :], start=True, stop=False)
                    pe.matmul(o, acc[3][1][:, half * HALF:half * HALF + TT], pw3[:, 1 + img, :],
                              start=False, stop=False)
                    mm = pe.matmul(o, row0[:, :], bias3[:, :], start=False, stop=True)
                mm.then_inc(S["tok_done"], 1)

            def body(it, on):
                if on[3]:
                    p = it - 3
                    pe.wait_ge(S["joined"], p * 2 + 2)
                    pe.wait_ge(S["first_chain"], capped(it, pairs) * chain3 - chain3 + first_reads)
                    taps("3", 0)
                    taps("3", 1)
                if on[0]:
                    conv(it, 0)
                if on[0]:
                    conv(it, 1)
                if on[1]:
                    p = it - 1
                    pe.wait_ge(S["first_dw"], p * 3 + 3)
                    if on[2]:
                        pe.wait_ge(S["relu1"], p * 2)
                    pointwise_first(pw["loc"], acc_first[0], acc_first[2], S["pw_loc"])
                if on[2]:
                    p = it - 2
                    if on[3]:
                        pe.wait_ge(S["start3"], (it - 3) * 2 + 2)
                    else:
                        pe.wait_ge(S["first_chain"], it * chain3)
                    pe.wait_ge(S["relu1"], p * 2 + 2)
                    taps("2", 0)
                    taps("2", 1)
                if on[1]:
                    p = it - 1
                    pe.wait_ge(S["loc_out"], p * 2 + 2)
                    pointwise_first(pw["glob"], acc_first[1], acc_first[2], S["pw_glob"])
                if on[1]:
                    p = it - 1
                    pe.wait_ge(S["gg_out"], p * 2 + 2)
                    pointwise_one(pw["glob2"], gg[0], gg[1], S["pw_glob2"])
                if on[1]:
                    p = it - 1
                    if on[2]:
                        pe.wait_ge(S["start2"], (it - 2) * 2 + 2)
                    else:
                        pe.wait_ge(S["first_chain"], it * chain3)
                    pe.wait_ge(S["fused"], p * 3 + 3)
                    taps("1", 0)
                    taps("1", 1)
                if on[0]:
                    conv(it, 2)
                if on[0]:
                    if on[1]:
                        pe.wait_ge(S["chain1"], (it - 1) * chain2 + 2)
                    pe.wait_ge(S["gelu_done"], it * 3 + 2)
                    taps("first", 0)
                    taps("first", 1)
                if on[3]:
                    tokens(it - 3, 0)
                if on[0]:
                    pe.wait_ge(S["gelu_done"], it * 3 + 3)
                    pe.wait_ge(S["first_chain"], it * chain3 + 1)
                    taps("first", 2)
                if on[2]:
                    p = it - 2
                    pe.wait_ge(S["dw2"], p * 2 + 2)
                    pe.wait_ge(S["fused"], capped(p * 3 + 6, pairs * 3))
                    pointwise_one(pw["fuse2"], acc[2][0], acc[2][1], S["pw2"])
                if on[5]:
                    transposes(it - 5, 0)
                if on[1]:
                    p = it - 1
                    pe.wait_ge(S["dw1"], p * 2 + 2)
                    if on[2]:
                        pe.wait_ge(S["relu2"], (it - 2) * 2 + 2)
                    else:
                        pe.wait_ge(S["fused"], p * 3 + 3)
                    pointwise_one(pw["fuse1"], acc[1][0], acc[1][1], S["pw1"])
                if on[3]:
                    tokens(it - 3, 1)
                if on[5]:
                    transposes(it - 5, 1)

            run(pe, body)

        @block.scalar
        def _(act):
            for n in range(KT):
                act.wait_ge(S["fold_done"], n + 1)
                nc.scalar.copy(w_conv[:, n, 1, :], conv_ps[n % 2][:, 0:P]).then_inc(S["fold_copied"], 1)
                nc.scalar.copy(w_conv[:, n, 2, HI:P], conv_ps[n % 2][:, P:D]).then_inc(S["fold_copied"], 1)
            act.wait_ge(S["weights"], 16 * len(loads))
            nc.scalar.activation(gate[:, :], alpha[:, :], ACT.Tanh).then_inc(S["gate_act"], 1)
            act.wait_ge(S["gate_ready"], 3)
            act.wait_ge(S["zeroed"], 1)

            def tap_products(name, p, filled):
                first, pads, _, rows, _ = layers[name]
                act.wait_ge(filled, p * 2 + 2)
                if not (type(p) is int and p == 0):
                    act.wait_ge(S["dw" + name], p * 2)
                for tap in range(pe_taps + 1, TAPS):
                    for t in range(2):
                        nc.scalar.activation(grid(products[name][t][tap - pe_taps - 1], rows[t]),
                                             shifted(pads[t], tap, rows[t]), ACT.Identity,
                                             scale=dw_w[:, first + t, tap:tap + 1]).then_inc(S["mul" + name], 1)

            def token_copy(p, img):
                act.wait_ge(S["tok_done"], p * 2 + img + 1)
                if img == 0 and not (type(p) is int and p == 0):
                    act.wait_ge(S["ln1_norm"], p * 4)
                nc.scalar.copy(tok[:, 2 * img:2 * img + 2, :],
                               tok_ps[0:TT, 0:2 * D].rearrange("p (h c) -> p h c", h=2)).then_inc(S["tok_copied"], 1)

            def transpose_copy(p, part):
                act.wait_ge(S["tr_done"], p * 2 + part + 1)
                if part == 0 and not (type(p) is int and p == 0):
                    act.wait_ge(S["xt_stored"], p * 16)
                nc.scalar.copy(xt[:, part, :], tr_ps[:, 0:2 * L]).then_inc(S["tr_copied"], 1)

            def body(it, on):
                def gelu(t):
                    act.wait_ge(S["conv_done"], it * 3 + t + 1)
                    if not (type(it) is int and it == 0):
                        act.wait_ge(S["first_dw"], it * 3)
                    nc.scalar.activation(maps(pad_first[t]), as_maps(conv_ps[t % 2][:, 0:2 * PX]), ACT.Gelu,
                                         bias=conv_bias[:, t:t + 1]).then_inc(S["gelu_done"], 1)

                if on[3]:
                    tap_products("3", it - 3, S["joined"])
                if on[0]:
                    gelu(0)
                if on[0]:
                    gelu(1)
                if on[1]:
                    p = it - 1
                    for t in range(2):
                        act.wait_ge(S["pw_loc"], p * 2 + t + 1)
                        if t == 0 and not (type(p) is int and p == 0):
                            act.wait_ge(S["loc_kept"], p * 2)
                            act.wait_ge(S["part_out"], p * 2)
                        nc.scalar.activation(loc[t][:, :], pw_ps[t][:, 0:(2 - t) * PX], ACT.Identity,
                                             bias=pw_bias[:, 0, t:t + 1]).then_inc(S["loc_out"], 1)
                if on[1]:
                    p = it - 1
                    for t in range(2):
                        act.wait_ge(S["pw_glob"], p * 2 + t + 1)
                        if t == 0 and not (type(p) is int and p == 0):
                            act.wait_ge(S["pw_glob2"], p * 2)
                        nc.scalar.activation(gg[t][:, :], pw_ps[t][:, 0:(2 - t) * PX], ACT.Gelu,
                                             bias=pw_bias[:, 1, t:t + 1]).then_inc(S["gg_out"], 1)
                    for t in range(2):
                        act.wait_ge(S["loc_out"], p * 2 + 2)
                        if t == 0 and not (type(p) is int and p == 0):
                            act.wait_ge(S["fused"], p * 3)
                        nc.scalar.activation(loc_part[t][:, :], loc[t][:, :], ACT.Identity, scale=one_minus[:, t:t + 1],
                                             bias=gate_b[:, t:t + 1]).then_inc(S["part_out"], 1)
                if on[2]:
                    tap_products("2", it - 2, S["relu1"])
                if on[0]:
                    gelu(2)
                if on[2]:
                    p = it - 2
                    for t in range(2):
                        act.wait_ge(S["pw2"], p * 2 + t + 1)
                        if t == 0 and not (type(p) is int and p == 0):
                            act.wait_ge(S["joined"], p * 2)
                        nc.scalar.activation(relu2[t][:, :], pw_ps[t][:, 0:(2 - t) * PX], ACT.Relu,
                                             bias=pw_bias[:, 4, t:t + 1]).then_inc(S["relu2"], 1)
                if on[3]:
                    token_copy(it - 3, 0)
                if on[5]:
                    transpose_copy(it - 5, 0)
                if on[1]:
                    p = it - 1
                    for t in range(2):
                        act.wait_ge(S["pw1"], p * 2 + t + 1)
                        if t == 0 and not (type(p) is int and p == 0):
                            act.wait_ge(S["dw2"], p * 2)
                        dst, src = ((maps(pad[2][0]), as_maps(pw_ps[0][:, 0:2 * PX])) if t == 0 else
                                    (pad[2][1][:, 1:G + 1, 1:G + 1], grid(pw_ps[1], G)))
                        nc.scalar.activation(dst, src, ACT.Relu, bias=pw_bias[:, 3, t:t + 1]).then_inc(S["relu1"], 1)
                if on[5]:
                    transpose_copy(it - 5, 1)
                if on[3]:
                    token_copy(it - 3, 1)

            run(act, body)

        @block.gpsimd
        def _(pool):
            for t in pad_first + pad[1] + pad[2] + pad[3]:
                nc.gpsimd.memset(t[:], 0.0)
            nc.gpsimd.memset(acc[3][0][:, 0:1], 0.0)
            nc.gpsimd.memset(acc[3][1][:, 0:1], 0.0)
            nc.gpsimd.memset(minus_half[:], -0.5).then_inc(S["zeroed"], 1)
            pool.wait_ge(S["weights"], 16 * len(loads))
            pool.wait_ge(S["zeroed"], 1)

            def other_steps(name, p):
                first, pads, accs, rows, lo = layers[name]
                for tap in range(pe_taps + 1, TAPS):
                    for t in range(2):
                        dst = grid(accs[t], rows[t], lo)
                        if tap == pe_taps + 1:
                            pool.wait_ge(S["start" + name], p * 2 + t + 1)
                        else:
                            pool.wait_ge(S["chain" + name], p * (chain2 - 2) + (tap - pe_taps - 2) * 2 + t + 1)
                        pool.wait_ge(S["mul" + name], p * chain2 + (tap - pe_taps - 1) * 2 + t + 1)
                        nc.gpsimd.tensor_tensor(dst, dst, grid(products[name][t][tap - pe_taps - 1], rows[t]), ALU.add)\
                            .then_inc(S[("chain" if tap < TAPS - 1 else "dw") + name], 1)

            def body(it, on):
                if on[5]:
                    p = it - 5
                    pool.wait_ge(S["ln2_stats"], p * 9 + 9)
                    nc.gpsimd.tensor_tensor(rs2[:, :], ve2[:, :], minus_half[:, :], ALU.pow).then_inc(S["ln2_rs"], 1)
                if on[3]:
                    other_steps("3", it - 3)
                if on[4]:
                    p = it - 4
                    pool.wait_ge(S["ln1_stats"], p * 9 + 9)
                    nc.gpsimd.tensor_tensor(rs1[:, :], ve1[:, :], minus_half[:, :], ALU.pow).then_inc(S["ln1_rs"], 1)
                if on[2]:
                    other_steps("2", it - 2)
                if on[4]:
                    p = it - 4
                    pool.wait_ge(S["ln1_norm"], p * 4 + 4)
                    nc.gpsimd.tensor_tensor(hg[:, :, :], hn[:, :, :], ln_g[:, :].unsqueeze(1).broadcast_to([TT, 4, D]),
                                            ALU.mult).then_inc(S["ln1_affine"], 1)
                    pool.wait_ge(S["ln1_affine"], p * 4 + 1)
                    if not (type(p) is int and p == 0):
                        pool.wait_ge(S["h_stored"], p * 16)
                        pool.wait_ge(S["ln2_norm"], p * 4)
                    nc.gpsimd.tensor_tensor(h[:, :, :], hg[:, :, :], ln_b[:, :].unsqueeze(1).broadcast_to([TT, 4, D]),
                                            ALU.add).then_inc(S["ln1_affine"], 1)
                    pool.wait_ge(S["ln1_affine"], p * 4 + 2)
                    for img in range(2):
                        if img == 0:
                            pool.sem_inc(S["fence"], 1)
                        nc.gpsimd.tensor_copy(h[0:1, 2 * img, :], cls[0:1, :]).then_inc(S["ln1_affine"], 1)
                if on[2]:
                    p = it - 2
                    for t in range(2):
                        pool.wait_ge(S["relu2"], p * 2 + t + 1)
                        if t == 0 and not (type(p) is int and p == 0):
                            pool.wait_ge(S["dw3"], p * 2)
                        if t == 0:
                            pool.wait_ge(S["loc_kept"], p * 2 + 2)
                            nc.gpsimd.tensor_tensor(maps(pad[3][0]), as_maps(relu2[0][:, :]), as_maps(loc_old[0][:, :]),
                                                    ALU.add).then_inc(S["joined"], 1)
                        else:
                            nc.gpsimd.tensor_tensor(pad[3][1][:, 1:G + 1, 1:G + 1], grid(relu2[1], G), grid(loc_old[1], G),
                                                    ALU.add).then_inc(S["joined"], 1)
                if on[1]:
                    p = it - 1
                    for t in range(2):
                        pool.wait_ge(S["loc_out"], p * 2 + t + 1)
                        if on[2]:
                            pool.wait_ge(S["joined"], (it - 2) * 2 + t + 1)
                        pool.sem_inc(S["fence"], 1)
                        nc.gpsimd.tensor_copy(loc_old[t][:, :], loc[t][:, :]).then_inc(S["loc_kept"], 1)

            run(pool, body)

        @block.vector
        def _(dve):
            dve.wait_ge(S["conv_weights"], 16 * len(conv_loads))
            for n in range(KT):
                nc.vector.tensor_copy(w_conv[:, n, 0, :], w_loc[:, n, 0:P])
                last = nc.vector.tensor_copy(w_conv[:, n, 2, 0:HI], w_loc[:, n, P:D])
            last.then_inc(S["setup"], 1)
            dve.wait_ge(S["weights"], 16 * len(loads))
            for q in range(9):
                for k in range(pe_taps):
                    nc.vector.tensor_scalar(dw_diag[:, q, k, :], ident[:, :], dw_w[:, q, k:k + 1], None,
                                            ALU.mult).then_inc(S["diag"], 1)
            dve.wait_ge(S["gate_act"], 1)
            nc.vector.tensor_scalar(one_minus[:, :], gate[:, :], -0.5, 0.5, ALU.mult, ALU.add).then_inc(S["gate_ready"], 1)
            dve.wait_ge(S["gate_ready"], 1)
            nc.vector.tensor_scalar(gate[:, :], gate[:, :], 0.5, 0.5, ALU.mult, ALU.add).then_inc(S["gate_ready"], 1)
            dve.wait_ge(S["gate_ready"], 2)
            nc.vector.tensor_tensor(gate_b[:, :], gate[:, :], pw_bias[:, 2, :], ALU.mult).then_inc(S["gate_ready"], 1)
            dve.wait_ge(S["gate_ready"], 3)
            dve.wait_ge(S["zeroed"], 1)

            def depthwise(name, p, dep_sem, dep):
                first, pads, accs, rows, lo = layers[name]
                n = len(pads)
                steps = TAPS - pe_taps
                taps_done = S["taps_first" if name == "first" else "taps" + name]
                chain = S["first_chain" if name == "first" else "chain" + name]
                done = S["first_dw" if name == "first" else "dw" + name]
                order = [(k - 2 * (t // 2), t) for k in range(steps + 2) for t in range(n) if 0 <= k - 2 * (t // 2) < steps]
                at = {}
                count = 0
                per = n * (steps - 1)
                for k, t in order:
                    tap = pe_taps + k
                    dst = grid(accs[t], rows[t], lo)
                    if k == 0:
                        dve.wait_ge(taps_done, p * n + t + 1)
                        src = grid(tap_ps[t % 2], rows[t])
                        if t == 0 and dep is not None:
                            dve.wait_ge(dep_sem, dep)
                    else:
                        dve.wait_ge(chain, p * per + at[t])
                        src = dst
                    ins = nc.vector.scalar_tensor_tensor(out=dst, in0=shifted(pads[t], tap, rows[t]),
                                                         scalar=dw_w[:, first + t, tap:tap + 1], in1=src,
                                                         op0=ALU.mult, op1=ALU.add)
                    if k < steps - 1:
                        ins.then_inc(chain, 1)
                        count += 1
                        at[t] = count
                    else:
                        ins.then_inc(done, 1)

            def first_step(name, p, read):
                first, pads, accs, rows, lo = layers[name]
                for t in range(2):
                    dve.wait_ge(S["taps" + name], p * 2 + t + 1)
                    if t == 0 and not (type(p) is int and p == 0):
                        dve.wait_ge(read, p * 2)
                    nc.vector.scalar_tensor_tensor(out=grid(accs[t], rows[t], lo), in0=shifted(pads[t], pe_taps, rows[t]),
                                                   scalar=dw_w[:, first + t, pe_taps:pe_taps + 1],
                                                   in1=grid(tap_ps[t], rows[t]), op0=ALU.mult, op1=ALU.add)\
                        .then_inc(S["start" + name], 1)

            def stats(p, src, st, mv, ve, s, norm):
                if not (type(p) is int and p == 0):
                    dve.wait_ge(norm, p * 4)
                for q in range(4):
                    nc.vector.bn_stats(st[:, q, :], src[:, q, :]).then_inc(s, 1)
                for q in range(4):
                    dve.wait_ge(s, p * 9 + q + 1)
                    dve.sem_inc(S["fence"], 1)
                    nc.vector.bn_aggr(mv[:, q, :], st[:, q, :]).then_inc(s, 1)
                dve.wait_ge(s, p * 9 + 8)
                nc.vector.tensor_scalar(ve[:, :], mv[:, :, 1], LN_EPS, None, ALU.add).then_inc(s, 1)

            def normalise(dst, src, mv, rs, s):
                for q in range(4):
                    nc.vector.tensor_scalar(dst[:, q, :], src[:, q, :], mv[:, q, 0:1], rs[:, q:q + 1],
                                            ALU.subtract, ALU.mult).then_inc(s, 1)

            def body(it, on):
                if on[5]:
                    p = it - 5
                    dve.wait_ge(S["ln1_affine"], p * 4 + 4)
                    if not (type(p) is int and p == 0):
                        dve.wait_ge(S["ln2_rs"], p)
                    stats(p, h, st2, mv2, ve2, S["ln2_stats"], S["ln2_norm"])
                if on[3]:
                    p = it - 3
                    first_step("3", p, S["tok_done"])
                if on[2]:
                    p = it - 2
                    first_step("2", p, S["pw2"])
                if on[4]:
                    p = it - 4
                    dve.wait_ge(S["tok_copied"], p * 2 + 2)
                    if not (type(p) is int and p == 0):
                        dve.wait_ge(S["ln1_rs"], p)
                    stats(p, tok, st1, mv1, ve1, S["ln1_stats"], S["ln1_norm"])
                if on[5]:
                    p = it - 5
                    dve.wait_ge(S["ln2_rs"], p + 1)
                    if not (type(p) is int and p == 0):
                        dve.wait_ge(S["x_stored"], p * 16)
                        dve.wait_ge(S["tr_done"], p * 2)
                    normalise(xn, h, mv2, rs2, S["ln2_norm"])
                if on[4]:
                    p = it - 4
                    dve.wait_ge(S["ln1_rs"], p + 1)
                    if not (type(p) is int and p == 0):
                        dve.wait_ge(S["ln1_affine"], p * 4)
                    normalise(hn, tok, mv1, rs1, S["ln1_norm"])
                if on[1]:
                    p = it - 1
                    if not (type(p) is int and p == 0):
                        dve.wait_ge(S["dw1"], p * 2)
                    dve.wait_ge(S["part_out"], p * 2 + 2)
                    dve.wait_ge(S["pw_glob2"], p * 2 + 2)
                    for img in range(2):
                        nc.vector.scalar_tensor_tensor(out=pad[1][0][:, 1 + img * (G + 1):1 + img * (G + 1) + G, 1:G + 1],
                                                       in0=grid(pw_ps[0], G, img * PX), scalar=gate[:, 0:1],
                                                       in1=grid(loc_part[0], G, img * PX),
                                                       op0=ALU.mult, op1=ALU.add).then_inc(S["fused"], 1)
                    nc.vector.scalar_tensor_tensor(out=pad[1][1][:, 1:G + 1, 1:G + 1], in0=grid(pw_ps[1], G),
                                                   scalar=gate[:, 1:2], in1=grid(loc_part[1], G),
                                                   op0=ALU.mult, op1=ALU.add).then_inc(S["fused"], 1)
                if on[1]:
                    p = it - 1
                    first = type(p) is int and p == 0
                    depthwise("1", p, S["pw1"], None if first else p * 2)
                if on[0]:
                    first = type(it) is int and it == 0
                    depthwise("first", it, S["pw_glob"], None if first else it * 2)

            run(dve, body)


B_ROWS, DECAYS, DRIVES, HIDS, PRODS = 4, 16, 12, 4, 8

PE_START = (0, 2, 4, 15, 17, 20, 22, 24, 32, 34, 36)
PE_PROJECT = (10, 13)
ACT_START = (5, 8, 10, 21, 22, 25, 27, 29, 38, 41, 42)
PE_ROW_LEAD = 3
ACT_ROW_LEAD = 4
ACT_SILU = (16, 47)
ACT_OUT = (16, 17)
ACT_SPLIT = (22, 32, 41)
ACT_SOFTPLUS = (30, 33, 34)
POOL_GATE = (9, 11, 13)
POOL_ROOT = 31
POOL_SPLIT = (29, 40)
POOL_AFFINE = (36, 41, 42)
DVE_SKIP = (1, 2, 3)
DVE_END = (17, 21, 22, 23, 27)
DVE_SOFTPLUS = (33, 34, 35, 36)


def token_mixer_weights(sb):
    return {"ident": sb("b_ident", [P, P]), "w_in": sb("b_w_in", [P, 2, 2 * DT, P]), "w_x": sb("b_w_x", [P, DT, P]),
            "w_bc": sb("b_w_bc", [P, DT, 96]), "w_dt": sb("b_w_dt", [P, DT, P]), "b_dt": sb("b_b_dt", [P, DT]),
            "a_log": sb("b_a_log", [P, DT, NS]), "d_skip": sb("b_d_skip", [P, DT]), "w_out": sb("b_w_out", [P, DT, D]),
            "gamma": sb("b_gamma", [TT, D]), "beta": sb("b_beta", [TT, D]), "pick": sb("b_pick_row", [96, 2 * NS])}


def mix_tokens(nc, w, loaded, h_in, x_in, xt_in, h_out, pairs):
    assert pairs % 2 == 0 and pairs >= 6
    W = 2 * L
    UNITS = NS * DT
    with ExitStack() as ctx:
        def sb(name, shape, dt=F32):
            return ctx.enter_context(nc.sbuf_tensor(name, shape, dt))

        def sem(name):
            return ctx.enter_context(nc.semaphore(name))

        def bank(name):
            return ctx.enter_context(nc.psum_tensor(name, [P, 512], F32))

        ident, w_in, w_x, w_bc, w_dt, b_dt = (w[n] for n in ("ident", "w_in", "w_x", "w_bc", "w_dt", "b_dt"))
        a_log, d_skip, w_out, gamma, beta = (w[n] for n in ("a_log", "d_skip", "w_out", "gamma", "beta"))
        a_exp = sb("b_a_exp", [P, DT, NS])
        a_neg = sb("b_a_neg", [P, DT, NS])
        pick = sb("b_pick", [96, 2 * NS, P], BF16)
        minus_half = sb("b_minus_half", [TT, 4])

        xt = sb("b_xt", [P, 2, W])
        xz_raw = sb("b_xz_raw", [P, 2 * DT, W])
        xz = [sb(f"b_xz{q}", [P, 2 * DT, W]) for q in range(2)]
        xd = sb("b_xd", [P, W])
        bc_f = sb("b_bc_f", [96, W])
        bc_hi = sb("b_bc_hi", [96, W], BF16)
        bc_r = sb("b_bc_r", [96, W])
        bc_mid = sb("b_bc_mid", [96, W], BF16)
        bc = [sb(f"b_bc{q}", [96, W], BF16) for q in range(2)]
        absd = sb("b_absd", [P, DT, W])
        relud = sb("b_relud", [P, DT, W])
        expd = sb("b_expd", [P, DT, W])
        onep = sb("b_onep", [P, DT, W])
        logd = sb("b_logd", [P, DT, W])
        lost, sumd = absd, logd
        dt = [sb(f"b_dt{q}", [P, DT, W]) for q in range(2)]
        dtx = [sb(f"b_dtx{q}", [P, DT, W]) for q in range(2)]
        b_row = [sb(f"b_b_row{i}", [P, W]) for i in range(B_ROWS)]
        decays = sb("b_decays", [P, DECAYS, W])
        dbx = [sb(f"b_dbx{i}", [P, W]) for i in range(DRIVES)]
        hid = [sb(f"b_hid{i}", [P, W]) for i in range(HIDS)]
        prod = [sb(f"b_prod{i}", [P, W]) for i in range(PRODS)]
        yd = sb("b_yd", [P, DT, W])
        yg = sb("b_yg", [P, DT, W])
        mo = sb("b_mo", [TT, 4, D])
        xn = sb("b_xn", [TT, 4, D])
        hin = sb("b_hin", [TT, 4, D])
        hs = sb("b_hs", [TT, 4, D])
        st = sb("b_st", [TT, 4, 6])
        mv = sb("b_mv", [TT, 4, 2])
        ve = sb("b_ve", [TT, 4])
        rs = sb("b_rs", [TT, 4])
        hn = sb("b_hn", [TT, 4, D])
        ha = sb("b_ha", [TT, 4, D])
        hb = hn
        h2 = sb("b_h2", [TT, 4, D])

        y_ps = [bank(f"b_y_ps{j}") for j in range(DT)]
        b_ps = bank("b_b_ps")
        c_ps = [bank(f"b_c_ps{i}") for i in range(2)]
        ob = [bank(f"b_ob{i}") for i in range(2)]

        S = {n: sem("b_" + n) for n in (
            "fence", "zeroed", "picks", "a_ready", "xt_loaded", "xn_loaded", "h_loaded",
            "in_done", "in_out", "silu", "bc_parts", "bc_rest", "dt_relu", "dt_act", "dt_ready", "dtx_ready",
            "b_done", "b_out", "c_done", "exp_done", "dbx_done", "scan_done", "prod_done", "acc_done",
            "yd_done", "yg_done", "out_done", "mo_out", "res", "stats", "rs_ready", "norm", "affine", "stored")}

        def run(eng, body):
            body(-1, 1, False, False, True)
            body(0, 0, False, True, True)
            body(1, 1, True, True, True)
            body(2, 0, True, True, True)
            with eng.Fori(1, (pairs - 2) // 2) as m:
                body(m * 2 + 1, 1, True, True, True)
                body(m * 2 + 2, 0, True, True, True)
            body(pairs - 1, 1, True, True, False)
            body(pairs, 0, True, False, False)

        def late(p):
            return not (type(p) is int and p == 0)

        def images(t):
            return t.rearrange("p (i l) -> p i l", i=2)

        block = ctx.enter_context(nc.Block())

        @block.sync
        def _(sp):
            def body(k, q, last, now, nxt):
                if nxt:
                    p = k + 1
                    if late(p):
                        sp.wait_ge(S["in_done"], p * 11)
                    sp.dma_start(xt[:], xt_in[p]).then_inc(S["xt_loaded"], 16)
                if last:
                    p = k - 1
                    if late(p):
                        sp.wait_ge(S["res"], p)
                    sp.dma_start(xn[:], x_in[p]).then_inc(S["xn_loaded"], 16)
                    if late(p):
                        sp.wait_ge(S["affine"], p * 3)
                    sp.dma_start(hin[:], h_in[p]).then_inc(S["h_loaded"], 16)
                    sp.wait_ge(S["affine"], p * 3 + 3)
                    sp.dma_start(h_out[p], h2[:]).then_inc(S["stored"], 16)

            run(sp, body)
            sp.wait_ge(S["stored"], pairs * 16)

        @block.tensor
        def _(pe):
            pe.wait_ge(loaded, 16 * len(w))
            pe.wait_ge(S["picks"], 1)

            def start(p, q, i, ends):
                if i == 0:
                    pe.wait_ge(S["xt_loaded"], p * 16 + 16)
                if i >= 2:
                    pe.wait_ge(S["in_out"], p * 11 + i - 1)
                elif late(p):
                    pe.wait_ge(S["in_out"], p * 11)
                if i in (3, 4) and ends:
                    pe.wait_ge(S["mo_out"], p * 2 + i - 6)
                if i == 3:
                    pe.wait_ge(S["silu"], p * 2 + 1)
                if i == 5:
                    pe.wait_ge(S["in_out"], p * 11 + 4)
                o = ob[i % 2][:, 0:W]
                if i < 3 or i >= 8:
                    tile = i if i < 3 else i - 8 + DT
                    for part in range(2):
                        mm = pe.matmul(o, w_in[:, part, tile, :], xt[:, part, :], start=(part == 0), stop=(part == 1))
                elif i == 3:
                    for j in range(DT):
                        mm = pe.matmul(o, w_x[:, j, :], xz[q][:, j, :], start=(j == 0), stop=(j == DT - 1))
                elif i == 4:
                    for j in range(DT):
                        mm = pe.matmul(o[0:96, :], w_bc[:, j, :], xz[q][:, j, :], start=(j == 0), stop=(j == DT - 1))
                else:
                    mm = pe.matmul(o, w_dt[:, i - 5, :], xd[:, :], start=True, stop=True)
                mm.then_inc(S["in_done"], 1)

            def row_b(p, q, n):
                if n == 0:
                    pe.wait_ge(S["bc_parts"], p * 4 + 4)
                    pe.wait_ge(S["bc_rest"], p * 2 + 2)
                if late(p) or n > 0:
                    pe.wait_ge(S["b_out"], p * NS + n)
                pe.matmul(b_ps[:, 0:W], pick[:, n, :], bc[q][:, :], start=True, stop=True).then_inc(S["b_done"], 1)

            def row_c(p, q, n):
                if late(p) or n > 1:
                    pe.wait_ge(S["prod_done"], p * UNITS + (n - 1) * DT)
                pe.matmul(c_ps[n % 2][:, 0:W], pick[:, NS + n, :], bc[q][:, :], start=True, stop=True)\
                    .then_inc(S["c_done"], 1)

            def add_up(p, u):
                n, j = u // DT, u % DT
                if n == 0 and late(p):
                    pe.wait_ge(S["yd_done"], p * DT - DT + j + 1)
                pe.wait_ge(S["prod_done"], p * UNITS + u + 1)
                pe.matmul(y_ps[j][:, 0:W], ident[:, :], prod[u % PRODS][:, :], start=(n == 0), stop=(n == NS - 1))\
                    .then_inc(S["acc_done"], 1)

            def project(p, img, starts):
                if img == 0:
                    pe.wait_ge(S["yg_done"], p * DT + DT)
                if starts:
                    pe.wait_ge(S["in_out"], p * 11 + 2 * 11 + 2 + img)
                else:
                    pe.wait_ge(S["in_out"], pairs * 11)
                if late(p):
                    pe.wait_ge(S["mo_out"], p * 2)
                for half in range(2):
                    lo = img * L + half * HALF
                    for j in range(DT):
                        mm = pe.matmul(ob[1 - img][0:TT, half * D:(half + 1) * D], yg[:, j, lo:lo + TT], w_out[:, j, :],
                                       start=(j == 0), stop=(j == DT - 1))
                mm.then_inc(S["out_done"], 1)

            def body(k, q, last, now, nxt):
                for u in range(UNITS):
                    n, j = u // DT, u % DT
                    if j == 0:
                        if n + PE_ROW_LEAD < NS:
                            if now:
                                row_b(k, q, n + PE_ROW_LEAD)
                        elif nxt:
                            row_b(k + 1, 1 - q, n + PE_ROW_LEAD - NS)
                        if n + 1 < NS:
                            if now:
                                row_c(k, q, n + 1)
                        elif nxt:
                            row_c(k + 1, 1 - q, 0)
                    if nxt and u in PE_START:
                        start(k + 1, 1 - q, PE_START.index(u), last)
                    if last and u in PE_PROJECT:
                        project(k - 1, PE_PROJECT.index(u), nxt)
                    if now:
                        add_up(k, u)

            run(pe, body)

        @block.scalar
        def _(act):
            act.wait_ge(loaded, 16 * len(w))
            act.wait_ge(S["zeroed"], 1)
            nc.scalar.activation(a_exp[:, :, :], a_log[:, :, :], ACT.Exp).then_inc(S["a_ready"], 1)
            act.wait_ge(S["a_ready"], 1)
            nc.scalar.mul(a_neg[:, :, :], a_exp[:, :, :], -1.0).then_inc(S["a_ready"], 1)
            act.wait_ge(S["a_ready"], 2)

            def start(p, q, i):
                act.wait_ge(S["in_done"], p * 11 + i + 1)
                if i < 3 or i >= 8:
                    tile = i if i < 3 else i - 8 + DT
                    if i in (0, 8) and late(p):
                        act.wait_ge(S["silu"], p * 2 + i // 8)
                    nc.scalar.copy(xz_raw[:, tile, :], ob[i % 2][:, 0:W]).then_inc(S["in_out"], 1)
                elif i == 3:
                    nc.scalar.copy(xd[:, :], ob[1][:, 0:W]).then_inc(S["in_out"], 1)
                elif i == 4:
                    if late(p):
                        act.wait_ge(S["bc_rest"], p * 2)
                    nc.scalar.copy(bc_f[:, :], ob[0][0:96, 0:W]).then_inc(S["in_out"], 1)
                else:
                    j = i - 5
                    if j == 0 and late(p):
                        act.wait_ge(S["dt_act"], p * 3)
                        act.wait_ge(S["dt_ready"], p * 3)
                    nc.scalar.activation(relud[:, j, :], ob[i % 2][:, 0:W], ACT.Relu, bias=b_dt[:, j:j + 1]).then_inc(S["dt_relu"], 1)
                    nc.scalar.activation(absd[:, j, :], ob[i % 2][:, 0:W], ACT.Abs, bias=b_dt[:, j:j + 1]).then_inc(S["in_out"], 1)

            def silu(p, q, part):
                act.wait_ge(S["in_out"], p * 11 + (11 if part else 3))
                if type(p) is not int or p >= 2:
                    act.wait_ge(S["yg_done"], p * DT - DT)
                nc.scalar.activation(xz[q][:, part * DT:part * DT + DT, :], xz_raw[:, part * DT:part * DT + DT, :], ACT.Silu)\
                    .then_inc(S["silu"], 1)

            def bc_step(p, q, i):
                if i == 0:
                    act.wait_ge(S["in_out"], p * 11 + 5)
                    if late(p):
                        act.wait_ge(S["bc_parts"], p * 4)
                        act.wait_ge(S["bc_rest"], p * 2)
                    nc.scalar.copy(bc_hi[:, :], bc_f[:, :]).then_inc(S["bc_parts"], 1)
                elif i == 1:
                    act.wait_ge(S["bc_rest"], p * 2 + 1)
                    nc.scalar.copy(bc_mid[:, :], bc_r[:, :]).then_inc(S["bc_parts"], 1)
                else:
                    act.wait_ge(S["bc_rest"], p * 2 + 2)
                    nc.scalar.copy(bc[q][0:32, :], bc_hi[0:32, :]).then_inc(S["bc_parts"], 1)
                    nc.scalar.copy(bc[q][32:64, :], bc_mid[32:64, :]).then_inc(S["bc_parts"], 1)

            def softplus(p, i):
                if i == 0:
                    act.wait_ge(S["in_out"], p * 11 + 8)
                    nc.scalar.activation(expd[:, :, :], absd[:, :, :], ACT.Exp, scale=-1.0).then_inc(S["dt_act"], 1)
                elif i == 1:
                    act.wait_ge(S["dt_act"], p * 3 + 1)
                    nc.scalar.activation(onep[:, :, :], expd[:, :, :], ACT.Identity, bias=1.0).then_inc(S["dt_act"], 1)
                else:
                    act.wait_ge(S["dt_act"], p * 3 + 2)
                    nc.scalar.activation(logd[:, :, :], onep[:, :, :], ACT.Ln).then_inc(S["dt_act"], 1)

            def b_row_out(p, n):
                act.wait_ge(S["b_done"], p * NS + n + 1)
                if late(p) or n >= B_ROWS:
                    act.wait_ge(S["dbx_done"], p * UNITS + (n - B_ROWS + 1) * DT)
                nc.scalar.copy(b_row[n % B_ROWS][:, :], b_ps[:, 0:W]).then_inc(S["b_out"], 1)

            def decay(p, q, u):
                n, j = u // DT, u % DT
                if u == 0:
                    act.wait_ge(S["dt_ready"], p * 3 + 3)
                if late(p) or u >= DECAYS:
                    act.wait_ge(S["scan_done"], p * UNITS + u + 1 - DECAYS)
                nc.scalar.activation(images(decays[:, u % DECAYS, :])[:, :, 1:L], images(dt[q][:, j, :])[:, :, 1:L], ACT.Exp,
                                     scale=a_neg[:, j, n:n + 1]).then_inc(S["exp_done"], 1)

            def body(k, q, last, now, nxt):
                for u in range(UNITS):
                    n, j = u // DT, u % DT
                    if (u + ACT_ROW_LEAD) % DT == 0:
                        m = (u + ACT_ROW_LEAD) // DT
                        if m < NS:
                            if now:
                                b_row_out(k, m)
                        elif nxt:
                            b_row_out(k + 1, m - NS)
                    if now:
                        decay(k, q, u)
                    if nxt and u in ACT_START:
                        start(k + 1, 1 - q, ACT_START.index(u))
                    if nxt and u in ACT_SILU:
                        silu(k + 1, 1 - q, ACT_SILU.index(u))
                    if last and u in ACT_OUT:
                        p, img = k - 1, ACT_OUT.index(u)
                        act.wait_ge(S["out_done"], p * 2 + img + 1)
                        if img == 0 and late(p):
                            act.wait_ge(S["res"], p)
                        nc.scalar.copy(mo[:, 2 * img:2 * img + 2, :],
                                       ob[1 - img][0:TT, 0:2 * D].rearrange("p (h c) -> p h c", h=2)).then_inc(S["mo_out"], 1)
                    if nxt and u in ACT_SPLIT:
                        bc_step(k + 1, 1 - q, ACT_SPLIT.index(u))
                    if nxt and u in ACT_SOFTPLUS:
                        softplus(k + 1, ACT_SOFTPLUS.index(u))

            run(act, body)

        @block.gpsimd
        def _(pool):
            nc.gpsimd.memset(minus_half[:], -0.5).then_inc(S["fence"], 1)
            pool.wait_ge(S["fence"], 1)
            pool.wait_ge(loaded, 16 * len(w))

            def drive(p, q, u):
                n, j = u // DT, u % DT
                if u == 0:
                    pool.wait_ge(S["dtx_ready"], p + 1)
                if j == 0:
                    pool.wait_ge(S["b_out"], p * NS + n + 1)
                if late(p) or u >= DRIVES:
                    pool.wait_ge(S["scan_done"], p * UNITS + u + 1 - DRIVES)
                nc.gpsimd.tensor_tensor(dbx[u % DRIVES][:, :], dtx[q][:, j, :], b_row[n % B_ROWS][:, :], ALU.mult)\
                    .then_inc(S["dbx_done"], 1)

            def affine(p, i):
                if i == 0:
                    pool.wait_ge(S["norm"], p * 4 + 4)
                    nc.gpsimd.tensor_tensor(ha[:, :, :], hn[:, :, :], gamma[:, :].unsqueeze(1).broadcast_to([TT, 4, D]),
                                            ALU.mult).then_inc(S["affine"], 1)
                elif i == 1:
                    pool.wait_ge(S["affine"], p * 3 + 1)
                    nc.gpsimd.tensor_tensor(hb[:, :, :], ha[:, :, :], beta[:, :].unsqueeze(1).broadcast_to([TT, 4, D]),
                                            ALU.add).then_inc(S["affine"], 1)
                else:
                    pool.wait_ge(S["affine"], p * 3 + 2)
                    pool.wait_ge(S["h_loaded"], p * 16 + 16)
                    if late(p):
                        pool.wait_ge(S["stored"], p * 16)
                    nc.gpsimd.tensor_tensor(h2[:, :, :], hb[:, :, :], hin[:, :, :], ALU.add).then_inc(S["affine"], 1)

            def gate(p, q, j):
                pool.wait_ge(S["yd_done"], p * DT + j + 1)
                pool.wait_ge(S["silu"], p * 2 + 2)
                if j == 0 and late(p):
                    pool.wait_ge(S["out_done"], p * 2)
                nc.gpsimd.tensor_tensor(yg[:, j, :], yd[:, j, :], xz[q][:, DT + j, :], ALU.mult).then_inc(S["yg_done"], 1)

            def bc_step(p, q, i):
                pool.wait_ge(S["bc_parts"], p * 4 + i + 1)
                if i == 0:
                    nc.gpsimd.tensor_tensor(bc_r[:, :], bc_f[:, :], bc_hi[:, :], ALU.subtract).then_inc(S["bc_rest"], 1)
                else:
                    if type(p) is not int or p >= 2:
                        pool.wait_ge(S["c_done"], p * NS - NS)
                    nc.gpsimd.tensor_tensor(bc[q][:, :], bc_r[:, :], bc_mid[:, :], ALU.subtract).then_inc(S["bc_rest"], 1)

            def body(k, q, last, now, nxt):
                for u in range(UNITS):
                    if now:
                        drive(k, q, u)
                    if last and u in POOL_GATE:
                        gate(k - 1, 1 - q, POOL_GATE.index(u))
                    if last and u == POOL_ROOT:
                        pool.wait_ge(S["stats"], k * 9)
                        nc.gpsimd.tensor_tensor(rs[:, :], ve[:, :], minus_half[:, :], ALU.pow).then_inc(S["rs_ready"], 1)
                    if last and u in POOL_AFFINE:
                        affine(k - 1, POOL_AFFINE.index(u))
                    if nxt and u in POOL_SPLIT:
                        bc_step(k + 1, 1 - q, POOL_SPLIT.index(u))

            run(pool, body)

        @block.vector
        def _(dve):
            dve.wait_ge(loaded, 16 * len(w))
            nc.vector.tensor_copy(pick[:, :, :], w["pick"][:, :].unsqueeze(2).broadcast_to([96, 2 * NS, P])).then_inc(S["picks"], 1)
            nc.vector.memset(decays[:, :, :], 0.0).then_inc(S["zeroed"], 1)

            def scan(p, u):
                dve.wait_ge(S["exp_done"], p * UNITS + u + 1)
                dve.wait_ge(S["dbx_done"], p * UNITS + u + 1)
                if late(p) or u >= HIDS:
                    dve.wait_ge(S["prod_done"], p * UNITS + u + 1 - HIDS)
                nc.vector.tensor_tensor_scan(hid[u % HIDS][:, :], decays[:, u % DECAYS, :], dbx[u % DRIVES][:, :], 0.0,
                                             ALU.mult, ALU.add).then_inc(S["scan_done"], 1)

            def product(p, u):
                n, j = u // DT, u % DT
                dve.wait_ge(S["scan_done"], p * UNITS + u + 1)
                if j == 0:
                    dve.wait_ge(S["c_done"], p * NS + n + 1)
                if late(p) or u >= PRODS:
                    dve.wait_ge(S["acc_done"], p * UNITS + u + 1 - PRODS)
                nc.vector.tensor_tensor(prod[u % PRODS][:, :], hid[u % HIDS][:, :], c_ps[n % 2][:, 0:W], ALU.mult)\
                    .then_inc(S["prod_done"], 1)

            def skip_path(p, q, j):
                dve.wait_ge(S["acc_done"], p * UNITS + UNITS - DT + j + 1)
                if j == 0 and late(p):
                    dve.wait_ge(S["yg_done"], p * DT)
                nc.vector.scalar_tensor_tensor(out=yd[:, j, :], in0=xz[q][:, j, :], scalar=d_skip[:, j:j + 1],
                                               in1=y_ps[j][:, 0:W], op0=ALU.mult, op1=ALU.add)\
                    .then_inc(S["yd_done"], 1)

            def end(p, i):
                if i == 0:
                    dve.wait_ge(S["mo_out"], p * 2 + 2)
                    dve.wait_ge(S["xn_loaded"], p * 16 + 16)
                    if late(p):
                        dve.wait_ge(S["norm"], p * 4)
                    nc.vector.tensor_tensor(hs[:, :, :], mo[:, :, :], xn[:, :, :], ALU.add).then_inc(S["res"], 1)
                elif i == 1:
                    dve.wait_ge(S["res"], p + 1)
                    for t in range(4):
                        nc.vector.bn_stats(st[:, t, :], hs[:, t, :]).then_inc(S["stats"], 1)
                elif i == 2:
                    dve.wait_ge(S["stats"], p * 9 + 4)
                    dve.sem_inc(S["fence"], 1)
                    for t in range(4):
                        nc.vector.bn_aggr(mv[:, t, :], st[:, t, :]).then_inc(S["stats"], 1)
                elif i == 3:
                    dve.wait_ge(S["stats"], p * 9 + 8)
                    if late(p):
                        dve.wait_ge(S["rs_ready"], p)
                    nc.vector.tensor_scalar(ve[:, :], mv[:, :, 1], LN_EPS, None, ALU.add).then_inc(S["stats"], 1)
                else:
                    dve.wait_ge(S["rs_ready"], p + 1)
                    if late(p):
                        dve.wait_ge(S["affine"], p * 3)
                    for t in range(4):
                        nc.vector.tensor_scalar(hn[:, t, :], hs[:, t, :], mv[:, t, 0:1], rs[:, t:t + 1],
                                                ALU.subtract, ALU.mult).then_inc(S["norm"], 1)

            def softplus(p, q, i):
                if i == 0:
                    dve.wait_ge(S["dt_act"], p * 3 + 2)
                    nc.vector.scalar_tensor_tensor(out=lost[:, :, :], in0=onep[:, :, :], scalar=1.0, in1=expd[:, :, :],
                                                   op0=ALU.subtract, op1=ALU.subtract).then_inc(S["dt_ready"], 1)
                elif i == 1:
                    dve.wait_ge(S["dt_act"], p * 3 + 3)
                    dve.wait_ge(S["dt_relu"], p * 3 + 3)
                    nc.vector.tensor_tensor(sumd[:, :, :], relud[:, :, :], logd[:, :, :], ALU.add).then_inc(S["dt_ready"], 1)
                elif i == 2:
                    dve.wait_ge(S["dt_ready"], p * 3 + 2)
                    if type(p) is not int or p >= 2:
                        dve.wait_ge(S["exp_done"], p * UNITS - UNITS)
                    nc.vector.tensor_tensor(dt[q][:, :, :], sumd[:, :, :], lost[:, :, :], ALU.subtract)\
                        .then_inc(S["dt_ready"], 1)
                else:
                    dve.wait_ge(S["dt_ready"], p * 3 + 3)
                    dve.wait_ge(S["silu"], p * 2 + 1)
                    if type(p) is not int or p >= 2:
                        dve.wait_ge(S["dbx_done"], p * UNITS - UNITS)
                    nc.vector.tensor_tensor(dtx[q][:, :, :], dt[q][:, :, :], xz[q][:, 0:DT, :], ALU.mult)\
                        .then_inc(S["dtx_ready"], 1)

            def body(k, q, last, now, nxt):
                for u in range(UNITS):
                    if now:
                        scan(k, u)
                        if u > 0:
                            product(k, u - 1)
                    if last and u in DVE_SKIP:
                        skip_path(k - 1, 1 - q, DVE_SKIP.index(u))
                    if last and u in DVE_END:
                        end(k - 1, DVE_END.index(u))
                    if nxt and u in DVE_SOFTPLUS:
                        softplus(k + 1, 1 - q, DVE_SOFTPLUS.index(u))
                if now:
                    product(k, UNITS - 1)

            run(dve, body)


def slot_mixer_weights(sb):
    return {"slots": sb("c_slot_raw", [P, 2, SLOTS]),
            "scale": sb("c_scale", [P, 1]), "w_down": sb("c_w_down", [P, 2, 2, P]), "b_down": sb("c_b_down", [P, 2]),
            "w_up": sb("c_w_up", [P, 2, D]), "b_up": sb("c_b_up", [SLOTS, D]),
            "own": sb("c_own", [P, 2, SLOTS])}


def mix_slots(nc, w, ident, loaded, h_in, out, pairs):
    stages = 6
    TURN = 4
    assert pairs % TURN == 0 and pairs > 2 * TURN and 2 * TURN > stages
    W = 2 * L
    with ExitStack() as ctx:
        def sb(name, shape, dt=F32):
            return ctx.enter_context(nc.sbuf_tensor(name, shape, dt))

        def sem(name):
            return ctx.enter_context(nc.semaphore(name))

        def bank(name):
            return ctx.enter_context(nc.psum_tensor(name, [P, 512], F32))

        slot_raw, scale, own = w["slots"], w["scale"], w["own"]
        w_down, b_down, w_up, b_up = w["w_down"], w["b_down"], w["w_up"], w["b_up"]
        slot_sq = sb("c_slot_sq", [P, 2, SLOTS])
        slot_sum = sb("c_slot_sum", [P, 2, NP_])
        slot_norm = sb("c_slot_norm", [P, 2, NP_])
        slots = sb("c_slots", [P, 2, SLOTS])
        minus_half = sb("c_minus_half", [TT, 4])
        plus_half = sb("c_plus_half", [P, 2, NP_])
        minus_one = sb("c_minus_one", [P, 2, NP_])

        h = [sb(f"c_h{q}", [TT, 4, D]) for q in range(2)]
        st = sb("c_st", [TT, 4, 6])
        mv = sb("c_mv", [TT, 4, 2])
        sm = [sb(f"c_sm{i}", [TT, 4]) for i in range(9)]
        xn = [sb(f"c_xn{r}", [TT, 4, D]) for r in range(TURN)]
        xt = [sb(f"c_xt{q}", [P, 2, W]) for q in range(2)]
        mx_d = sb("c_mx_d", [SLOTS, 2])
        e_d = sb("c_e_d", [SLOTS, 2, L])
        sum_d = sb("c_sum_d", [SLOTS, 2])
        inv_d = sb("c_inv_d", [SLOTS, 2])
        p_d = sb("c_p_d", [SLOTS, 2, L])
        mx_c = sb("c_mx_c", [TT, 4])
        l_c = sb("c_l_c", [TT, 4, SLOTS])
        e_c = sb("c_e_c", [TT, 4, SLOTS])
        sum_c = sb("c_sum_c", [TT, 4])
        inv_c = sb("c_inv_c", [TT, 4])
        p_c = sb("c_p_c", [TT, 4, SLOTS])
        dm = sb("c_dm", [TT, 4, SLOTS])
        ct = [sb(f"c_ct{q}", [SLOTS, 4, TT]) for q in range(2)]
        xs = sb("c_xs", [P, 2, 2 * SLOTS])
        hid = sb("c_hid", [P, 2, 2 * SLOTS])
        own_hid = sb("c_own_hid", [P, 2, 2 * SLOTS])
        ys = sb("c_ys", [SLOTS, 2, D])
        h_again = sb("c_h_again", [TT, 4, D])
        res = sb("c_res", [TT, 4, D])

        tr_ps = bank("c_tr_ps")
        lg_ps = bank("c_lg_ps")
        lt_ps = bank("c_lt_ps")
        xs_ps = bank("c_xs_ps")
        hid_ps = bank("c_hid_ps")
        ys_ps = bank("c_ys_ps")
        out_ps = [bank("c_out_ps0"), bank("c_out_ps1")]

        S = {n: sem("c_" + n) for n in (
            "fence", "consts", "slot_steps", "slots_ready",
            "h_loaded0", "h_loaded1", "h_again_loaded", "stats", "steps", "norm", "tr_done", "xt_out",
            "lg_done", "lt_done", "mx", "e_d", "d_steps", "c_steps", "e_c", "dm_done", "dm_out", "ct_done", "ct_out",
            "xs_done", "xs_out", "hid_done", "hid_out", "masked", "ys_done", "ys_out", "out_done", "summed", "stored")}

        def run(eng, body):
            def peeled(k):
                body(k, k // 2, k % TURN, [0 <= k - stage < pairs for stage in range(stages)])

            for k in range(2 * TURN):
                peeled(k)
            with eng.Fori(2, pairs // TURN) as turn:
                for q in range(TURN):
                    body(turn * TURN + q, turn * (TURN // 2) + q // 2, q, [True] * stages)
            for k in range(pairs, pairs + stages - 1):
                peeled(k)

        def late(p, n=1):
            return not (type(p) is int and p < n)

        block = ctx.enter_context(nc.Block())

        @block.sync
        def _(sp):
            def body(k, m, q, on):
                if on[0]:
                    if late(k, 2):
                        sp.wait_ge(S["norm"], k * 4 - 4)
                    sp.dma_start(h[q % 2][:], h_in[k]).then_inc(S[f"h_loaded{q % 2}"], 16)
                if on[5]:
                    p = k - 5
                    sp.wait_ge(S["summed"], p * 2 + 2)
                    sp.dma_start(out[p], res[:]).then_inc(S["stored"], 16)
                if on[4]:
                    p = k - 4
                    if late(p):
                        sp.wait_ge(S["summed"], p * 2)
                    sp.dma_start(h_again[:], h_in[p]).then_inc(S["h_again_loaded"], 16)

            run(sp, body)
            sp.wait_ge(S["stored"], 16 * pairs)

        @block.tensor
        def _(pe):
            pe.wait_ge(loaded, 16 * len(w))
            pe.wait_ge(S["slots_ready"], 2)

            def body(k, m, q, on):
                if on[4]:
                    p = k - 4
                    pe.wait_ge(S["xs_out"], p + 1)
                    pe.wait_ge(S["ct_out"], p + 1)
                    for t in range(2):
                        for part in range(2):
                            mm = pe.matmul(hid_ps[:, t * 2 * SLOTS:(t + 1) * 2 * SLOTS], w_down[:, part, t, :],
                                           xs[:, part, :], start=(part == 0), stop=(part == 1))
                    mm.then_inc(S["hid_done"], 1)
                if on[2]:
                    p = k - 2
                    pe.wait_ge(S["xt_out"], p * 2 + 2)
                    if late(p):
                        pe.wait_ge(S["c_steps"], p * 4 - 3)
                        pe.wait_ge(S["e_d"], p * 2)
                    for i in range(4):
                        lo = (i // 2) * L + (i % 2) * HALF
                        for part in range(2):
                            mm = pe.matmul(lg_ps[0:TT, i * SLOTS:(i + 1) * SLOTS], xt[q % 2][:, part, lo:lo + TT],
                                           slots[:, part, :], start=(part == 0), stop=(part == 1))
                    mm.then_inc(S["lg_done"], 1)
                    for part in range(2):
                        mm = pe.matmul(lt_ps[0:SLOTS, 0:W], slots[:, part, :], xt[q % 2][:, part, :],
                                       start=(part == 0), stop=(part == 1))
                    mm.then_inc(S["lt_done"], 1)
                if on[3]:
                    p = k - 3
                    if late(p):
                        pe.wait_ge(S["xs_out"], p)
                    pe.wait_ge(S["d_steps"], p * 4 + 4)
                    pe.sem_inc(S["fence"], 1)
                    for i in range(4):
                        rows, lo = (HALF, 0) if i % 2 == 0 else (TT, HALF)
                        mm = pe.transpose(xs_ps[0:rows, i * SLOTS:(i + 1) * SLOTS], p_d[:, i // 2, lo:lo + rows],
                                          ident[0:SLOTS, 0:SLOTS])
                    mm.then_inc(S["dm_done"], 1)
                if on[3]:
                    p = k - 3
                    pe.wait_ge(S["dm_out"], p * 2 + 2)
                    if late(p):
                        pe.wait_ge(S["xs_out"], p)
                    for part in range(2):
                        for img in range(2):
                            o = xs_ps[:, (part * 2 + img) * SLOTS:(part * 2 + img + 1) * SLOTS]
                            for half, rows in ((0, HALF), (1, TT)):
                                mm = pe.matmul(o, xn[(q - 3) % TURN][0:rows, 2 * img + half, part * HI:part * HI + P],
                                               dm[0:rows, 2 * img + half, :], start=(half == 0), stop=(half == 1))
                    mm.then_inc(S["xs_done"], 1)
                if on[4]:
                    p = k - 4
                    pe.wait_ge(S["masked"], p + 1)
                    if late(p):
                        pe.wait_ge(S["ys_out"], p)
                    for img in range(2):
                        for t in range(2):
                            mm = pe.matmul(ys_ps[0:SLOTS, img * D:(img + 1) * D],
                                           own_hid[:, t, img * SLOTS:(img + 1) * SLOTS], w_up[:, t, :],
                                           start=(t == 0), stop=(t == 1))
                    mm.then_inc(S["ys_done"], 1)
                if on[1]:
                    p = k - 1
                    pe.wait_ge(S["norm"], p * 4 + 4)
                    for part in range(2):
                        if late(p) or part == 1:
                            pe.wait_ge(S["xt_out"], p * 2 + part)
                        for i in range(4):
                            lo = (i // 2) * L + (i % 2) * HALF
                            mm = pe.transpose(tr_ps[:, lo:lo + TT], xn[(q - 1) % TURN][:, i, part * HI:part * HI + P], ident[0:TT, 0:TT])
                        mm.then_inc(S["tr_done"], 1)
                if on[3]:
                    p = k - 3
                    pe.wait_ge(S["c_steps"], p * 4 + 4)
                    if late(p):
                        pe.wait_ge(S["hid_out"], p * 2)
                    for i in range(4):
                        mm = pe.transpose(hid_ps[0:SLOTS, i * TT:(i + 1) * TT], p_c[:, i, :], ident[0:TT, 0:TT])
                    mm.then_inc(S["ct_done"], 1)
                if on[4]:
                    p = k - 4
                    pe.wait_ge(S["ys_out"], p + 1)
                    if late(p):
                        pe.wait_ge(S["summed"], p * 2)
                    for img in range(2):
                        for half in range(2):
                            mm = pe.matmul(out_ps[img][0:TT, half * D:(half + 1) * D], ct[q % 2][:, 2 * img + half, :],
                                           ys[:, img, :], start=True, stop=True)
                        mm.then_inc(S["out_done"], 1)

            run(pe, body)

        @block.scalar
        def _(act):
            act.wait_ge(loaded, 16 * len(w))
            nc.scalar.activation(slot_sq[:, :, :], slot_raw[:, :, :], ACT.Square).then_inc(S["slot_steps"], 1)

            def body(k, m, q, on):
                if on[4]:
                    p = k - 4
                    act.wait_ge(S["hid_done"], p + 1)
                    if late(p):
                        act.wait_ge(S["masked"], p)
                    for t in range(2):
                        nc.scalar.activation(hid[:, t, :], hid_ps[:, t * 2 * SLOTS:(t + 1) * 2 * SLOTS], ACT.Gelu,
                                             bias=b_down[:, t:t + 1]).then_inc(S["hid_out"], 1)
                if on[3]:
                    p = k - 3
                    act.wait_ge(S["dm_done"], p + 1)
                    if late(p):
                        act.wait_ge(S["xs_done"], p)
                    for half, rows in ((0, HALF), (1, TT)):
                        nc.scalar.copy(dm[0:rows, half::2, :], xs_ps[0:rows, 0:4 * SLOTS].rearrange(
                            "p (i s) -> p i s", i=4)[:, half::2, :]).then_inc(S["dm_out"], 1)
                if on[2]:
                    p = k - 2
                    act.wait_ge(S["mx"], p * 2 + 1)
                    if late(p):
                        act.wait_ge(S["d_steps"], p * 4)
                    for img in range(2):
                        nc.scalar.activation(e_d[:, img, :], lt_ps[0:SLOTS, img * L:(img + 1) * L], ACT.Exp,
                                             bias=mx_d[:, img:img + 1]).then_inc(S["e_d"], 1)
                    act.wait_ge(S["c_steps"], p * 4 + 1)
                    nc.scalar.activation(e_c[:, :, :], l_c[:, :, :], ACT.Exp).then_inc(S["e_c"], 1)
                if on[1]:
                    p = k - 1
                    for part in range(2):
                        act.wait_ge(S["tr_done"], p * 2 + part + 1)
                        if part == 0 and late(p, 2):
                            act.wait_ge(S["lt_done"], p - 1)
                        nc.scalar.copy(xt[(q - 1) % 2][:, part, :], tr_ps[:, 0:W]).then_inc(S["xt_out"], 1)
                if on[3]:
                    p = k - 3
                    act.wait_ge(S["ct_done"], p + 1)
                    if late(p, 2):
                        act.wait_ge(S["out_done"], p * 2 - 2)
                    nc.scalar.copy(ct[(q - 1) % 2][:, :, :], hid_ps[0:SLOTS, 0:4 * TT].rearrange("p (i t) -> p i t", i=4))\
                        .then_inc(S["ct_out"], 1)
                if on[3]:
                    p = k - 3
                    act.wait_ge(S["xs_done"], p + 1)
                    if late(p):
                        act.wait_ge(S["hid_done"], p)
                    nc.scalar.copy(xs[:, :, :], xs_ps[:, 0:4 * SLOTS].rearrange("p (a s) -> p a s", a=2))\
                        .then_inc(S["xs_out"], 1)

            run(act, body)

        @block.gpsimd
        def _(pool):
            nc.gpsimd.memset(minus_half[:], -0.5).then_inc(S["consts"], 1)
            nc.gpsimd.memset(plus_half[:], 0.5).then_inc(S["consts"], 1)
            nc.gpsimd.memset(minus_one[:], -1.0).then_inc(S["consts"], 1)
            pool.wait_ge(S["consts"], 3)
            pool.wait_ge(S["slot_steps"], 2)
            nc.gpsimd.tensor_tensor(slot_norm[:, :, :], slot_sum[:, :, :], plus_half[:, :, :], ALU.pow).then_inc(S["slot_steps"], 1)
            pool.wait_ge(S["slot_steps"], 3)
            nc.gpsimd.tensor_scalar(slot_sum[:, :, :], slot_norm[:, :, :], L2_EPS, None, ALU.add).then_inc(S["slot_steps"], 1)
            pool.wait_ge(S["slot_steps"], 4)
            nc.gpsimd.tensor_tensor(slot_norm[:, :, :], slot_sum[:, :, :], minus_one[:, :, :], ALU.pow).then_inc(S["slot_steps"], 1)

            def body(k, m, q, on):
                if on[4]:
                    p = k - 4
                    pool.wait_ge(S["hid_out"], p * 2 + 2)
                    if late(p):
                        pool.wait_ge(S["ys_done"], p)
                    nc.gpsimd.tensor_tensor(own_hid[:, :, :].rearrange("p m (i s) -> p m i s", i=2),
                                            hid[:, :, :].rearrange("p m (i s) -> p m i s", i=2),
                                            own[:, :, :].unsqueeze(2).broadcast_to([P, 2, 2, SLOTS]), ALU.mult)\
                        .then_inc(S["masked"], 1)
                if on[0]:
                    v = [x[:, :] for x in sm]
                    pool.wait_ge(S["stats"], k * 10 + 10)
                    if late(k):
                        pool.wait_ge(S["norm"], k * 4)
                    nc.gpsimd.tensor_tensor(v[2], v[0], minus_half[:, :], ALU.pow).then_inc(S["steps"], 1)
                    pool.wait_ge(S["steps"], k * 7 + 1)
                    nc.gpsimd.tensor_tensor(v[3], v[2], v[2], ALU.mult).then_inc(S["steps"], 1)
                    pool.wait_ge(S["steps"], k * 7 + 2)
                    nc.gpsimd.tensor_tensor(v[4], v[3], v[1], ALU.mult).then_inc(S["steps"], 1)
                    pool.wait_ge(S["steps"], k * 7 + 3)
                    nc.gpsimd.tensor_tensor(v[5], v[4], plus_half[0:TT, 0, :], ALU.pow).then_inc(S["steps"], 1)
                    pool.wait_ge(S["steps"], k * 7 + 4)
                    pool.sem_inc(S["fence"], 1)
                    nc.gpsimd.tensor_scalar(v[6], v[5], L2_EPS, None, ALU.add).then_inc(S["steps"], 1)
                    pool.wait_ge(S["steps"], k * 7 + 5)
                    nc.gpsimd.tensor_tensor(v[7], v[6], minus_one[0:TT, 0, :], ALU.pow).then_inc(S["steps"], 1)
                    pool.wait_ge(S["steps"], k * 7 + 6)
                    nc.gpsimd.tensor_tensor(v[8], v[7], v[2], ALU.mult).then_inc(S["steps"], 1)

            run(pool, body)

        @block.vector
        def _(dve):
            dve.wait_ge(loaded, 16 * len(w))
            dve.wait_ge(S["slot_steps"], 1)
            nc.vector.tensor_reduce(slot_sum[:, :, :], slot_sq[:, :, :].rearrange("p a (n s) -> p a s n", s=NP_), AX_X,
                                    ALU.add).then_inc(S["slot_steps"], 1)
            dve.wait_ge(S["slot_steps"], 5)
            for part in range(2):
                nc.vector.scalar_tensor_tensor(out=slots[:, part, :].rearrange("p (n s) -> p n s", s=NP_),
                                               in0=slot_raw[:, part, :].rearrange("p (n s) -> p n s", s=NP_),
                                               scalar=scale[:, 0:1],
                                               in1=slot_norm[:, part, :].unsqueeze(1).broadcast_to([P, NE, NP_]),
                                               op0=ALU.mult, op1=ALU.mult).then_inc(S["slots_ready"], 1)

            def body(k, m, q, on):
                if on[2]:
                    p = k - 2
                    dve.wait_ge(S["lt_done"], p + 1)
                    if late(p):
                        dve.wait_ge(S["e_d"], p * 2)
                    nc.vector.tensor_reduce(mx_d[:, :], lt_ps[0:SLOTS, 0:W].rearrange("p (i l) -> p i l", i=2), AX_X,
                                            ALU.max, negate=True).then_inc(S["mx"], 1)
                    if late(p):
                        dve.wait_ge(S["c_steps"], p * 4)
                    lg = lg_ps[0:TT, 0:4 * SLOTS].rearrange("p (i s) -> p i s", i=4)
                    nc.vector.tensor_reduce(mx_c[:, :], lg, AX_X, ALU.max).then_inc(S["mx"], 1)
                    dve.wait_ge(S["mx"], p * 2 + 2)
                    if late(p):
                        dve.wait_ge(S["e_c"], p)
                    nc.vector.tensor_tensor(l_c[:, :, :], lg, mx_c[:, :].unsqueeze(2).broadcast_to([TT, 4, SLOTS]),
                                            ALU.subtract).then_inc(S["c_steps"], 1)
                if on[1]:
                    p = k - 1
                    dve.wait_ge(S["steps"], p * 7 + 7)
                    if late(p, TURN):
                        dve.wait_ge(S["xs_done"], p - TURN + 1)
                        dve.wait_ge(S["tr_done"], (p - TURN) * 2 + 2)
                    for i in range(4):
                        nc.vector.tensor_scalar(xn[(q - 1) % TURN][:, i, :], h[(q - 1) % 2][:, i, :], mv[:, i, 0:1], sm[8][:, i:i + 1],
                                                ALU.subtract, ALU.mult).then_inc(S["norm"], 1)
                if on[4]:
                    p = k - 4
                    dve.wait_ge(S["ys_done"], p + 1)
                    if late(p):
                        dve.wait_ge(S["out_done"], p * 2)
                    nc.vector.tensor_tensor(ys[:, :, :], ys_ps[0:SLOTS, 0:2 * D].rearrange("p (i d) -> p i d", i=2),
                                            b_up[:, :].unsqueeze(1).broadcast_to([SLOTS, 2, D]), ALU.add)\
                        .then_inc(S["ys_out"], 1)
                if on[0]:
                    dve.wait_ge(S[f"h_loaded{q % 2}"], m * 16 + 16)
                    if late(k):
                        dve.wait_ge(S["norm"], k * 4)
                        dve.wait_ge(S["steps"], k * 7)
                    for i in range(4):
                        nc.vector.bn_stats(st[:, i, :], h[q % 2][:, i, :]).then_inc(S["stats"], 1)
                if on[0]:
                    for i in range(4):
                        dve.wait_ge(S["stats"], k * 10 + i + 1)
                        dve.sem_inc(S["fence"], 1)
                        nc.vector.bn_aggr(mv[:, i, :], st[:, i, :]).then_inc(S["stats"], 1)
                    dve.wait_ge(S["stats"], k * 10 + 8)
                    nc.vector.tensor_scalar(sm[0][:, :], mv[:, :, 1], LN_EPS, None, ALU.add).then_inc(S["stats"], 1)
                    nc.vector.tensor_scalar(sm[1][:, :], mv[:, :, 1], float(D), None, ALU.mult).then_inc(S["stats"], 1)
                if on[2]:
                    p = k - 2
                    dve.wait_ge(S["e_d"], p * 2 + 2)
                    nc.vector.tensor_reduce(sum_d[:, :], e_d[:, :, :], AX_X, ALU.add).then_inc(S["d_steps"], 1)
                    dve.wait_ge(S["d_steps"], p * 4 + 1)
                    nc.vector.reciprocal(inv_d[:, :], sum_d[:, :]).then_inc(S["d_steps"], 1)
                    dve.wait_ge(S["d_steps"], p * 4 + 2)
                    if late(p):
                        dve.wait_ge(S["dm_done"], p)
                    for img in range(2):
                        nc.vector.tensor_scalar(p_d[:, img, :], e_d[:, img, :], inv_d[:, img:img + 1], None,
                                                ALU.mult).then_inc(S["d_steps"], 1)
                    dve.wait_ge(S["e_c"], p + 1)
                    nc.vector.tensor_reduce(sum_c[:, :], e_c[:, :, :], AX_X, ALU.add).then_inc(S["c_steps"], 1)
                    dve.wait_ge(S["c_steps"], p * 4 + 2)
                    nc.vector.reciprocal(inv_c[:, :], sum_c[:, :]).then_inc(S["c_steps"], 1)
                    dve.wait_ge(S["c_steps"], p * 4 + 3)
                    if late(p):
                        dve.wait_ge(S["ct_done"], p)
                    nc.vector.tensor_tensor(p_c[:, :, :], e_c[:, :, :], inv_c[:, :].unsqueeze(2).broadcast_to([TT, 4, SLOTS]),
                                            ALU.mult).then_inc(S["c_steps"], 1)
                if on[4]:
                    p = k - 4
                    dve.wait_ge(S["h_again_loaded"], p * 16 + 16)
                    if late(p):
                        dve.wait_ge(S["stored"], p * 16)
                    for img in range(2):
                        dve.wait_ge(S["out_done"], p * 2 + img + 1)
                        nc.vector.tensor_tensor(res[:, 2 * img:2 * img + 2, :],
                                                out_ps[img][0:TT, 0:2 * D].rearrange("p (i d) -> p i d", i=2),
                                                h_again[:, 2 * img:2 * img + 2, :], ALU.add).then_inc(S["summed"], 1)

            run(dve, body)


def pointwise_tiles(w, mode):
    wt = np.ascontiguousarray(w.reshape(D, D).T)
    o = np.zeros((P, 6, P), wt.dtype)
    if mode == "one":
        o[:, 0] = wt[:P, :P]
        for i in range(2):
            o[HI * i:HI * i + HI, 1 + i] = wt[P:, :P]
            o[:, 3 + i, HI * i:HI * i + HI] = wt[:P, P:]
            o[HI * i:HI * i + HI, 5, HI * i:HI * i + HI] = wt[P:, P:]
    else:
        r = 0 if mode == "loc" else HI
        o[:, 0] = wt[:P, :P]
        o[r:r + HI, 1] = wt[P:, :P]
        for i in range(2):
            o[:, 2 + 2 * i, HI * i:HI * i + HI] = wt[:P, P:]
            o[r:r + HI, 3 + 2 * i, HI * i:HI * i + HI] = wt[P:, P:]
    return o


def low_high(v):
    return np.stack([v[:P], np.concatenate([v[P:], v[P:]])], 1)


def haar_bands():
    bands = np.zeros((256, 256), np.float32)
    for b in range(256):
        for i in range(16):
            for j in range(16):
                odd = 0
                for level in range(4):
                    digit = (b >> (2 * (3 - level))) & 3
                    odd ^= (digit >> 1) & (j >> level) & 1
                    odd ^= digit & (i >> level) & 1
                bands[b, i * 16 + j] = -0.0625 if odd else 0.0625
    return bands


def host_inputs(i, pairs):
    f = {}
    x = i["x"][:2 * pairs].reshape(pairs, 2, 3, G, 16, G, 16)
    x = x.transpose(0, 2, 4, 6, 1, 3, 5).reshape(pairs, KT, P, 2 * PX)
    f["x_t"] = x.transpose(0, 2, 1, 3)
    t = {k[7:]: v for k, v in i.items() if k.startswith("L0_tok_")}
    f["ident"] = np.eye(P, dtype=np.float32)
    f["haar"] = haar_bands().reshape(2, P, 256).transpose(1, 0, 2)
    f["w_wave"] = t["pg_w1"].reshape(D, 2, P, 3).transpose(2, 1, 3, 0)
    f["w_loc"] = t["pl_w"].reshape(D, KT, P).transpose(2, 1, 0)
    f["conv_bias"] = np.stack([t["pl_b"][:P], t["pg_b1"][:P], np.concatenate([t["pl_b"][P:], t["pg_b1"][P:]])], 1)
    dw = [t[n].reshape(D, TAPS) for n in ("pl_dw", "pg_dw", "f1_dw", "f2_dw", "f3_dw")]
    tiles = [dw[0][:P], dw[1][:P], np.concatenate([dw[0][P:], dw[1][P:]])]
    for w in dw[2:]:
        tiles += [w[:P], np.concatenate([w[P:], w[P:]])]
    f["dw_w"] = np.stack(tiles, 1)
    f["pw_loc"] = pointwise_tiles(t["pl_pw"], "loc")
    f["pw_glob"] = pointwise_tiles(t["pg_pw"], "glob")
    f["pw_glob2"] = pointwise_tiles(t["pg_w2"], "one")
    f["pw_fuse1"] = pointwise_tiles(t["f1_pw"], "one")
    f["pw_fuse2"] = pointwise_tiles(t["f2_pw"], "one")
    biases = np.stack([t[n] for n in ("pl_pwb", "pg_pwb", "pg_b2", "f1_pwb", "f2_pwb")], 1)
    f["pw_bias"] = low_high(biases).transpose(0, 2, 1)
    w3 = t["f3_pw"].reshape(D, D).T
    f["pw3"] = np.zeros((P, 3, D), np.float32)
    f["pw3"][:, 0] = w3[:P]
    for n in range(2):
        f["pw3"][HI * n:HI * n + HI, 1 + n] = w3[P:]
    f["bias3"] = np.zeros((P, D), np.float32)
    f["bias3"][0] = t["f3_pwb"]
    f["row0"] = np.zeros((P, TT), np.float32)
    f["row0"][0] = 1.0
    f["alpha"] = low_high(t["alpha"].reshape(D, 1))[:, :, 0]
    f["ln_g"] = np.broadcast_to(t["ln_g"], (TT, D))
    f["ln_b"] = np.broadcast_to(t["ln_b"], (TT, D))
    f["cls"] = t["cls"].reshape(1, D)
    a = {k[8:]: v for k, v in i.items() if k.startswith("L0_attn_")}

    def high_part(w):
        o = w[HI:].copy()
        o[:HI] = 0.0
        return o

    f["w_in"] = np.stack([a["W_in"][:P], high_part(a["W_in"])], 1).reshape(P, 2, 2 * DT, P)
    wx = a["W_x"].reshape(DT, P, RANK + 2 * NS).transpose(1, 0, 2)
    f["w_x"] = np.zeros((P, DT, P), np.float32)
    f["w_x"][:, :, :RANK] = wx[:, :, :RANK]
    f["w_bc"] = np.concatenate([wx[:, :, RANK:]] * 3, 2)
    f["w_dt"] = np.zeros((P, DT, P), np.float32)
    f["w_dt"][:RANK] = a["W_dt"].reshape(RANK, DT, P)
    f["b_dt"] = a["b_dt"].reshape(DT, P).T
    f["a_log"] = a["A_log"].reshape(DT, P, NS).transpose(1, 0, 2)
    f["d_skip"] = a["D_skip"].reshape(DT, P).T
    f["w_out"] = a["W_out"].reshape(DT, P, D).transpose(1, 0, 2)
    f["gamma"] = np.broadcast_to(a["gamma"], (TT, D))
    f["beta"] = np.broadcast_to(a["beta"], (TT, D))
    pick = np.zeros((96, 2 * NS), np.float32)
    pick[np.arange(96), np.arange(96) % (2 * NS)] = 1.0
    f["pick"] = pick
    s = {k[7:]: v for k, v in i.items() if k.startswith("L0_ffn_")}
    raw = s["slot_params"].reshape(D, SLOTS)
    f["slots"] = np.stack([raw[:P], high_part(raw)], 1)
    f["scale"] = np.broadcast_to(s["scale"].reshape(1, 1), (P, 1))
    down = s["W_down"].transpose(1, 0, 2).reshape(D, D)
    down = np.stack([down[:, :P], down[:, HI:]], 1).reshape(D, 2 * P)
    f["w_down"] = np.stack([down[:P], high_part(down)], 1).reshape(P, 2, 2, P)
    b = s["b_down"].reshape(D)
    f["b_down"] = np.stack([b[:P], b[HI:]], 1)
    up = s["W_up"].reshape(D, D)
    f["w_up"] = np.stack([up[:P], high_part(up)], 1)
    f["b_up"] = np.repeat(s["b_up"], NP_, 0)
    own = np.zeros((D, SLOTS), np.float32)
    for e in range(NE):
        own[e * HID:(e + 1) * HID, e * NP_:(e + 1) * NP_] = 1.0
    f["own"] = np.stack([own[:P], own[HI:]], 1)
    return {name: np.ascontiguousarray(v) for name, v in f.items()}


def kernel(**inputs):
    import concourse.bacc as bacc
    from concourse.bass_utils import run_bass_kernel_spmd

    given = {name: np.asarray(v) for name, v in inputs.items()}
    images = given["x"].shape[0]
    pairs = images // 2
    arrays = host_inputs(given, pairs)
    nc = bacc.Bacc("TRN2", target_bir_lowering=False, num_devices=1)
    t_in = {name: nc.dram_tensor("in_" + name, v.shape, mybir.dt.from_np(v.dtype), kind="ExternalInput").ap()
            for name, v in arrays.items()}
    out = nc.dram_tensor("out_tokens", (pairs, TT, 4, D), F32, kind="ExternalOutput").ap()
    bass_vit_tower(nc, t_in, out, pairs)
    got = run_bass_kernel_spmd(nc, [{"in_" + name: v for name, v in arrays.items()}], core_ids=[0])
    tiles = np.asarray(got.results[0]["out_tokens"]).reshape(pairs, TT, 2, 2, D).transpose(0, 2, 3, 1, 4)
    return np.concatenate([tiles[:, :, 0, :HALF], tiles[:, :, 1]], 2).reshape(images, L, D)
```
